# Optimizing a Trainium2 kernel written in Bass

```python
import numpy as np
import jax
import jax.numpy as jnp

def _softmax(x, axis=-1):
    return jax.nn.softmax(x, axis=axis)

def _gelu(x):
    return jax.nn.gelu(x, approximate=True)

def _silu(x):
    return jax.nn.silu(x)

def _sigmoid(x):
    return jax.nn.sigmoid(x)

def _layernorm(x, axis=-1, eps=1e-05):
    m = jnp.mean(x, axis=axis, keepdims=True)
    v = jnp.var(x, axis=axis, keepdims=True)
    return (x - m) / jnp.sqrt(v + eps)

def _scatter_add(tgt, idx, src, axis=0):
    return tgt.at[idx].add(src)

def _segment_sum(src, seg, n):
    return jax.ops.segment_sum(src, seg, n)
kernel_name = 'mk_sandwich_d2_jaxref_r4_52badd'

def setup_inputs(seed: int=0):
    np.random.seed(seed)
    _w = jnp.asarray

    def _L0_attn_setup():
        import jax, jax.numpy as jnp
        import numpy as np
        B, L, DM = (4, 128, 256)
        DS, DC, EXP = (16, 4, 2)
        DI = EXP * DM
        DTR = (DM + 15) // 16
        EPS = 1e-12
        SLOPE = 0.01

        def _ln(x, w, b):
            m = x.mean(-1, keepdims=True)
            v = ((x - m) ** 2).mean(-1, keepdims=True)
            return (x - m) * jax.lax.rsqrt(v + EPS) * w + b

        def _mamba(x, in_proj_w, conv_w, conv_b, x_proj_w, dt_proj_w, dt_proj_b, A_log, D, out_proj_w):
            xz = jnp.einsum('bld,ed->ble', x, in_proj_w)
            xs, z = jnp.split(xz, 2, axis=-1)
            kern = conv_w.T[:, None, :]
            xs = jax.lax.conv_general_dilated(xs, kern, window_strides=(1,), padding=[(DC - 1, 0)], dimension_numbers=('NWC', 'WIO', 'NWC'), feature_group_count=DI)
            xs = jax.nn.silu(xs + conv_b)
            x_dbl = jnp.einsum('bld,ed->ble', xs, x_proj_w)
            dt_r = x_dbl[..., :DTR]
            Bm = x_dbl[..., DTR:DTR + DS]
            Cm = x_dbl[..., DTR + DS:]
            dt = jax.nn.softplus(jnp.einsum('blr,dr->bld', dt_r, dt_proj_w) + dt_proj_b)
            A = -jnp.exp(A_log)
            dA = jnp.exp(dt[..., None] * A)
            dBx = dt[..., None] * Bm[:, :, None, :] * xs[..., None]

            def step(h, inp):
                dA_t, dBx_t, C_t = inp
                h = dA_t * h + dBx_t
                y = jnp.einsum('bdn,bn->bd', h, C_t)
                return (h, y)
            h0 = jnp.zeros((x.shape[0], DI, DS), dtype=x.dtype)
            _, ys = jax.lax.scan(step, h0, (dA.transpose(1, 0, 2, 3), dBx.transpose(1, 0, 2, 3), Cm.transpose(1, 0, 2)))
            y = ys.transpose(1, 0, 2) + D * xs
            y = y * jax.nn.silu(z)
            return jnp.einsum('bld,ed->ble', y, out_proj_w)
        key = jax.random.key(seed)
        ks = jax.random.split(key, 16)
        s = 0.02
        inp = {'x': jax.random.normal(ks[0], (B, L, DM), dtype=jnp.float32), 'in_proj_w': jax.random.normal(ks[1], (2 * DI, DM), dtype=jnp.float32) * s, 'conv_w': jax.random.normal(ks[2], (DI, DC), dtype=jnp.float32) * s, 'conv_b': jnp.zeros((DI,), dtype=jnp.float32), 'x_proj_w': jax.random.normal(ks[3], (DTR + 2 * DS, DI), dtype=jnp.float32) * s, 'dt_proj_w': jax.random.normal(ks[4], (DI, DTR), dtype=jnp.float32) * s, 'dt_proj_b': jax.random.normal(ks[5], (DI,), dtype=jnp.float32) * s, 'A_log': jnp.log(jnp.tile(jnp.arange(1, DS + 1, dtype=jnp.float32), (DI, 1))), 'D': jnp.ones((DI,), dtype=jnp.float32), 'out_proj_w': jax.random.normal(ks[6], (DM, DI), dtype=jnp.float32) * s, 'ln1_w': jnp.ones((DM,), dtype=jnp.float32), 'ln1_b': jnp.zeros((DM,), dtype=jnp.float32), 'ffn_w1': jax.random.normal(ks[7], (2 * DM, DM), dtype=jnp.float32) * s, 'ffn_b1': jnp.zeros((2 * DM,), dtype=jnp.float32), 'ffn_w2': jax.random.normal(ks[8], (DM, 2 * DM), dtype=jnp.float32) * s, 'ffn_b2': jnp.zeros((DM,), dtype=jnp.float32), 'ln2_w': jnp.ones((DM,), dtype=jnp.float32), 'ln2_b': jnp.zeros((DM,), dtype=jnp.float32)}
        return inp
    _L0_attn_in = _L0_attn_setup()

    def _L0_ffn_setup():
        import jax, jax.numpy as jnp
        import numpy as np
        EPS = 1e-05

        def _quantize(W):
            gamma = jnp.mean(jnp.abs(W))
            return jnp.clip(jnp.round(W / (gamma + EPS)), -1.0, 1.0)
        key = jax.random.key(seed)
        k_x, k_w1, k_b1, k_w2, k_b2 = jax.random.split(key, 5)
        n_embd = 256
        d_ff = 4 * n_embd
        B, S = (4, 1024)
        bound1 = 1.0 / np.sqrt(n_embd)
        bound2 = 1.0 / np.sqrt(d_ff)
        x = jax.random.normal(k_x, (B, S, n_embd), dtype=jnp.float32)
        W1 = jax.random.uniform(k_w1, (d_ff, n_embd), jnp.float32, -bound1, bound1)
        b1 = jax.random.uniform(k_b1, (d_ff,), jnp.float32, -bound1, bound1)
        W2 = jax.random.uniform(k_w2, (n_embd, d_ff), jnp.float32, -bound2, bound2)
        b2 = jax.random.uniform(k_b2, (n_embd,), jnp.float32, -bound2, bound2)
        return {'x': x, 'W1': W1, 'b1': b1, 'W2': W2, 'b2': b2}
    _L0_ffn_in = _L0_ffn_setup()

    def _L1_attn_setup():
        import jax, jax.numpy as jnp
        import numpy as np
        B, S, D, H = (2, 512, 256, 16)
        HD = D // H
        LN_EPS = 1e-05
        key = jax.random.key(seed)
        ks = jax.random.split(key, 8)
        inv = 1.0 / np.sqrt(D)
        return {'embedded': jax.random.normal(ks[0], (B, S, D), dtype=jnp.float32), 'Wq': jax.random.normal(ks[1], (D, D), dtype=jnp.float32) * inv, 'bq': jax.random.normal(ks[2], (D,), dtype=jnp.float32) * 0.01, 'Wk': jax.random.normal(ks[3], (D, D), dtype=jnp.float32) * inv, 'bk': jax.random.normal(ks[4], (D,), dtype=jnp.float32) * 0.01, 'Wv': jax.random.normal(ks[5], (D, D), dtype=jnp.float32) * inv, 'bv': jax.random.normal(ks[6], (D,), dtype=jnp.float32) * 0.01, 'gamma': jnp.ones((D,), dtype=jnp.float32), 'beta': jnp.zeros((D,), dtype=jnp.float32)}
    _L1_attn_in = _L1_attn_setup()

    def _L1_ffn_setup():
        import jax, jax.numpy as jnp
        import numpy as np
        H = 256
        M = 128
        E = 16
        TOP_K = 4
        N_GROUP = 4
        TOPK_GROUP = 2
        SCALE = 2.5
        B, S = (2, 256)

        def _gate(x2d, gate_kernel, gate_bias):
            n = x2d.shape[0]
            logits = jnp.dot(x2d.astype(jnp.float32), gate_kernel.astype(jnp.float32))
            scores = jax.nn.sigmoid(logits)
            scores_for_choice = scores + gate_bias
            group_scores = scores_for_choice.reshape(n, N_GROUP, E // N_GROUP)
            top2 = jax.lax.top_k(group_scores, k=2)[0]
            group_sum = jnp.sum(top2, axis=-1)
            group_idx = jax.lax.top_k(group_sum, k=TOPK_GROUP)[1]
            group_mask = jnp.zeros_like(group_sum).at[jnp.arange(n)[:, None], group_idx].set(1.0)
            score_mask = jnp.repeat(group_mask[:, :, None], E // N_GROUP, axis=2).reshape(n, E)
            masked_scores = jnp.where(score_mask > 0, scores_for_choice, 0.0)
            topk_weight, topk_idx = jax.lax.top_k(masked_scores, k=TOP_K)
            topk_weight = topk_weight / (jnp.sum(topk_weight, axis=-1, keepdims=True) + 1e-20)
            topk_weight = topk_weight * SCALE
            return (topk_idx, topk_weight)
        key = jax.random.key(seed)
        ks = jax.random.split(key, 9)
        sc_h = 1.0 / np.sqrt(H)
        sc_m = 1.0 / np.sqrt(M)
        return {'hidden_states': jax.random.normal(ks[0], (B, S, H), jnp.float32), 'gate_kernel': jax.random.normal(ks[1], (H, E), jnp.float32) * sc_h, 'gate_bias': jax.random.normal(ks[2], (E,), jnp.float32) * 0.01, 'w_gate': jax.random.normal(ks[3], (E, H, M), jnp.float32) * sc_h, 'w_up': jax.random.normal(ks[4], (E, H, M), jnp.float32) * sc_h, 'w_down': jax.random.normal(ks[5], (E, M, H), jnp.float32) * sc_m, 'sw_gate': jax.random.normal(ks[6], (H, 2 * M), jnp.float32) * sc_h, 'sw_up': jax.random.normal(ks[7], (H, 2 * M), jnp.float32) * sc_h, 'sw_down': jax.random.normal(ks[8], (2 * M, H), jnp.float32) * (1.0 / np.sqrt(2 * M))}
    _L1_ffn_in = _L1_ffn_setup()
    _d = {'L0_attn_x': _L0_attn_in['x'], 'L0_attn_in_proj_w': _L0_attn_in['in_proj_w'], 'L0_attn_conv_w': _L0_attn_in['conv_w'], 'L0_attn_conv_b': _L0_attn_in['conv_b'], 'L0_attn_x_proj_w': _L0_attn_in['x_proj_w'], 'L0_attn_dt_proj_w': _L0_attn_in['dt_proj_w'], 'L0_attn_dt_proj_b': _L0_attn_in['dt_proj_b'], 'L0_attn_A_log': _L0_attn_in['A_log'], 'L0_attn_D': _L0_attn_in['D'], 'L0_attn_out_proj_w': _L0_attn_in['out_proj_w'], 'L0_attn_ln1_w': _L0_attn_in['ln1_w'], 'L0_attn_ln1_b': _L0_attn_in['ln1_b'], 'L0_attn_ffn_w1': _L0_attn_in['ffn_w1'], 'L0_attn_ffn_b1': _L0_attn_in['ffn_b1'], 'L0_attn_ffn_w2': _L0_attn_in['ffn_w2'], 'L0_attn_ffn_b2': _L0_attn_in['ffn_b2'], 'L0_attn_ln2_w': _L0_attn_in['ln2_w'], 'L0_attn_ln2_b': _L0_attn_in['ln2_b'], 'L0_ffn_W1': _L0_ffn_in['W1'], 'L0_ffn_b1': _L0_ffn_in['b1'], 'L0_ffn_W2': _L0_ffn_in['W2'], 'L0_ffn_b2': _L0_ffn_in['b2'], 'L1_attn_Wq': _L1_attn_in['Wq'], 'L1_attn_bq': _L1_attn_in['bq'], 'L1_attn_Wk': _L1_attn_in['Wk'], 'L1_attn_bk': _L1_attn_in['bk'], 'L1_attn_Wv': _L1_attn_in['Wv'], 'L1_attn_bv': _L1_attn_in['bv'], 'L1_attn_gamma': _L1_attn_in['gamma'], 'L1_attn_beta': _L1_attn_in['beta'], 'L1_ffn_gate_kernel': _L1_ffn_in['gate_kernel'], 'L1_ffn_gate_bias': _L1_ffn_in['gate_bias'], 'L1_ffn_w_gate': _L1_ffn_in['w_gate'], 'L1_ffn_w_up': _L1_ffn_in['w_up'], 'L1_ffn_w_down': _L1_ffn_in['w_down'], 'L1_ffn_sw_gate': _L1_ffn_in['sw_gate'], 'L1_ffn_sw_up': _L1_ffn_in['sw_up'], 'L1_ffn_sw_down': _L1_ffn_in['sw_down']}
    _x0 = _d['L0_attn_x']
    _d['L0_attn_x'] = jax.random.normal(jax.random.fold_in(jax.random.key(seed), 1), (1, 4096, 256), dtype=_x0.dtype)
    del _x0
    return _d

def reference(L0_attn_x, L0_attn_in_proj_w, L0_attn_conv_w, L0_attn_conv_b, L0_attn_x_proj_w, L0_attn_dt_proj_w, L0_attn_dt_proj_b, L0_attn_A_log, L0_attn_D, L0_attn_out_proj_w, L0_attn_ln1_w, L0_attn_ln1_b, L0_attn_ffn_w1, L0_attn_ffn_b1, L0_attn_ffn_w2, L0_attn_ffn_b2, L0_attn_ln2_w, L0_attn_ln2_b, L0_ffn_W1, L0_ffn_b1, L0_ffn_W2, L0_ffn_b2, L1_attn_Wq, L1_attn_bq, L1_attn_Wk, L1_attn_bk, L1_attn_Wv, L1_attn_bv, L1_attn_gamma, L1_attn_beta, L1_ffn_gate_kernel, L1_ffn_gate_bias, L1_ffn_w_gate, L1_ffn_w_up, L1_ffn_w_down, L1_ffn_sw_gate, L1_ffn_sw_up, L1_ffn_sw_down):

    def _L0_attn_ref(x, in_proj_w, conv_w, conv_b, x_proj_w, dt_proj_w, dt_proj_b, A_log, D, out_proj_w, ln1_w, ln1_b, ffn_w1, ffn_b1, ffn_w2, ffn_b2, ln2_w, ln2_b):
        import jax, jax.numpy as jnp
        import numpy as np
        B, L, DM = (4, 128, 256)
        DS, DC, EXP = (16, 4, 2)
        DI = EXP * DM
        DTR = (DM + 15) // 16
        EPS = 1e-12
        SLOPE = 0.01

        def _ln(x, w, b):
            m = x.mean(-1, keepdims=True)
            v = ((x - m) ** 2).mean(-1, keepdims=True)
            return (x - m) * jax.lax.rsqrt(v + EPS) * w + b

        def _mamba(x, in_proj_w, conv_w, conv_b, x_proj_w, dt_proj_w, dt_proj_b, A_log, D, out_proj_w):
            xz = jnp.einsum('bld,ed->ble', x, in_proj_w)
            xs, z = jnp.split(xz, 2, axis=-1)
            kern = conv_w.T[:, None, :]
            xs = jax.lax.conv_general_dilated(xs, kern, window_strides=(1,), padding=[(DC - 1, 0)], dimension_numbers=('NWC', 'WIO', 'NWC'), feature_group_count=DI)
            xs = jax.nn.silu(xs + conv_b)
            x_dbl = jnp.einsum('bld,ed->ble', xs, x_proj_w)
            dt_r = x_dbl[..., :DTR]
            Bm = x_dbl[..., DTR:DTR + DS]
            Cm = x_dbl[..., DTR + DS:]
            dt = jax.nn.softplus(jnp.einsum('blr,dr->bld', dt_r, dt_proj_w) + dt_proj_b)
            A = -jnp.exp(A_log)
            dA = jnp.exp(dt[..., None] * A)
            dBx = dt[..., None] * Bm[:, :, None, :] * xs[..., None]

            def step(h, inp):
                dA_t, dBx_t, C_t = inp
                h = dA_t * h + dBx_t
                y = jnp.einsum('bdn,bn->bd', h, C_t)
                return (h, y)
            h0 = jnp.zeros((x.shape[0], DI, DS), dtype=x.dtype)
            _, ys = jax.lax.scan(step, h0, (dA.transpose(1, 0, 2, 3), dBx.transpose(1, 0, 2, 3), Cm.transpose(1, 0, 2)))
            y = ys.transpose(1, 0, 2) + D * xs
            y = y * jax.nn.silu(z)
            return jnp.einsum('bld,ed->ble', y, out_proj_w)
        h = _mamba(x, in_proj_w, conv_w, conv_b, x_proj_w, dt_proj_w, dt_proj_b, A_log, D, out_proj_w)
        h = _ln(h + x, ln1_w, ln1_b)
        f = jnp.einsum('bld,ed->ble', h, ffn_w1) + ffn_b1
        f = jnp.where(f >= 0, f, SLOPE * f)
        f = jnp.einsum('ble,de->bld', f, ffn_w2) + ffn_b2
        return _ln(f + h, ln2_w, ln2_b)

    def _L0_ffn_ref(x, W1, b1, W2, b2):
        import jax, jax.numpy as jnp
        import numpy as np
        EPS = 1e-05

        def _quantize(W):
            gamma = jnp.mean(jnp.abs(W))
            return jnp.clip(jnp.round(W / (gamma + EPS)), -1.0, 1.0)
        Wq1 = _quantize(W1)
        Wq2 = _quantize(W2)
        h = jax.nn.relu(jnp.einsum('bsd,fd->bsf', x, Wq1) + b1)
        out = jnp.einsum('bsf,df->bsd', h, Wq2) + b2
        return out

    def _L1_attn_ref(embedded, Wq, bq, Wk, bk, Wv, bv, gamma, beta):
        import jax, jax.numpy as jnp
        import numpy as np
        B, S, D, H = (2, 512, 256, 16)
        HD = D // H
        LN_EPS = 1e-05
        b, s, d = embedded.shape
        q = embedded @ Wq.T + bq
        k = embedded @ Wk.T + bk
        v = embedded @ Wv.T + bv
        q = q.reshape(b, s, H, HD).transpose(0, 2, 1, 3)
        k = k.reshape(b, s, H, HD).transpose(0, 2, 1, 3)
        v = v.reshape(b, s, H, HD).transpose(0, 2, 1, 3)
        qk = jnp.einsum('bhqd,bhkd->bhqk', q, k)
        qk = jnp.where(jnp.isnan(qk), -jnp.inf, qk)
        qk = qk / jnp.float32(np.sqrt(s))
        p = jax.nn.softmax(qk, axis=-1)
        p = jnp.where(jnp.isnan(p), 0.0, p)
        v = jnp.where(jnp.isnan(v), 0.0, v)
        mask = jnp.triu(jnp.ones((s, s), dtype=p.dtype), k=0)
        p = p * mask
        z = jnp.einsum('bhqk,bhkd->bhqd', p, v)
        z = z.reshape(b, s, d)
        x = embedded + z
        mu = jnp.mean(x, axis=-1, keepdims=True)
        var = jnp.mean(jnp.square(x - mu), axis=-1, keepdims=True)
        out = (x - mu) * jax.lax.rsqrt(var + LN_EPS) * gamma + beta
        return out

    def _L1_ffn_ref(hidden_states, gate_kernel, gate_bias, w_gate, w_up, w_down, sw_gate, sw_up, sw_down):
        import jax, jax.numpy as jnp
        import numpy as np
        H = 256
        M = 128
        E = 16
        TOP_K = 4
        N_GROUP = 4
        TOPK_GROUP = 2
        SCALE = 2.5
        B, S = (2, 256)

        def _gate(x2d, gate_kernel, gate_bias):
            n = x2d.shape[0]
            logits = jnp.dot(x2d.astype(jnp.float32), gate_kernel.astype(jnp.float32))
            scores = jax.nn.sigmoid(logits)
            scores_for_choice = scores + gate_bias
            group_scores = scores_for_choice.reshape(n, N_GROUP, E // N_GROUP)
            top2 = jax.lax.top_k(group_scores, k=2)[0]
            group_sum = jnp.sum(top2, axis=-1)
            group_idx = jax.lax.top_k(group_sum, k=TOPK_GROUP)[1]
            group_mask = jnp.zeros_like(group_sum).at[jnp.arange(n)[:, None], group_idx].set(1.0)
            score_mask = jnp.repeat(group_mask[:, :, None], E // N_GROUP, axis=2).reshape(n, E)
            masked_scores = jnp.where(score_mask > 0, scores_for_choice, 0.0)
            topk_weight, topk_idx = jax.lax.top_k(masked_scores, k=TOP_K)
            topk_weight = topk_weight / (jnp.sum(topk_weight, axis=-1, keepdims=True) + 1e-20)
            topk_weight = topk_weight * SCALE
            return (topk_idx, topk_weight)
        orig_shape = hidden_states.shape
        x = hidden_states.reshape(-1, orig_shape[-1])
        topk_idx, topk_weight = _gate(x, gate_kernel, gate_bias)
        onehot = (topk_idx[:, :, None] == jnp.arange(E)[None, None, :]).astype(topk_weight.dtype)
        combine = jnp.einsum('nke,nk->ne', onehot, topk_weight)
        g = jnp.einsum('nh,ehm->enm', x, w_gate)
        u = jnp.einsum('nh,ehm->enm', x, w_up)
        inter = jax.nn.silu(g) * u
        y_e = jnp.einsum('enm,emh->enh', inter, w_down)
        y = jnp.einsum('ne,enh->nh', combine, y_e)
        shared = jnp.dot(jax.nn.silu(jnp.dot(x, sw_gate)) * jnp.dot(x, sw_up), sw_down)
        return (y + shared).reshape(orig_shape)
    x = L0_attn_x
    x = x + _layernorm(_L0_attn_ref(_layernorm(x, axis=-1), L0_attn_in_proj_w, L0_attn_conv_w, L0_attn_conv_b, L0_attn_x_proj_w, L0_attn_dt_proj_w, L0_attn_dt_proj_b, L0_attn_A_log, L0_attn_D, L0_attn_out_proj_w, L0_attn_ln1_w, L0_attn_ln1_b, L0_attn_ffn_w1, L0_attn_ffn_b1, L0_attn_ffn_w2, L0_attn_ffn_b2, L0_attn_ln2_w, L0_attn_ln2_b), axis=-1)
    x = x + _layernorm(_L0_ffn_ref(_layernorm(x, axis=-1), L0_ffn_W1, L0_ffn_b1, L0_ffn_W2, L0_ffn_b2), axis=-1)
    x = x + _layernorm(_L1_attn_ref(_layernorm(x, axis=-1), L1_attn_Wq, L1_attn_bq, L1_attn_Wk, L1_attn_bk, L1_attn_Wv, L1_attn_bv, L1_attn_gamma, L1_attn_beta), axis=-1)
    x = x + _layernorm(_L1_ffn_ref(_layernorm(x, axis=-1), L1_ffn_gate_kernel, L1_ffn_gate_bias, L1_ffn_w_gate, L1_ffn_w_up, L1_ffn_w_down, L1_ffn_sw_gate, L1_ffn_sw_up, L1_ffn_sw_down), axis=-1)
    return x

_drawn_inputs = setup_inputs


def setup_inputs(seed=0):
    import zlib

    import numpy as np

    out = dict(_drawn_inputs(seed))
    spreads = {'L0_attn_conv_b': (0.0, 0.691),
     'L0_attn_D': (1.0, 0.6),
     'L0_attn_ln1_w': (1.0, 0.2),
     'L0_attn_ln1_b': (0.0, 0.1),
     'L0_attn_ffn_b1': (0.0, 0.1),
     'L0_attn_ffn_b2': (0.0, 0.1),
     'L0_attn_ln2_w': (1.0, 0.2),
     'L0_attn_ln2_b': (0.0, 0.1),
     'L1_attn_gamma': (1.0, 0.2),
     'L1_attn_beta': (0.0, 0.1)}
    factors = {'L0_attn_in_proj_w': 5.371,
     'L0_attn_conv_w': 8.0,
     'L0_attn_x_proj_w': 8.0,
     'L0_attn_dt_proj_w': 8.0,
     'L0_attn_dt_proj_b': 8.0,
     'L0_attn_A_log': 8.0,
     'L0_attn_out_proj_w': 5.149,
     'L0_ffn_b1': 7.565,
     'L0_ffn_b2': 64.0,
     'L1_attn_Wq': 8.0,
     'L1_attn_bq': 39.713,
     'L1_attn_Wk': 8.0,
     'L1_attn_bk': 64.0,
     'L1_attn_bv': 6.472}
    for name, (base, spread) in spreads.items():
        noise = np.random.default_rng([zlib.crc32(name.encode()), seed]).standard_normal(out[name].shape)
        drawn = base * np.exp(spread * noise) if base else spread * noise
        out[name] = jnp.asarray(drawn.astype(out[name].dtype))
    for name, factor in factors.items():
        out[name] = (out[name] * factor).astype(out[name].dtype)
    return out
```

```python
import numpy as np
from contextlib import ExitStack
import concourse.bass as bass
from concourse import mybir

F32 = mybir.dt.float32
BF16 = mybir.dt.bfloat16
ALU = mybir.AluOpType
ACT = mybir.ActivationFunctionType
AX = mybir.AxisListType

P = 128
T = 4096
DM = 256
NT = T // P
CH = 512
NCH = T // CH
TPC = CH // P
KD = DM // P
DI = 512
ND = DI // P
DS = 16
DTR = 16
DC = 4
SPLIT = 3
BC = 2 * DS
XP = SPLIT * BC + DTR
LN_EPS = 1e-5
MAMBA_EPS = 1e-12
FREE = 1


class Order:

    def __init__(self, eng, sem, base=0):
        self.eng, self.sem, self.base, self.n = eng, sem, base, 0

    def close(self, per_pass):
        assert self.n == per_pass, (self.n, per_pass)

    def done(self, ins):
        ins.then_inc(self.sem, 1)
        self.n += 1
        self.eng.wait_ge(self.sem, self.base + self.n)


def peeled(eng, count, first, second):
    first(0)
    with eng.Fori(0, count - 1) as i:
        first(i + 1)
        second(i)
    second(count - 1)


def tok(c, t):
    return c * TPC + t


def mamba(nc, sem, X, ident, a):
    with ExitStack() as ctx:
        def sb(name, shape, dt=F32):
            return ctx.enter_context(nc.sbuf_tensor(name, shape, dt))

        NH = 3
        w_in = sb("w_in", [P, KD, 2 * DI])
        w_out = sb("w_out", [P, ND, DM])
        w_xp = sb("w_xp", [P, ND, XP])
        w_dt = sb("w_dt", [P, DI])
        conv_w = sb("conv_w", [P, ND, DC])
        conv_b = sb("conv_b", [P, ND])
        dt_b = sb("dt_b", [P, ND])
        skip_d = sb("skip_d", [P, ND])
        a_neg = sb("m_a_neg", [P, ND, DS])
        spread = sb("spread", [SPLIT * BC, BC, P], BF16)
        stats = sb("m_stats", [P, TPC, 6])
        mv = sb("m_mv", [P, TPC, 2])
        var = sb("m_var", [P, TPC])
        spare = sb("m_spare", [P, 1])
        rstd = sb("m_rstd", [P, TPC])
        half = sb("m_half", [P, TPC])
        xn = sb("m_xn", [P, TPC, DM])
        xnT = sb("m_xnT", [P, KD, CH])
        raw = sb("m_raw", [P, ND, CH + DC - 1])
        conv = sb("m_conv", [P, ND, CH])
        u = conv
        xs = sb("m_xs", [P, ND, CH])
        zs = sb("m_zs", [P, ND, CH])
        soft = sb("m_soft", [P, ND, CH])
        yg = soft
        dt = sb("m_dt", [P, ND, CH])
        bc3 = sb("m_bc3", [SPLIT * BC, CH], BF16)
        mid = sb("m_mid", [SPLIT * BC, CH], BF16)
        low = sb("m_low", [SPLIT * BC, CH], BF16)
        rest = sb("m_rest", [SPLIT * BC, CH])
        dtr = sb("m_dtr", [P, CH])
        dA = sb("m_dA", [P, 2, ND, CH])
        spread_f = dA[0:SPLIT * BC].rearrange("p a b t -> p (a b t)")
        dBx = sb("m_dBx", [P, ND, CH])
        h = sb("m_h", [P, NH, ND, CH])
        crep = sb("m_crep", [P, NH, CH])
        h_end = sb("m_h_end", [P, DS, ND])
        bank = [ctx.enter_context(nc.psum_tensor(f"m_bank{b}", [P, CH], F32)) for b in range(8)]
        YB, BB, CB = 0, 4, 6

        w_ready, x_ready = sem("m_w_ready"), sem("m_x_ready")
        const_ready, spread_ready = sem("m_const_ready"), sem("m_spread_ready")
        var_ready, rstd_ready = sem("m_var_ready"), sem("m_rstd_ready")
        xn_ready, xT_ready, xnT_ready = sem("m_xn_ready"), sem("m_xT_ready"), sem("m_xnT_ready")
        proj_ready, raw_ready, conv_ready = sem("m_proj_ready"), sem("m_raw_ready"), sem("m_conv_ready")
        z_ready, xs_ready, xp_ready = sem("m_z_ready"), sem("m_xs_ready"), sem("m_xp_ready")
        bc_ready, dtr_ready, dtp_ready = sem("m_bc_ready"), sem("m_dtr_ready"), sem("m_dtp_ready")
        soft_ready, dt_ready = sem("m_soft_ready"), sem("m_dt_ready")
        b_spread, c_spread, crep_ready = sem("m_b_spread"), sem("m_c_spread"), sem("m_crep_ready")
        dA_ready, b_used = sem("m_dA_ready"), sem("m_b_used")
        h_ready, h_kept, g_ready, g_summed = sem("m_h_ready"), sem("m_h_kept"), sem("m_g_ready"), sem("m_g_summed")
        yg_ready, out_ready = sem("m_yg_ready"), sem("m_out_ready")
        v_own, s_own = sem("m_v_own"), sem("m_s_own")
        NW = 10
        V_OWN, S_OWN = 12, 4

        with nc.Block() as block:
            @block.sync
            def _(sp):
                for q in range(4):
                    sp.dma_start(X[:, q * 8:(q + 1) * 8, :],
                                 a["L0_attn_x"][0, q * 8 * P:(q + 1) * 8 * P, :].rearrange("(j p) d -> p j d", p=P)
                                 ).then_inc(x_ready, 16)
                    if q == 0:
                        sp.dma_start(ident[:], a["ident"]).then_inc(w_ready, 16)
                        sp.dma_start(w_in[:], a["in_proj_t"]).then_inc(w_ready, 16)
                sp.dma_start(w_xp[:], a["x_proj_t"]).then_inc(w_ready, 16)
                sp.dma_start(w_dt[SPLIT * BC:XP, :], a["dt_proj_t"]).then_inc(w_ready, 16)
                sp.dma_start(w_out[:], a["out_proj_t"]).then_inc(w_ready, 16)
                sp.dma_start(spread_f, a["spread"]).then_inc(w_ready, 16)

            @block.gpsimd
            def _(pool):
                nc.gpsimd.memset(half[:], -0.5).then_inc(const_ready, 1)
                nc.gpsimd.memset(h_end[:], 0.0).then_inc(const_ready, 1)
                nc.gpsimd.memset(raw[:, :, CH:], 0.0).then_inc(const_ready, 1)
                pool.wait_ge(const_ready, 3)
                with pool.Fori(0, NCH) as i:
                    pool.wait_ge(var_ready, i + 1)
                    nc.gpsimd.tensor_tensor(rstd[:], var[:], half[:], ALU.pow).then_inc(rstd_ready, 1)
                    for n in range(DS):
                        pool.wait_ge(crep_ready, i * DS + n + 1)
                        pool.wait_ge(h_kept, i * DS + n + 1)
                        nc.gpsimd.tensor_tensor(h[:, n % NH], h[:, n % NH],
                                                crep[:, n % NH:n % NH + 1, :].broadcast_to([P, ND, CH]),
                                                ALU.mult).then_inc(g_ready, 1)

            @block.scalar
            def _(act):
                act.dma_start(conv_w[:], a["conv_w"]).then_inc(w_ready, 16)
                act.dma_start(conv_b[:], a["conv_b"]).then_inc(w_ready, 16)
                act.dma_start(dt_b[:], a["dt_b"]).then_inc(w_ready, 16)
                act.dma_start(skip_d[:], a["skip_d"]).then_inc(w_ready, 16)
                act.dma_start(a_neg[:], a["a_log"]).then_inc(w_ready, 16)
                act.wait_ge(w_ready, 16 * (NW + 1))
                act.wait_ge(spread_ready, 1)
                setup = Order(act, s_own)
                setup.done(nc.scalar.activation(a_neg[:], a_neg[:], ACT.Exp))
                setup.done(nc.scalar.mul(a_neg[:], a_neg[:], -1.0))
                act.wait_ge(const_ready, 3)
                with act.Fori(0, NCH) as i:
                    own = Order(act, s_own, i * S_OWN + 2)
                    act.wait_ge(xT_ready, i + 1)
                    for k in range(KD):
                        last = nc.scalar.copy(xnT[:, k, :], bank[BB + k][:])
                    last.then_inc(xnT_ready, 1)
                    own.done(nc.scalar.copy(raw[:, :, 0:DC - 1], raw[:, :, CH:]))
                    for m in range(ND):
                        act.wait_ge(proj_ready, i * 2 * ND + m + 1)
                        nc.scalar.copy(raw[:, m, DC - 1:], bank[YB + m][:]).then_inc(raw_ready, 1)
                    for m in range(ND):
                        act.wait_ge(proj_ready, i * 2 * ND + ND + m + 1)
                        nc.scalar.activation(zs[:, m, :], bank[BB + m][:], ACT.Silu).then_inc(z_ready, 1)
                    for m in range(ND):
                        act.wait_ge(conv_ready, i * ND + m + 1)
                        nc.scalar.activation(xs[:, m, :], conv[:, m, :], ACT.Silu,
                                             bias=conv_b[:, m:m + 1]).then_inc(xs_ready, 1)
                    act.wait_ge(xp_ready, i + 1)
                    nc.scalar.copy(dtr[SPLIT * BC:XP, :], bank[CB][SPLIT * BC:XP, :]).then_inc(dtr_ready, 1)
                    for m in range(ND):
                        act.wait_ge(dtp_ready, i * ND + m + 1)
                        last = nc.scalar.activation(dt[:, m, :], bank[YB + m][:], ACT.Identity, bias=dt_b[:, m:m + 1])
                    own.done(last)
                    own.done(nc.scalar.activation(soft[:], dt[:], ACT.Abs))
                    own.done(nc.scalar.activation(soft[:], soft[:], ACT.Exp, scale=-1.0))
                    nc.scalar.activation(soft[:], soft[:], ACT.Ln, bias=1.0).then_inc(soft_ready, 1)
                    act.wait_ge(dt_ready, i + 1)

                    def keep_end(n):
                        act.wait_ge(h_ready, i * DS + n + 1)
                        nc.scalar.copy(h_end[:, n, :], h[:, n % NH, :, CH - 1]).then_inc(h_kept, 1)

                    for n in range(DS):
                        for m in range(ND):
                            last = nc.scalar.activation(dA[:, n % 2, m, :], dt[:, m, :], ACT.Exp,
                                                        scale=a_neg[:, m, n:n + 1])
                        last.then_inc(dA_ready, 1)
                        act.wait_ge(c_spread, i * DS + n + 1)
                        if n >= NH:
                            act.wait_ge(g_ready, i * DS + n - NH + 1)
                        nc.scalar.copy(crep[:, n % NH, :], bank[CB + n % 2][:]).then_inc(crep_ready, 1)
                        if n >= 1:
                            keep_end(n - 1)
                    keep_end(DS - 1)
                    own.close(S_OWN)

            @block.vector
            def _(dve):
                dve.wait_ge(w_ready, 16 * (NW + 1))
                nc.vector.tensor_copy(spread[:].rearrange("p r c -> p (r c)"), spread_f).then_inc(spread_ready, 1)
                dve.wait_ge(x_ready, 16 * 4)
                with dve.Fori(0, NCH) as i:
                    own = Order(dve, v_own, i * V_OWN)
                    for t in range(TPC):
                        last = nc.vector.bn_stats(stats[:, t, :], X[:, tok(i, t), :])
                    own.done(last)
                    nc.vector.memset(spare[:], 0.0)
                    for t in range(TPC):
                        last = nc.vector.bn_aggr(mv[:, t, :], stats[:, t, :])
                    own.done(last)
                    nc.vector.tensor_scalar(var[:], mv[:, :, 1], LN_EPS, None, ALU.add).then_inc(var_ready, 1)
                    dve.wait_ge(rstd_ready, i + 1)
                    for t in range(TPC):
                        last = nc.vector.tensor_scalar(xn[:, t, :], X[:, tok(i, t), :], mv[:, t, 0:1], rstd[:, t:t + 1],
                                                       ALU.subtract, ALU.mult)
                    last.then_inc(xn_ready, 1)
                    for k in range(DC):
                        for m in range(ND):
                            if k == 0:
                                dve.wait_ge(raw_ready, i * ND + m + 1)
                                last = nc.vector.tensor_scalar(conv[:, m, :], raw[:, m, 0:CH], conv_w[:, m, 0:1],
                                                               None, ALU.mult)
                            else:
                                last = nc.vector.scalar_tensor_tensor(conv[:, m, :], raw[:, m, k:k + CH],
                                                                      conv_w[:, m, k:k + 1], conv[:, m, :],
                                                                      ALU.mult, ALU.add)
                                if k == DC - 1:
                                    last.then_inc(conv_ready, 1)
                        if k < DC - 1:
                            own.done(last)
                    dve.wait_ge(xp_ready, i + 1)
                    dve.wait_ge(dtr_ready, i + 1)
                    own.done(nc.vector.tensor_copy(bc3[:], bank[CB][0:SPLIT * BC, :]))
                    own.done(nc.vector.tensor_tensor(rest[:], bank[CB][0:SPLIT * BC, :], bc3[:], ALU.subtract))
                    own.done(nc.vector.tensor_copy(mid[:], rest[:]))
                    nc.vector.tensor_copy(bc3[BC:2 * BC, :], mid[BC:2 * BC, :])
                    own.done(nc.vector.tensor_tensor(low[:], rest[:], mid[:], ALU.subtract))
                    nc.vector.tensor_copy(bc3[2 * BC:, :], low[2 * BC:, :]).then_inc(bc_ready, 1)
                    dve.wait_ge(soft_ready, i + 1)
                    nc.vector.scalar_tensor_tensor(dt[:], dt[:], 0.0, soft[:], ALU.max, ALU.add).then_inc(dt_ready, 1)
                    dve.wait_ge(dt_ready, i + 1)
                    dve.wait_ge(xs_ready, i * ND + ND)
                    own.done(nc.vector.tensor_tensor(u[:], dt[:], xs[:], ALU.mult))
                    for n in range(DS):
                        dve.wait_ge(b_spread, i * DS + n + 1)
                        if n >= 1:
                            dve.wait_ge(h_ready, i * DS + n)
                        nc.vector.tensor_tensor(dBx[:], u[:],
                                                bank[BB + n % 2][:].rearrange("p (o t) -> p o t", o=1)
                                                .broadcast_to([P, ND, CH]), ALU.mult).then_inc(b_used, 1)
                        dve.wait_ge(b_used, i * DS + n + 1)
                        dve.wait_ge(dA_ready, i * DS + n + 1)
                        if n >= NH:
                            dve.wait_ge(g_summed, i * DS + n - NH + 1)
                        for m in range(ND):
                            last = nc.vector.tensor_tensor_scan(h[:, n % NH, m, :], dA[:, n % 2, m, :], dBx[:, m, :],
                                                                h_end[:, n, m:m + 1], ALU.mult, ALU.add)
                        last.then_inc(h_ready, 1)
                    dve.wait_ge(g_summed, i * DS + DS)
                    for m in range(ND):
                        last = nc.vector.scalar_tensor_tensor(yg[:, m, :], xs[:, m, :], skip_d[:, m:m + 1],
                                                              bank[YB + m][:], ALU.mult, ALU.add)
                    own.done(last)
                    dve.wait_ge(z_ready, i * ND + ND)
                    nc.vector.tensor_tensor(yg[:], yg[:], zs[:], ALU.mult).then_inc(yg_ready, 1)
                    for t in range(TPC):
                        dve.wait_ge(out_ready, i * TPC + t + 1)
                        last = nc.vector.tensor_tensor(X[:, tok(i, t), :], bank[BB + t][:, 0:DM], xn[:, t, :], ALU.add)
                    own.done(last)
                    own.close(V_OWN)

            @block.tensor
            def _(pe):
                pe.wait_ge(w_ready, 16 * (NW + 1))
                pe.wait_ge(spread_ready, 1)
                with pe.Fori(0, NCH) as i:
                    pe.wait_ge(xn_ready, i + 1)
                    for t in range(TPC):
                        for k in range(KD):
                            last = nc.tensor.transpose(bank[BB + k][:, t * P:(t + 1) * P],
                                                       xn[:, t, k * P:(k + 1) * P], ident[:])
                    last.then_inc(xT_ready, 1)
                    pe.wait_ge(xnT_ready, i + 1)
                    for m in range(2 * ND):
                        for k in range(KD):
                            last = nc.tensor.matmul(bank[m][:], w_in[:, k, m * P:(m + 1) * P], xnT[:, k, :],
                                                    start=(k == 0), stop=(k == KD - 1))
                        last.then_inc(proj_ready, 1)
                    pe.wait_ge(z_ready, i * ND + ND)
                    for m in range(ND):
                        pe.wait_ge(xs_ready, i * ND + m + 1)
                        last = nc.tensor.matmul(bank[CB][0:XP, :], w_xp[:, m, :], xs[:, m, :],
                                                start=(m == 0), stop=(m == ND - 1))
                    last.then_inc(xp_ready, 1)
                    pe.wait_ge(dtr_ready, i + 1)
                    for m in range(ND):
                        nc.tensor.matmul(bank[YB + m][:], w_dt[SPLIT * BC:XP, m * P:(m + 1) * P],
                                         dtr[SPLIT * BC:XP, :], start=True, stop=True).then_inc(dtp_ready, 1)
                    pe.wait_ge(bc_ready, i + 1)

                    def spread_bc(n):
                        if n >= 2:
                            pe.wait_ge(b_used, i * DS + n - 1)
                        nc.tensor.matmul(bank[BB + n % 2][:], spread[:, n, :], bc3[:],
                                         start=True, stop=True).then_inc(b_spread, 1)
                        if n >= 2:
                            pe.wait_ge(crep_ready, i * DS + n - 1)
                        nc.tensor.matmul(bank[CB + n % 2][:], spread[:, DS + n, :], bc3[:],
                                         start=True, stop=True).then_inc(c_spread, 1)

                    spread_bc(0)
                    spread_bc(1)
                    for n in range(DS):
                        if n + 2 < DS:
                            spread_bc(n + 2)
                        pe.wait_ge(g_ready, i * DS + n + 1)
                        for m in range(ND):
                            last = nc.tensor.matmul(bank[YB + m][:], ident[:], h[:, n % NH, m, :],
                                                    start=(n == 0), stop=(n == DS - 1))
                        last.then_inc(g_summed, 1)
                    pe.wait_ge(yg_ready, i + 1)
                    for t in range(TPC):
                        for m in range(ND):
                            last = nc.tensor.matmul(bank[BB + t][:, 0:DM], yg[:, m, t * P:(t + 1) * P], w_out[:, m, :],
                                                    start=(m == 0), stop=(m == ND - 1))
                        last.then_inc(out_ready, 1)


def staged(eng, stages):
    ahead = max(lead for lead, _ in stages)

    def step(s, at):
        for lead, run in stages:
            if not isinstance(s, int) or 0 <= s + lead < NCH:
                run(s + lead, (at + lead) % 2)

    for s in range(-ahead, 2):
        step(s, s)
    passes = (NCH - ahead - 2) // 2
    with eng.Fori(1, 1 + passes) as j:
        step(2 * j, 0)
        step(2 * j + 1, 1)
    for s in range(2 + 2 * passes, NCH):
        step(s, s)


def before(c, lag):
    return not isinstance(c, int) or c >= lag


class Norm:

    ORDERS = 2

    def __init__(self, nc, ctx, sem, name, eps):
        def sb(part, shape):
            return ctx.enter_context(nc.sbuf_tensor(f"{name}_{part}", shape, F32))

        self.nc, self.eps = nc, eps
        self.stats, self.mv = sb("stats", [P, TPC, 6]), sb("mv", [P, TPC, 2])
        self.var, self.rstd, self.spare = sb("var", [P, TPC]), sb("rstd", [P, TPC]), sb("spare", [P, 1])
        self.var_ready, self.rstd_ready = sem(f"{name}_var_ready"), sem(f"{name}_rstd_ready")

    def begin(self, own, src):
        for t in range(TPC):
            last = self.nc.vector.bn_stats(self.stats[:, t, :], src(t))
        own.done(last)
        self.nc.vector.memset(self.spare[:], 0.0)
        for t in range(TPC):
            last = self.nc.vector.bn_aggr(self.mv[:, t, :], self.stats[:, t, :])
        own.done(last)
        self.nc.vector.tensor_scalar(self.var[:], self.mv[:, :, 1], self.eps, None, ALU.add).then_inc(self.var_ready, 1)

    def power(self, pool, half, c):
        pool.wait_ge(self.var_ready, c + 1)
        self.nc.gpsimd.tensor_tensor(self.rstd[:], self.var[:], half[:], ALU.pow).then_inc(self.rstd_ready, 1)

    def scale(self, dve, c, out, src):
        dve.wait_ge(self.rstd_ready, c + 1)
        for t in range(TPC):
            last = self.nc.vector.tensor_scalar(out(t), src(t), self.mv[:, t, 0:1], self.rstd[:, t:t + 1],
                                                ALU.subtract, ALU.mult)
        return last


def feed_forward(nc, sem, X, ident, a, name, hidden, tail):
    NM = hidden // P
    with ExitStack() as ctx:
        def sb(part, shape, dt=F32):
            return ctx.enter_context(nc.sbuf_tensor(f"{name}_{part}", shape, dt))

        def sig(part):
            return sem(f"{name}_{part}")

        w1 = sb("w1", [P, KD, hidden])
        w2 = sb("w2", [P, NM, DM])
        b1 = sb("b1", [P, NM])
        b2 = sb("b2", [1, DM])
        ones = sb("ones", [P, P])
        half = sb("half", [P, TPC])
        n = sb("n", [P, 2, TPC, DM])
        hT = sb("hT", [P, 2, KD, CH])
        fT = sb("fT", [P, 2, NM, CH])
        f = sb("f", [P, 2, TPC, DM])
        norm_in = Norm(nc, ctx, sem, f"{name}_in", MAMBA_EPS if tail else LN_EPS)
        norm_out = Norm(nc, ctx, sem, f"{name}_out", LN_EPS)
        if tail:
            norm_mid = Norm(nc, ctx, sem, f"{name}_mid", MAMBA_EPS)
            in_w, in_b = sb("in_w", [P, KD]), sb("in_b", [P, KD])
            mid_w, mid_b = sb("mid_w", [P, 1, DM]), sb("mid_b", [P, 1, DM])
            x = sb("x", [P, TPC, DM])
        else:
            gamma = sb("gamma", [P, 2])
            bound = sb("bound", [P, 2, 2])
            below = sb("below", [P, KD * hidden])
        bank = [ctx.enter_context(nc.psum_tensor(f"{name}_bank{b}", [P, CH], F32)) for b in range(8)]
        TB, FB, OB = 0, 2, 6

        w_ready, const_ready, q_ready = sig("w_ready"), sig("const_ready"), sig("q_ready")
        n_ready, nT_ready, hT_ready = sig("n_ready"), sig("nT_ready"), sig("hT_ready")
        up_ready, up_read, down_ready, f_ready = sig("up_ready"), sig("up_read"), sig("down_ready"), sig("f_ready")
        f_used, x_ready = sig("f_used"), sig("x_ready")
        mid_ready, mid_affine, mid_own = sig("mid_ready"), sig("mid_affine"), sig("mid_own")
        first_own, second_own, setup_own = sig("first_own"), sig("second_own"), sig("setup_own")
        abs_ready, sum_ready = sig("abs_ready"), sig("sum_ready")
        loads = [(w1, "w1"), (w2, "w2"), (b1, "b1"), (b2, "b2")]
        if tail:
            loads += [(in_w, "in_w"), (in_b, "in_b"), (mid_w, "mid_w"), (mid_b, "mid_b")]
        N_LOADS = 16 * len(loads)
        leaked = sig("leaked") if tail else None
        fT_ready = leaked if tail else up_read
        FIRST, SECOND = Norm.ORDERS, (2 if tail else 1) * Norm.ORDERS + 1

        with nc.Block() as block:
            @block.sync
            def _(sp):
                for dst, src in loads:
                    sp.dma_start(dst[:], a[f"{name}_{src}"]).then_inc(w_ready, 16)
                if tail:
                    with sp.Fori(0, NCH) as c:
                        sp.wait_ge(f_used, c + 1)
                        sp.dma_start(x[:], a["x_tiles"][bass.ds(c, 1)].rearrange("o (t p) d -> p (o t) d", p=P)
                                     ).then_inc(x_ready, 16)

            @block.gpsimd
            def _(pool):
                nc.gpsimd.memset(half[:], -0.5).then_inc(const_ready, 1)
                nc.gpsimd.memset(ones[:], 1.0).then_inc(const_ready, 1)
                pool.wait_ge(const_ready, 2)
                pool.wait_ge(w_ready, N_LOADS)

                def first(c, b):
                    norm_in.power(pool, half, c)

                def second(c, b):
                    if tail:
                        norm_mid.power(pool, half, c)
                        pool.wait_ge(mid_ready, c + 1)
                        nc.gpsimd.tensor_tensor(f[:, b], f[:, b], mid_w[:].broadcast_to([P, TPC, DM]),
                                                ALU.mult).then_inc(mid_own, 1)
                        pool.wait_ge(mid_own, c + 1)
                        nc.gpsimd.tensor_tensor(f[:, b], f[:, b], mid_b[:].broadcast_to([P, TPC, DM]),
                                                ALU.add).then_inc(mid_affine, 1)
                    norm_out.power(pool, half, c)

                staged(pool, [(2, first), (0, second)])

            @block.scalar
            def _(act):
                act.wait_ge(w_ready, N_LOADS)
                if not tail:
                    nc.scalar.activation(below[:], w1[:].rearrange("p k e -> p (k e)"), ACT.Abs,
                                         accum_out=gamma[:, 0:1]).then_inc(abs_ready, 1)
                    act.wait_ge(abs_ready, 1)
                    nc.scalar.activation(below[:], w2[:].rearrange("p k e -> p (k e)"), ACT.Abs,
                                         accum_out=gamma[:, 1:2]).then_inc(abs_ready, 1)

                def transposed(c, b):
                    act.wait_ge(nT_ready, c + 1)
                    for k in range(KD):
                        if tail:
                            last = nc.scalar.activation(hT[:, b, k, :], bank[TB + k][:], ACT.Identity,
                                                        bias=in_b[:, k:k + 1], scale=in_w[:, k:k + 1])
                        else:
                            last = nc.scalar.copy(hT[:, b, k, :], bank[TB + k][:])
                    last.then_inc(hT_ready, 1)

                def up(c, b):
                    for m in range(NM):
                        act.wait_ge(up_ready, c * NM + m + 1)
                        if tail:
                            last = nc.scalar.activation(fT[:, b, m, :], bank[FB + m % 4][:], ACT.Identity,
                                                        bias=b1[:, m:m + 1])
                        else:
                            last = nc.scalar.activation(fT[:, b, m, :], bank[FB + m % 4][:], ACT.Relu,
                                                        bias=b1[:, m:m + 1])
                        last.then_inc(up_read, 1)

                def down(c, b):
                    act.wait_ge(f_used, c)
                    for t in range(TPC):
                        act.wait_ge(down_ready, c * TPC + t + 1)
                        nc.scalar.copy(f[:, b, t, :], bank[OB + t % 2][:, 0:DM]).then_inc(f_ready, 1)

                staged(act, [(1, transposed), (0, down), (1, up)])

            @block.vector
            def _(dve):
                nc.vector.memset(norm_out.stats[:], 0.0).then_inc(f_used, 1)
                dve.wait_ge(w_ready, N_LOADS)
                if not tail:
                    setup = Order(dve, setup_own)
                    dve.wait_ge(sum_ready, 1)
                    setup.done(nc.vector.tensor_scalar(bound[:, 0, :], bank[TB][:, 0:2], 0.5 / (hidden * DM),
                                                       0.5 * LN_EPS, ALU.mult, ALU.add))
                    setup.done(nc.vector.tensor_scalar(bound[:, 1, :], bound[:, 0, :], -1.0, None, ALU.mult))
                    for q, w in enumerate((w1, w2)):
                        flat = w[:].rearrange("p k e -> p (k e)")
                        setup.done(nc.vector.tensor_scalar(below[:], flat, bound[:, 1, q:q + 1], None, ALU.is_lt))
                        last = nc.vector.scalar_tensor_tensor(flat, flat, bound[:, 0, q:q + 1], below[:],
                                                              ALU.is_gt, ALU.subtract)
                        setup.done(last)
                    nc.vector.tensor_scalar(bound[:, 1, :], bound[:, 0, :], -1.0, None, ALU.mult).then_inc(q_ready, 1)

                def first(c, b):
                    own = Order(dve, first_own, c * FIRST)
                    norm_in.begin(own, lambda t: X[:, tok(c, t), :])
                    if before(c, 2):
                        dve.wait_ge(nT_ready, c - 1)
                    norm_in.scale(dve, c, lambda t: n[:, b, t, :], lambda t: X[:, tok(c, t), :]).then_inc(n_ready, 1)
                    own.close(FIRST)

                def second(c, b):
                    own = Order(dve, second_own, c * SECOND)
                    dve.wait_ge(f_ready, c * TPC + TPC)
                    part = lambda t: f[:, b, t, :]
                    if tail:
                        norm_mid.begin(own, part)
                        norm_mid.scale(dve, c, part, part).then_inc(mid_ready, 1)
                        dve.wait_ge(mid_affine, c + 1)
                    norm_out.begin(own, part)
                    own.done(norm_out.scale(dve, c, part, part))
                    if tail:
                        dve.wait_ge(x_ready, 16 * c + 16)
                    for t in range(TPC):
                        last = nc.vector.tensor_tensor(X[:, tok(c, t), :], x[:, t, :] if tail else X[:, tok(c, t), :],
                                                       part(t), ALU.add)
                    last.then_inc(f_used, 1)
                    own.close(SECOND)

                def leak(c, b):
                    for m in range(NM):
                        dve.wait_ge(up_read, c * NM + m + 1)
                        nc.vector.scalar_tensor_tensor(fT[:, b, m, :], fT[:, b, m, :], 0.01, fT[:, b, m, :],
                                                       ALU.mult, ALU.max).then_inc(leaked, 1)

                staged(dve, [(2, first), (0, second)] + ([(1, leak)] if tail else []))

            @block.tensor
            def _(pe):
                pe.wait_ge(w_ready, N_LOADS)
                pe.wait_ge(const_ready, 2)
                if not tail:
                    pe.wait_ge(abs_ready, 2)
                    nc.tensor.matmul(bank[TB][:, 0:2], ones[:], gamma[:], start=True, stop=True).then_inc(sum_ready, 1)
                    pe.wait_ge(q_ready, 1)

                def transposes(c, b):
                    pe.wait_ge(n_ready, c + 1)
                    pe.wait_ge(hT_ready, c)
                    for t in range(TPC):
                        for k in range(KD):
                            last = nc.tensor.transpose(bank[TB + k][:, t * P:(t + 1) * P], n[:, b, t, k * P:(k + 1) * P],
                                                       ident[:])
                    last.then_inc(nT_ready, 1)

                def up(c, b):
                    pe.wait_ge(hT_ready, c + 1)
                    for m in range(NM):
                        pe.wait_ge(up_read, c * NM + max(0, m - 3))
                        for k in range(KD):
                            last = nc.tensor.matmul(bank[FB + m % 4][:], w1[:, k, m * P:(m + 1) * P], hT[:, b, k, :],
                                                    start=(k == 0), stop=(k == KD - 1))
                        last.then_inc(up_ready, 1)

                def down(c, b):
                    pe.wait_ge(fT_ready, c * NM + NM)
                    for t in range(TPC):
                        pe.wait_ge(f_ready, c * TPC + max(0, t - 1))
                        out = bank[OB + t % 2]
                        for m in range(NM):
                            nc.tensor.matmul(out[:, 0:DM], fT[:, b, m, t * P:(t + 1) * P], w2[:, m, :],
                                             start=(m == 0), stop=False)
                        if tail:
                            for k in range(KD):
                                nc.tensor.matmul(out[:, k * P:(k + 1) * P], hT[:, b, k, t * P:(t + 1) * P], ident[:],
                                                 start=False, stop=False)
                        nc.tensor.matmul(out[:, 0:DM], ones[0:1, :], b2[:], start=False,
                                         stop=True).then_inc(down_ready, 1)

                staged(pe, [(1, transposes), (0, down), (1, up)])


H = 16
HD = DM // H
SLOTS = ((0, 0), (0, 1), (1, 0), (1, 1), (0, 2), (2, 0))
QK_ROWS = len(SLOTS) * HD
ROWS = QK_ROWS + SPLIT
QS = 1.0 / 64
KC = 2 * CH
NKC = T // KC
RING = 8
VW = 32


def project(nc, sem, X, V, ident, a, parts_dram):
    with ExitStack() as ctx:
        def sb(part, shape, dt=F32):
            return ctx.enter_context(nc.sbuf_tensor(f"p_{part}", shape, dt))

        def sig(part):
            return sem(f"p_{part}")

        w = sb("w", [P, KD, 3 * DM])
        qk_b = sb("qk_b", [P, 2, KD])
        v_b = sb("v_b", [1, DM])
        ones, half = sb("ones", [1, P]), sb("half", [P, TPC])
        n = sb("n", [P, 2, TPC, DM])
        nT = sb("nT", [P, 2, KD, CH])
        full = sb("full", [P, 2, 2, KD, CH])
        parts = sb("parts", [P, 2, 2, SPLIT, KD, CH], BF16)
        norm = Norm(nc, ctx, sem, "p_norm", LN_EPS)
        bank = [ctx.enter_context(nc.psum_tensor(f"p_bank{b}", [P, CH], F32)) for b in range(8)]
        TB, QB, VB = 0, 2, 6

        w_ready, const_ready, bias_ready = sig("w_ready"), sig("const_ready"), sig("bias_ready")
        n_ready, nT_ps, nT_ready = sig("n_ready"), sig("nT_ps"), sig("nT_ready")
        qk_ps, full_ready, v_ps, v_ready = sig("qk_ps"), sig("full_ready"), sig("v_ps"), sig("v_ready")
        split_ready, norm_own, split_own = sig("split_ready"), sig("norm_own"), sig("split_own")
        stored = [sig(f"stored{b}") for b in range(2)]
        loads = [(w, "w"), (qk_b, "qk_b"), (v_b, "v_b")]
        N_LOADS = 16 * len(loads)
        STORES = 16 * 2 * SPLIT
        SPLITS = 3

        with nc.Block() as block:
            @block.sync
            def _(sp):
                for dst, src in loads:
                    sp.dma_start(dst[:], a[f"attn_{src}"]).then_inc(w_ready, 16)

                def store(c, b):
                    for x in range(2):
                        sp.wait_ge(split_ready, 2 * c + x + 1)
                        for s in range(SPLIT):
                            sp.dma_start(parts_dram[x, s, :, :, bass.ds(c * CH, CH)].rearrange("m p t -> p m t"),
                                         parts[:, b, x, s]).then_inc(stored[b], 16)

                staged(sp, [(0, store), (1, lambda c, b: None)])
                for b in range(2):
                    sp.wait_ge(stored[b], NCH // 2 * STORES)

            @block.gpsimd
            def _(pool):
                nc.gpsimd.memset(half[:], -0.5).then_inc(const_ready, 1)
                nc.gpsimd.memset(ones[:], 1.0).then_inc(const_ready, 1)
                pool.wait_ge(const_ready, 2)
                staged(pool, [(2, lambda c, b: norm.power(pool, half, c))])

            @block.scalar
            def _(act):
                act.wait_ge(w_ready, N_LOADS)
                nc.scalar.mul(qk_b[:, 0, :], qk_b[:, 0, :], QS).then_inc(bias_ready, 1)
                act.wait_ge(bias_ready, 1)

                def transposed(c, b):
                    act.wait_ge(nT_ps, c + 1)
                    for k in range(KD):
                        last = nc.scalar.copy(nT[:, b, k, :], bank[TB + k][:])
                    last.then_inc(nT_ready, 1)

                def projected(c, b):
                    if before(c, 2):
                        act.wait_ge(split_ready, 2 * c - 2)
                    for x in range(2):
                        for m in range(KD):
                            act.wait_ge(qk_ps, c * 2 * KD + x * KD + m + 1)
                            nc.scalar.activation(full[:, b, x, m, :], bank[QB + x * KD + m][:], ACT.Identity,
                                                 bias=qk_b[:, x, m:m + 1],
                                                 scale=QS if x == 0 else 1.0).then_inc(full_ready, 1)
                    for t in range(TPC):
                        act.wait_ge(v_ps, c * TPC + t + 1)
                        nc.scalar.copy(V[:, tok(c, t), :], bank[VB + t % 2][:, 0:DM]).then_inc(v_ready, 1)

                staged(act, [(1, transposed), (0, projected)])

            @block.vector
            def _(dve):
                def normed(c, b):
                    own = Order(dve, norm_own, c * Norm.ORDERS)
                    norm.begin(own, lambda t: X[:, tok(c, t), :])
                    if before(c, 2):
                        dve.wait_ge(nT_ps, c - 1)
                    norm.scale(dve, c, lambda t: n[:, b, t, :], lambda t: X[:, tok(c, t), :]).then_inc(n_ready, 1)

                def split(c, b):
                    own = Order(dve, split_own, c * 2 * SPLITS)
                    if before(c, 2):
                        dve.wait_ge(stored[b], (c - b) * (STORES // 2))
                    for x in range(2):
                        f = full[:, b, x]
                        dve.wait_ge(full_ready, c * 2 * KD + x * KD + KD)
                        own.done(nc.vector.tensor_copy(parts[:, b, x, 0], f))
                        own.done(nc.vector.tensor_tensor(f, f, parts[:, b, x, 0], ALU.subtract))
                        own.done(nc.vector.tensor_copy(parts[:, b, x, 1], f))
                        nc.vector.tensor_tensor(parts[:, b, x, 2], f, parts[:, b, x, 1],
                                                ALU.subtract).then_inc(split_ready, 1)
                    own.close(2 * SPLITS)

                staged(dve, [(2, normed), (0, split)])

            @block.tensor
            def _(pe):
                pe.wait_ge(w_ready, N_LOADS)
                pe.wait_ge(const_ready, 2)

                def transposes(c, b):
                    pe.wait_ge(n_ready, c + 1)
                    pe.wait_ge(nT_ready, c)
                    for t in range(TPC):
                        for k in range(KD):
                            last = nc.tensor.transpose(bank[TB + k][:, t * P:(t + 1) * P], n[:, b, t, k * P:(k + 1) * P],
                                                       ident[:])
                    last.then_inc(nT_ps, 1)

                def projections(c, b):
                    pe.wait_ge(nT_ready, c + 1)
                    for x in range(2):
                        pe.wait_ge(full_ready, c * 2 * KD)
                        for m in range(KD):
                            for k in range(KD):
                                last = nc.tensor.matmul(bank[QB + x * KD + m][:],
                                                        w[:, k, x * DM + m * P:x * DM + (m + 1) * P], nT[:, b, k, :],
                                                        start=(k == 0), stop=(k == KD - 1))
                            last.then_inc(qk_ps, 1)
                    for t in range(TPC):
                        pe.wait_ge(v_ready, c * TPC + max(0, t - 1))
                        out = bank[VB + t % 2][:, 0:DM]
                        for k in range(KD):
                            nc.tensor.matmul(out, nT[:, b, k, t * P:(t + 1) * P], w[:, k, 2 * DM:3 * DM],
                                             start=(k == 0), stop=False)
                        nc.tensor.matmul(out, ones[:], v_b[:], start=False, stop=True).then_inc(v_ps, 1)

                staged(pe, [(1, transposes), (0, projections)])


def head_events():
    events, j = [], 0
    for s in range(NCH + 2):
        units = [(s * TPC + t, c) for t in range(TPC) for c in range(NKC)] if s < NCH else []
        g = s - 1
        blocks = []
        if 0 <= g < NCH:
            blocks = [(g, kb, None) for kb in range(TPC * (g + 1), NT)] + [(g, TPC * g + r, r) for r in range(TPC)]
        heads, tails = [], []
        if 0 <= g < NCH:
            heads.append([("row", g)])
        if 0 <= s - 2 < NCH:
            heads.append([("zcopy", s - 2)])
            heads.append([("zout", s - 2)])
        made = []
        for q, blk in enumerate(blocks):
            made.append(("block", j + q, blk))
            if q >= 2:
                made.append(("value", j + q - 2, blocks[q - 2], q == 2, False))
        for q in (len(blocks) - 2, len(blocks) - 1):
            if blocks:
                made.append(("value", j + q, blocks[q], q == 0, q == len(blocks) - 1))
        j += len(blocks)
        lead = 3
        taken = 0
        for q in range(max(len(units), lead)):
            if q < len(units):
                events.append(("scores", units[q]))
            if q < len(heads):
                events += heads[q]
            if q >= lead - 1:
                upto = len(made) * (q - lead + 2) // max(1, len(units) - lead + 1) if units else len(made)
                events += made[taken:upto]
                taken = max(taken, upto)
        events += made[taken:]
        if s < NCH:
            events.append(("max", s))
    return events


def low_width(i, c):
    return max(0, min(KC, P * (i + 1) - KC * c))


def attend(nc, sem, V, ident, a, parts_dram, z_dram):
    with ExitStack() as ctx:
        def sb(part, shape, dt=F32):
            return ctx.enter_context(nc.sbuf_tensor(f"a_{part}", shape, dt))

        def sig(part):
            return sem(f"a_{part}")

        q = sb("q", [ROWS, 2, T], BF16)
        k = sb("k", [ROWS, 2, T], BF16)
        vh = sb("vh", [P, NT, VW])
        sel = sb("sel", [P, VW])
        identb = sb("identb", [P, P], BF16)
        prob = sb("prob", [P, RING, CH])
        zeros = sb("zeros", [P, CH])
        keep = sb("keep", [P, P])
        neg_c = sb("neg_c", [P, 2, NT, NKC])
        sums_c = sb("sums_c", [P, 2, NT, NKC])
        neg = sb("neg", [P, TPC])
        neg_rest = sb("neg_rest", [P, TPC])
        neg3 = sb("neg3", [P, TPC, ROWS], BF16)
        lift = sb("lift", [P, TPC, NKC])
        weight = sb("weight", [P, 2, TPC, NKC])
        part_l = sb("part_l", [P, TPC, NKC])
        total = sb("total", [P, TPC])
        zT = sb("zT", [P, CH])
        z = sb("z", [P, 2, NT, HD])
        S = [ctx.enter_context(nc.psum_tensor(f"a_S{b}", [P, KC], F32)) for b in range(2)]
        B = [ctx.enter_context(nc.psum_tensor(f"a_B{b}", [P, CH], F32)) for b in range(2)]
        zacc = ctx.enter_context(nc.psum_tensor("a_zacc", [P, CH], F32))
        misc = ctx.enter_context(nc.psum_tensor("a_misc", [P, CH], F32))

        const_ready, const_loaded, identb_ready, pool_own, vh_ready = (
            sig("const_ready"), sig("const_loaded"), sig("identb_ready"), sig("pool_own"), sig("vh_ready"))
        loaded = [sig(f"loaded{b}") for b in range(2)]
        z_stored = [sig(f"z_stored{b}") for b in range(2)]
        scored, unit_max, low_summed = sig("scored"), sig("unit_max"), sig("low_summed")
        neg_ready, neg_T, row_ready, weight_ready = sig("neg_ready"), sig("neg_T"), sig("row_ready"), sig("weight_ready")
        block_scored, prob_ready, masked, valued = sig("block_scored"), sig("prob_ready"), sig("masked"), sig("valued")
        z_copied, z_T, z_out, own_sem = sig("z_copied"), sig("z_T"), sig("z_out"), sig("own")

        events = head_events()
        UNITS, BLOCKS = NT * NKC, sum(e[0] == "block" for e in events)
        DIAGS = NT
        LOWS = sum(low_width(i, c) > 0 for i in range(NT) for c in range(NKC))
        OWN = NCH * (4 + 4)
        LOADS = 16 * 2 * len(SLOTS)
        for s in (unit_max, low_summed, z_out, prob_ready, valued, z_copied, weight_ready, z_T, *z_stored):
            nc.sync.sem_inc(s, FREE)


        def unit_number(u):
            return u[0] * NKC + u[1]

        def lows_upto(u):
            return sum(low_width(n // NKC, n % NKC) > 0 for n in range(unit_number(u) + 1))

        def blocks_upto(g):
            return sum(e[0] == "block" and e[2][0] <= g for e in events)

        def every_head(eng, head):
            with eng.Fori(0, H // 2) as j:
                head(2 * j, 0)
                head(2 * j + 1, 1)

        with nc.Block() as block:
            @block.sync
            def _(sp):
                sp.dma_start(sel[:], a["sel"]).then_inc(const_loaded, 16)

                def load(h, b):
                    for s, (pq, pk) in enumerate(SLOTS):
                        for dst, x, part in ((q, 0, pq), (k, 1, pk)):
                            src = parts_dram[x, part].rearrange("m p t -> (m p) t")
                            sp.dma_start(dst[s * HD:(s + 1) * HD, b, :], src[bass.ds(h * HD, HD), :]
                                         ).then_inc(loaded[b], 16)

                load(0, 0)
                load(1, 1)

                def store(h, b):
                    sp.wait_ge(z_out, FREE + (h + 1) * NCH)
                    sp.dma_start(z_dram[bass.ds(h, 1)].rearrange("o (i p) d -> p (o i) d", p=P),
                                 z[:, b]).then_inc(z_stored[b], 16)

                with sp.Fori(0, H // 2 - 1) as j:
                    for b in range(2):
                        h = 2 * j + b
                        sp.wait_ge(valued, FREE + (h + 1) * BLOCKS)
                        load(h + 2, b)
                        store(h, b)
                store(H - 2, 0)
                store(H - 1, 1)
                for b in range(2):
                    sp.wait_ge(z_stored[b], FREE + H // 2 * 16)

            @block.gpsimd
            def _(pool):
                own = Order(pool, pool_own)
                for tile, value in ((vh[:], 0.0), (k[QK_ROWS:, :, :], 1.0), (zeros[:], 0.0), (neg3[:], 0.0),
                                    (sums_c[:], 0.0), (neg_c[:], 0.0)):
                    own.done(nc.gpsimd.memset(tile, value))
                own.done(nc.gpsimd.memset(keep[:], 1.0))
                own.done(nc.gpsimd.affine_select(out=keep[:], in_=keep[:], pattern=[[-1, P]], compare_op=ALU.is_ge,
                                                 fill=0.0, base=0, channel_multiplier=1))
                nc.gpsimd.memset(vh[:, :, HD:HD + 1], 1.0).then_inc(const_ready, 1)
                pool.wait_ge(const_ready, 1)

                def head(h, b):
                    pool.wait_ge(valued, FREE + h * BLOCKS)
                    nc.gpsimd.tensor_copy(vh[:, :, 0:HD], V[:, :, bass.ds(h * HD, HD)]).then_inc(vh_ready, 1)
                    for e in events:
                        if e[0] == "block" and e[2][2] is not None:
                            r = e[2][2]
                            pool.wait_ge(prob_ready, FREE + h * BLOCKS + e[1] + 1)
                            blk = prob[:, e[1] % RING, r * P:(r + 1) * P]
                            nc.gpsimd.tensor_tensor(blk, blk, keep[:], ALU.mult).then_inc(masked, 1)

                every_head(pool, head)

            @block.scalar
            def _(act):
                act.wait_ge(const_ready, 1)

                def head(h, b):
                    for e in events:
                        if e[0] == "scores" and low_width(*e[1]):
                            i, c = e[1]
                            w = low_width(i, c)
                            act.wait_ge(unit_max, FREE + h * UNITS + unit_number(e[1]) + 1)
                            nc.scalar.activation(S[unit_number(e[1]) % 2][:, 0:w], S[unit_number(e[1]) % 2][:, 0:w],
                                                 ACT.Exp, bias=neg_c[:, b, i, c:c + 1],
                                                 accum_out=sums_c[:, b, i, c:c + 1]).then_inc(low_summed, 1)
                        elif e[0] == "row":
                            act.wait_ge(neg_ready, h * NCH + e[1] + 1)
                            nc.scalar.activation(weight[:, e[1] % 2], lift[:], ACT.Exp).then_inc(weight_ready, 1)
                        elif e[0] == "block":
                            j, (g, kb, r) = e[1], e[2]
                            w = CH if r is None else (r + 1) * P
                            act.wait_ge(block_scored, h * BLOCKS + j + 1)
                            act.wait_ge(valued, FREE + h * BLOCKS + max(0, j - RING + 1))
                            nc.scalar.activation(prob[:, j % RING, 0:w], B[j % 2][:, 0:w],
                                                 ACT.Exp).then_inc(prob_ready, 1)

                every_head(act, head)

            @block.vector
            def _(dve):
                dve.wait_ge(const_ready, 1)
                nc.vector.tensor_copy(identb[:], ident[:]).then_inc(identb_ready, 1)

                def head(h, b):
                    own = Order(dve, own_sem, h * OWN)
                    for e in events:
                        if e[0] == "scores":
                            (i, c), u = e[1], unit_number(e[1])
                            dve.wait_ge(scored, h * UNITS + u + 1)
                            nc.vector.tensor_reduce(neg_c[:, b, i, c:c + 1], S[u % 2][:], AX.X, ALU.max,
                                                    negate=True).then_inc(unit_max, 1)
                        elif e[0] == "max":
                            g = e[1]
                            units = neg_c[:, b, g * TPC:(g + 1) * TPC, :]
                            dve.wait_ge(unit_max, FREE + h * UNITS + (g + 1) * TPC * NKC)
                            own.done(nc.vector.tensor_reduce(neg[:], units, AX.X, ALU.min))
                            dve.wait_ge(weight_ready, FREE + h * NCH + g)
                            nc.vector.tensor_tensor(lift[:], neg[:].rearrange("p (t o) -> p t o", o=1)
                                                    .broadcast_to([P, TPC, NKC]), units, ALU.subtract)
                            own.done(nc.vector.tensor_copy(neg3[:, :, QK_ROWS], neg[:]))
                            own.done(nc.vector.tensor_tensor(neg_rest[:], neg[:], neg3[:, :, QK_ROWS], ALU.subtract))
                            own.done(nc.vector.tensor_copy(neg3[:, :, QK_ROWS + 1], neg_rest[:]))
                            nc.vector.tensor_tensor(neg3[:, :, QK_ROWS + 2], neg_rest[:], neg3[:, :, QK_ROWS + 1],
                                                    ALU.subtract).then_inc(neg_ready, 1)
                        elif e[0] == "row":
                            g = e[1]
                            dve.wait_ge(neg_T, h * NCH + g + 1)
                            nc.vector.tensor_copy(q[QK_ROWS:, b, g * CH:(g + 1) * CH],
                                                  misc[QK_ROWS:ROWS, :]).then_inc(row_ready, 1)
                        elif e[0] == "zcopy":
                            dve.wait_ge(valued, FREE + h * BLOCKS + blocks_upto(e[1]))
                            dve.wait_ge(z_T, FREE + h * NCH + e[1])
                            nc.vector.tensor_copy(zT[:], zacc[:]).then_inc(z_copied, 1)
                        elif e[0] == "zout":
                            g = e[1]
                            rows = slice(g * TPC, (g + 1) * TPC)
                            dve.wait_ge(weight_ready, FREE + h * NCH + g + 1)
                            own.done(nc.vector.tensor_tensor(part_l[:], weight[:, g % 2], sums_c[:, b, rows, :], ALU.mult))
                            own.done(nc.vector.tensor_reduce(total[:], part_l[:], AX.X, ALU.add))
                            dve.wait_ge(z_T, FREE + h * NCH + g + 1)
                            zt = misc[:, 0:TPC * VW].rearrange("p (t v) -> p t v", v=VW)
                            own.done(nc.vector.tensor_tensor(total[:], total[:], zt[:, :, HD], ALU.add))
                            own.done(nc.vector.reciprocal(total[:], total[:]))
                            if g == 0:
                                dve.wait_ge(z_stored[b], FREE + (h - b) * 8)
                            nc.vector.tensor_tensor(z[:, b, rows, :], zt[:, :, 0:HD],
                                                    total[:].rearrange("p (t o) -> p t o", o=1)
                                                    .broadcast_to([P, TPC, HD]), ALU.mult).then_inc(z_out, 1)
                            dve.wait_ge(z_out, FREE + h * NCH + g + 1)
                    own.close(OWN)

                every_head(dve, head)

            @block.tensor
            def _(pe):
                pe.wait_ge(const_ready, 1)
                pe.wait_ge(const_loaded, 16)
                pe.wait_ge(identb_ready, 1)

                def head(h, b):
                    pe.wait_ge(loaded[b], (h - b) * (LOADS // 2) + LOADS)
                    for e in events:
                        if e[0] == "scores":
                            (i, c), u = e[1], unit_number(e[1])
                            pe.wait_ge(unit_max, FREE + h * UNITS + max(0, u - 1))
                            pe.wait_ge(low_summed, FREE + h * LOWS + (lows_upto((((u - 2) // NKC), (u - 2) % NKC)) if u >= 2 else 0))
                            for s in range(KC // CH):
                                last = nc.tensor.matmul(S[u % 2][:, s * CH:(s + 1) * CH],
                                                        q[0:QK_ROWS, b, i * P:(i + 1) * P],
                                                        k[0:QK_ROWS, b, c * KC + s * CH:c * KC + (s + 1) * CH],
                                                        start=True, stop=True)
                            last.then_inc(scored, 1)
                        elif e[0] == "row":
                            g = e[1]
                            pe.wait_ge(neg_ready, h * NCH + g + 1)
                            pe.wait_ge(z_out, FREE + h * NCH + max(0, g - 1))
                            for t in range(TPC):
                                last = nc.tensor.matmul(misc[0:ROWS, t * P:(t + 1) * P], neg3[:, t, :], identb[:],
                                                        start=True, stop=True)
                            last.then_inc(neg_T, 1)
                        elif e[0] == "block":
                            j, (g, kb, r) = e[1], e[2]
                            w = CH if r is None else (r + 1) * P
                            pe.wait_ge(row_ready, h * NCH + g + 1)
                            pe.wait_ge(prob_ready, FREE + h * BLOCKS + max(0, j - 1))
                            nc.tensor.matmul(B[j % 2][:, 0:w], k[:, b, kb * P:(kb + 1) * P],
                                             q[:, b, g * CH:g * CH + w], start=True, stop=True).then_inc(block_scored, 1)
                        elif e[0] == "value":
                            _, j, (g, kb, r), first, final = e
                            col = kb % TPC * 32
                            if first:
                                pe.wait_ge(z_copied, FREE + h * NCH + g)
                                pe.wait_ge(vh_ready, h + 1)
                            if r is None:
                                pe.wait_ge(prob_ready, FREE + h * BLOCKS + j + 1)
                                last = nc.tensor.matmul(zacc[col:col + VW, :], vh[:, kb, :], prob[:, j % RING, :],
                                                        start=(kb < TPC * (g + 2)), stop=False)
                            else:
                                pe.wait_ge(masked, h * DIAGS + kb + 1)
                                if g == NCH - 1:
                                    nc.tensor.matmul(zacc[col:col + VW, :], vh[:, kb, :], zeros[:],
                                                     start=True, stop=False)
                                if r > 0:
                                    nc.tensor.matmul(zacc[col:col + VW, 0:r * P], vh[:, kb, :],
                                                     prob[:, j % RING, 0:r * P], start=False, stop=False)
                                last = nc.tensor.matmul(zacc[col:col + HD, r * P:(r + 1) * P], vh[:, kb, 0:HD],
                                                        prob[:, j % RING, r * P:(r + 1) * P], start=False, stop=True)
                            last.then_inc(valued, 1)
                        elif e[0] == "zout":
                            g = e[1]
                            pe.wait_ge(z_copied, FREE + h * NCH + g + 1)
                            pe.wait_ge(row_ready, h * NCH + min(NCH, g + 2))
                            for t in range(TPC):
                                last = nc.tensor.matmul(misc[:, t * VW:(t + 1) * VW], zT[:, t * P:(t + 1) * P], sel[:],
                                                        start=True, stop=True)
                            last.then_inc(z_T, 1)

                every_head(pe, head)


def attention_out(nc, sem, X, a, z_dram):
    with ExitStack() as ctx:
        def sb(part, shape, dt=F32):
            return ctx.enter_context(nc.sbuf_tensor(f"o_{part}", shape, dt))

        def sig(part):
            return sem(f"o_{part}")

        gamma, beta, half = sb("gamma", [P, 1, DM]), sb("beta", [P, 1, DM]), sb("half", [P, TPC])
        f = sb("f", [P, 2, TPC, DM])
        z = sb("z", [P, 2, TPC, DM])
        z_tiles = z_dram.rearrange("h q d -> (h q d)").rearrange("(j p d) -> p j d", p=P, d=DM)
        z_ready = [sig(f"z_ready{b}") for b in range(2)]
        norm_in, norm_mid, norm_out = (Norm(nc, ctx, sem, f"o_{x}", LN_EPS) for x in ("in", "mid", "out"))
        w_ready, const_ready = sig("w_ready"), sig("const_ready")
        mid_ready, mid_own, mid_affine, first_own, second_own = (
            sig("mid_ready"), sig("mid_own"), sig("mid_affine"), sig("first_own"), sig("second_own"))
        FIRST, SECOND = 2 * Norm.ORDERS + 2, Norm.ORDERS + 2

        with nc.Block() as block:
            @block.sync
            def _(sp):
                sp.dma_start(gamma[:], a["attn_gamma"]).then_inc(w_ready, 16)
                sp.dma_start(beta[:], a["attn_beta"]).then_inc(w_ready, 16)

                def load(c, b):
                    if before(c, 2):
                        sp.wait_ge(mid_ready, c - 1)
                    sp.dma_start(z[:, b], z_tiles[:, bass.ds(c * TPC, TPC), :]).then_inc(z_ready[b], 16)

                staged(sp, [(2, load), (0, lambda c, b: None)])

            @block.gpsimd
            def _(pool):
                nc.gpsimd.memset(half[:], -0.5).then_inc(const_ready, 1)
                pool.wait_ge(const_ready, 1)
                pool.wait_ge(w_ready, 32)

                def first(c, b):
                    norm_in.power(pool, half, c)
                    norm_mid.power(pool, half, c)
                    pool.wait_ge(mid_ready, c + 1)
                    nc.gpsimd.tensor_tensor(f[:, b], f[:, b], gamma[:].broadcast_to([P, TPC, DM]),
                                            ALU.mult).then_inc(mid_own, 1)
                    pool.wait_ge(mid_own, c + 1)
                    nc.gpsimd.tensor_tensor(f[:, b], f[:, b], beta[:].broadcast_to([P, TPC, DM]),
                                            ALU.add).then_inc(mid_affine, 1)

                staged(pool, [(1, first), (0, lambda c, b: norm_out.power(pool, half, c))])

            @block.vector
            def _(dve):
                def first(c, b):
                    own = Order(dve, first_own, c * FIRST)
                    part = lambda t: f[:, b, t, :]
                    norm_in.begin(own, lambda t: X[:, tok(c, t), :])
                    own.done(norm_in.scale(dve, c, part, lambda t: X[:, tok(c, t), :]))
                    dve.wait_ge(z_ready[b], (c - b) * 8 + 16)
                    own.done(nc.vector.tensor_tensor(f[:, b], f[:, b], z[:, b], ALU.add))
                    norm_mid.begin(own, part)
                    norm_mid.scale(dve, c, part, part).then_inc(mid_ready, 1)
                    own.close(FIRST)

                def second(c, b):
                    own = Order(dve, second_own, c * SECOND)
                    part = lambda t: f[:, b, t, :]
                    dve.wait_ge(mid_affine, c + 1)
                    norm_out.begin(own, part)
                    own.done(norm_out.scale(dve, c, part, part))
                    for t in range(TPC):
                        last = nc.vector.tensor_tensor(X[:, tok(c, t), :], X[:, tok(c, t), :], part(t), ALU.add)
                    own.done(last)
                    own.close(SECOND)

                staged(dve, [(1, first), (0, second)])


NE = 16
NG = 4
GE = NE // NG
TOP_K = 4
TOP_G = 2
SCALE = 2.5
ME = 128
NX = NE + 2 * ME // ME


def normed_transposed(nc, sem, X, nT, ident, name, extra=None):
    with ExitStack() as ctx:
        def sb(part, shape, dt=F32):
            return ctx.enter_context(nc.sbuf_tensor(f"{name}_{part}", shape, dt))

        def sig(part):
            return sem(f"{name}_{part}")

        half = sb("half", [P, TPC])
        n = sb("n", [P, 2, TPC, DM])
        norm = Norm(nc, ctx, sem, f"{name}_norm", LN_EPS)
        bank = [ctx.enter_context(nc.psum_tensor(f"{name}_bank{b}", [P, CH], F32)) for b in range(4)]
        const_ready, n_ready, nT_ps, nT_ready, own_sem = (
            sig("const_ready"), sig("n_ready"), sig("nT_ps"), sig("nT_ready"), sig("own"))

        with nc.Block() as block:
            @block.gpsimd
            def _(pool):
                nc.gpsimd.memset(half[:], -0.5).then_inc(const_ready, 1)
                pool.wait_ge(const_ready, 1)
                staged(pool, [(1, lambda c, b: norm.power(pool, half, c))])

            @block.vector
            def _(dve):
                def normed(c, b):
                    own = Order(dve, own_sem, c * Norm.ORDERS)
                    norm.begin(own, lambda t: X[:, tok(c, t), :])
                    if before(c, 2):
                        dve.wait_ge(nT_ps, c - 1)
                    norm.scale(dve, c, lambda t: n[:, b, t, :], lambda t: X[:, tok(c, t), :]).then_inc(n_ready, 1)

                staged(dve, [(2, normed)])

            @block.tensor
            def _(pe):
                def transposes(c, b):
                    pe.wait_ge(n_ready, c + 1)
                    if before(c, 2):
                        pe.wait_ge(nT_ready, c - 1)
                    for t in range(TPC):
                        for k in range(KD):
                            last = nc.tensor.transpose(bank[b * KD + k][:, t * P:(t + 1) * P],
                                                       n[:, b, t, k * P:(k + 1) * P], ident[:])
                    last.then_inc(nT_ps, 1)

                staged(pe, [(2, transposes)])

            @block.scalar
            def _(act):
                def copied(c, b):
                    act.wait_ge(nT_ps, c + 1)
                    for k in range(KD):
                        last = nc.scalar.copy(nT[:, k, bass.ds(c * CH, CH)], bank[b * KD + k][:])
                    last.then_inc(nT_ready, 1)

                staged(act, [(1, copied)])


def route(nc, sem, nT, combine, a):
    with ExitStack() as ctx:
        def sb(part, shape, dt=F32):
            return ctx.enter_context(nc.sbuf_tensor(f"g_{part}", shape, dt))

        def sig(part):
            return sem(f"g_{part}")

        w = sb("w", [P, KD, NE])
        bias = sb("bias", [P, 1, NE])
        score = sb("score", [P, NT, NE])
        group = sb("group", [P, NT, NG])
        pair = sb("pair", [P, NT, NG])
        g_rank = sb("g_rank", [P, NT, NG])
        wins = sb("wins", [P, NT, 1])
        rank = sb("rank", [P, NT, NE])
        beaten = sb("beaten", [P, NT, NE])
        total = sb("total", [P, NT, 1])
        logits = ctx.enter_context(nc.psum_tensor("g_logits", [P, NT, NE], F32))
        w_ready, logit_ready, score_ready, own_sem = sig("w_ready"), sig("logit_ready"), sig("score_ready"), sig("own")
        nT3 = nT[:].rearrange("p k (j t) -> p k j t", t=P)

        with nc.Block() as block:
            @block.sync
            def _(sp):
                sp.dma_start(w[:], a["gate_w"]).then_inc(w_ready, 16)
                sp.dma_start(bias[:], a["gate_b"]).then_inc(w_ready, 16)

            @block.tensor
            def _(pe):
                pe.wait_ge(w_ready, 32)
                for i in range(NT):
                    for k in range(KD):
                        last = nc.tensor.matmul(logits[:, i, :], nT3[:, k, i, :], w[:, k, :],
                                                start=(k == 0), stop=(k == KD - 1))
                last.then_inc(logit_ready, 1)

            @block.scalar
            def _(act):
                act.wait_ge(logit_ready, 1)
                nc.scalar.activation(score[:], logits[:], ACT.Sigmoid).then_inc(score_ready, 1)

            @block.vector
            def _(dve):
                own = Order(dve, own_sem)
                tt = nc.vector.tensor_tensor
                dve.wait_ge(w_ready, 32)
                dve.wait_ge(score_ready, 1)
                own.done(tt(score[:], score[:], bias[:].broadcast_to([P, NT, NE]), ALU.add))
                member = score[:].rearrange("p i (g e) -> p i g e", e=GE)
                pairs = [(x, y) for x in range(GE) for y in range(x + 1, GE)]
                for n, (x, y) in enumerate(pairs):
                    dst = pair if n else group
                    own.done(tt(dst[:], member[:, :, :, x], member[:, :, :, y], ALU.add))
                    if n:
                        own.done(tt(group[:], group[:], pair[:], ALU.max))
                own.done(nc.vector.memset(g_rank[:], 0.0))
                for x in range(NG):
                    for y in range(x + 1, NG):
                        gx, gy = group[:, :, x:x + 1], group[:, :, y:y + 1]
                        own.done(tt(wins[:], gx, gy, ALU.is_ge))
                        own.done(tt(g_rank[:, :, y:y + 1], g_rank[:, :, y:y + 1], wins[:], ALU.add))
                        own.done(tt(wins[:], gx, gy, ALU.is_lt))
                        own.done(tt(g_rank[:, :, x:x + 1], g_rank[:, :, x:x + 1], wins[:], ALU.add))
                own.done(nc.vector.tensor_scalar(g_rank[:], g_rank[:], float(TOP_G), None, ALU.is_lt))
                for x in range(GE):
                    last = tt(member[:, :, :, x], member[:, :, :, x], g_rank[:], ALU.mult)
                own.done(last)
                own.done(nc.vector.memset(rank[:], 0.0))
                for x in range(NE):
                    one = score[:, :, x:x + 1]
                    if x:
                        last = tt(beaten[:, :, 0:x], one.broadcast_to([P, NT, x]), score[:, :, 0:x], ALU.is_gt)
                    if x < NE - 1:
                        last = tt(beaten[:, :, x + 1:], one.broadcast_to([P, NT, NE - 1 - x]), score[:, :, x + 1:],
                                  ALU.is_ge)
                    own.done(last)
                    if x:
                        last = tt(rank[:, :, 0:x], rank[:, :, 0:x], beaten[:, :, 0:x], ALU.add)
                    if x < NE - 1:
                        last = tt(rank[:, :, x + 1:], rank[:, :, x + 1:], beaten[:, :, x + 1:], ALU.add)
                    own.done(last)
                own.done(nc.vector.tensor_scalar(rank[:], rank[:], float(TOP_K), None, ALU.is_lt))
                own.done(tt(score[:], score[:], rank[:], ALU.mult))
                own.done(nc.vector.tensor_reduce(total[:].rearrange("p i o -> p (i o)"), score[:], AX.X, ALU.add))
                own.done(nc.vector.tensor_scalar(total[:], total[:], 1e-20, None, ALU.add))
                own.done(nc.vector.reciprocal(total[:], total[:]))
                own.done(tt(score[:], score[:], total[:].broadcast_to([P, NT, NE]), ALU.mult))
                nc.vector.memset(combine[:, :, NE:], 1.0)
                own.done(nc.vector.tensor_scalar(combine[:, :, 0:NE], score[:], SCALE, None, ALU.mult))


def experts(nc, sem, nT, Y, combine, a):
    with ExitStack() as ctx:
        def sb(part, shape, dt=F32):
            return ctx.enter_context(nc.sbuf_tensor(f"e_{part}", shape, dt))

        def sig(part):
            return sem(f"e_{part}")

        wg, wu = sb("wg", [P, 2, KD, ME]), sb("wu", [P, 2, KD, ME])
        wd = sb("wd", [P, 2, DM])
        gate = sb("gate", [P, 2, CH])
        inter = sb("inter", [P, 2, CH])
        G = [ctx.enter_context(nc.psum_tensor(f"e_G{b}", [P, CH], F32)) for b in range(2)]
        U = [ctx.enter_context(nc.psum_tensor(f"e_U{b}", [P, CH], F32)) for b in range(2)]
        O = [ctx.enter_context(nc.psum_tensor(f"e_O{b}", [P, TPC, DM], F32)) for b in range(2)]
        gu_ps, gate_ready, inter_ready, out_ps, out_used, own_sem = (
            sig("gu_ps"), sig("gate_ready"), sig("inter_ready"), sig("out_ps"), sig("out_used"), sig("own"))
        loaded = [sig(f"loaded{b}") for b in range(2)]
        for s in (inter_ready,):
            nc.sync.sem_inc(s, FREE)


        def every(eng, step):
            with eng.Fori(0, NX // 2) as x:
                for eb in range(2):
                    with eng.Fori(0, NCH // 2) as j:
                        for b in range(2):
                            step(x * (2 * NCH) + j * 2 + (eb * NCH + b), x * 2 + eb, eb, j * 2 + b, b)

        with nc.Block() as block:
            @block.sync
            def _(sp):
                def load(e, eb):
                    for dst, src in ((wg, "wg"), (wu, "wu"), (wd, "wd")):
                        sp.dma_start(dst[:, eb], a[f"moe_{src}"][:, bass.ds(e, 1)].rearrange(
                            "p o k m -> p (o k) m" if src != "wd" else "p o m -> p (o m)")).then_inc(loaded[eb], 16)

                load(0, 0)
                load(1, 1)
                with sp.Fori(0, NX // 2 - 1) as x:
                    for eb in range(2):
                        e = 2 * x + eb
                        sp.wait_ge(out_ps, (e + 1) * NCH)
                        load(e + 2, eb)

            @block.scalar
            def _(act):
                def step(n, e, eb, c, b):
                    act.wait_ge(gu_ps, n + 1)
                    act.wait_ge(inter_ready, FREE + n)
                    nc.scalar.activation(gate[:, b], G[b][:], ACT.Silu).then_inc(gate_ready, 1)

                every(act, step)

            @block.vector
            def _(dve):
                nc.vector.memset(Y[:], 0.0).then_inc(own_sem, 1)
                dve.wait_ge(own_sem, 1)

                def step(n, e, eb, c, b):
                    dve.wait_ge(gate_ready, n + 1)
                    nc.vector.tensor_tensor(inter[:, b], gate[:, b], U[b][:], ALU.mult).then_inc(inter_ready, 1)
                    dve.wait_ge(out_ps, n + 1)
                    for t in range(TPC):
                        last = nc.vector.scalar_tensor_tensor(Y[:, tok(c, t), :], O[b][:, t, :],
                                                              combine[:, tok(c, t), bass.ds(e, 1)],
                                                              Y[:, tok(c, t), :], ALU.mult, ALU.add)
                    last.then_inc(out_used, 1)
                    dve.wait_ge(out_used, n + 1)

                every(dve, step)

            @block.tensor
            def _(pe):
                def step(n, e, eb, c, b):
                    pe.wait_ge(loaded[eb], (e - eb) * 24 + 48)
                    pe.wait_ge(inter_ready, FREE + n)
                    for ps, w in ((G, wg), (U, wu)):
                        for k in range(KD):
                            last = nc.tensor.matmul(ps[b][:], w[:, eb, k, :], nT[:, k, bass.ds(c * CH, CH)],
                                                    start=(k == 0), stop=(k == KD - 1))
                    last.then_inc(gu_ps, 1)
                    pe.wait_ge(inter_ready, FREE + n + 1)
                    for t in range(TPC):
                        last = nc.tensor.matmul(O[b][:, t, :], inter[:, b, t * P:(t + 1) * P], wd[:, eb, :],
                                                start=True, stop=True)
                    last.then_inc(out_ps, 1)

                every(pe, step)


def experts_out(nc, sem, X, Y, a):
    with ExitStack() as ctx:
        half = ctx.enter_context(nc.sbuf_tensor("f_half", [P, TPC], F32))
        norm = Norm(nc, ctx, sem, "f_norm", LN_EPS)
        const_ready, x_done, own_sem, stored = sem("f_const_ready"), sem("f_x_done"), sem("f_own"), sem("f_stored")
        out_tiles = a["out"][0].rearrange("(j p) d -> p j d", p=P)
        with nc.Block() as block:
            @block.sync
            def _(sp):
                def store(c, b):
                    sp.wait_ge(x_done, c + 1)
                    sp.dma_start(out_tiles[:, bass.ds(c * TPC, TPC), :], X[:, bass.ds(c * TPC, TPC), :]
                                 ).then_inc(stored, 16)

                staged(sp, [(0, store)])
                sp.wait_ge(stored, NCH * 16)

            @block.gpsimd
            def _(pool):
                nc.gpsimd.memset(half[:], -0.5).then_inc(const_ready, 1)
                pool.wait_ge(const_ready, 1)
                staged(pool, [(0, lambda c, b: norm.power(pool, half, c))])

            @block.vector
            def _(dve):
                def step(c, b):
                    own = Order(dve, own_sem, c * (Norm.ORDERS + 1))
                    norm.begin(own, lambda t: Y[:, tok(c, t), :])
                    own.done(norm.scale(dve, c, lambda t: Y[:, tok(c, t), :], lambda t: Y[:, tok(c, t), :]))
                    for t in range(TPC):
                        last = nc.vector.tensor_tensor(X[:, tok(c, t), :], X[:, tok(c, t), :], Y[:, tok(c, t), :],
                                                       ALU.add)
                    last.then_inc(x_done, 1)

                staged(dve, [(0, step)])


def host_arrays(g):
    c = np.ascontiguousarray
    spread = np.zeros((SPLIT * BC, BC, P), np.float32)
    for r in range(BC):
        for s in range(SPLIT):
            spread[s * BC + r, r, :] = 1
    xp = g["L0_attn_x_proj_w"].T

    def rows(w):
        return c(np.moveaxis(w.reshape(-1, P, *w.shape[1:]), 0, 1))

    def every(v):
        return c(np.broadcast_to(v, (P, 1, v.size)))

    def ffn(name, w1, b1, w2, b2):
        return {f"{name}_w1": rows(w1.T), f"{name}_b1": rows(b1), f"{name}_w2": rows(w2.T), f"{name}_b2": c(b2[None])}

    def up(w, shared):
        both = np.concatenate([w, shared.reshape(DM, -1, ME).transpose(1, 0, 2)], 0)
        return c(both.reshape(NX, KD, P, ME).transpose(2, 0, 1, 3))

    return {
        "L0_attn_x": c(g["L0_attn_x"]),
        "in_proj_t": rows(g["L0_attn_in_proj_w"].T),
        "x_proj_t": rows(np.concatenate([xp[:, DTR:]] * SPLIT + [xp[:, :DTR]], 1)),
        "dt_proj_t": c(g["L0_attn_dt_proj_w"].T),
        "out_proj_t": rows(g["L0_attn_out_proj_w"].T),
        "conv_w": rows(g["L0_attn_conv_w"]),
        "conv_b": rows(g["L0_attn_conv_b"]),
        "dt_b": rows(g["L0_attn_dt_proj_b"]),
        "skip_d": rows(g["L0_attn_D"]),
        "a_log": rows(g["L0_attn_A_log"]),
        "x_tiles": c(g["L0_attn_x"].reshape(NCH, CH, DM)),
        **ffn("tail", g["L0_attn_ffn_w1"], g["L0_attn_ffn_b1"], g["L0_attn_ffn_w2"], g["L0_attn_ffn_b2"]),
        "tail_in_w": rows(g["L0_attn_ln1_w"]), "tail_in_b": rows(g["L0_attn_ln1_b"]),
        "tail_mid_w": every(g["L0_attn_ln2_w"]), "tail_mid_b": every(g["L0_attn_ln2_b"]),
        **ffn("bit", g["L0_ffn_W1"], g["L0_ffn_b1"], g["L0_ffn_W2"], g["L0_ffn_b2"]),
        "attn_w": np.concatenate([rows(g[f"L1_attn_W{x}"].T) for x in "qkv"], 2),
        "attn_qk_b": np.stack([rows(g["L1_attn_bq"]), rows(g["L1_attn_bk"])], 1),
        "attn_v_b": c(g["L1_attn_bv"][None]),
        "attn_gamma": every(g["L1_attn_gamma"]), "attn_beta": every(g["L1_attn_beta"]),
        "gate_w": rows(g["L1_ffn_gate_kernel"]), "gate_b": every(g["L1_ffn_gate_bias"]),
        "moe_wg": up(g["L1_ffn_w_gate"], g["L1_ffn_sw_gate"]), "moe_wu": up(g["L1_ffn_w_up"], g["L1_ffn_sw_up"]),
        "moe_wd": c(np.concatenate([g["L1_ffn_w_down"], g["L1_ffn_sw_down"].reshape(-1, ME, DM)], 0).transpose(1, 0, 2)),
        "sel": np.tile(np.eye(VW, dtype=np.float32), (P // VW, 1)),
        "ident": np.eye(P, dtype=np.float32),
        "spread": spread.reshape(SPLIT * BC, BC * P),
    }


def phase(nc, build, *args):
    held = []

    def sem(name):
        held.append(nc.alloc_semaphore(name=name))
        return held[-1]

    build(nc, sem, *args)
    nc.clear_and_free_semaphores(held)
    nc.all_engine_barrier()


def program(nc, a):
    with ExitStack() as ctx:
        parts_dram = nc.dram_tensor("parts", (2, SPLIT, KD, P, T), BF16, kind="Internal").ap()
        z_dram = nc.dram_tensor("z", (H, T, HD), F32, kind="Internal").ap()
        X = ctx.enter_context(nc.sbuf_tensor("X", [P, NT, DM], F32))
        ident = ctx.enter_context(nc.sbuf_tensor("ident", [P, P], F32))
        phase(nc, mamba, X, ident, a)
        phase(nc, feed_forward, X, ident, a, "tail", 2 * DM, True)
        phase(nc, feed_forward, X, ident, a, "bit", 4 * DM, False)
        with nc.sbuf_tensor("V", [P, NT, DM], F32) as V:
            phase(nc, project, X, V, ident, a, parts_dram)
            phase(nc, attend, V, ident, a, parts_dram, z_dram)
        phase(nc, attention_out, X, a, z_dram)
        with nc.sbuf_tensor("combine", [P, NT, NX], F32) as combine, nc.sbuf_tensor("Y", [P, NT, DM], F32) as Y:
            with nc.sbuf_tensor("nT", [P, KD, T], F32) as nT:
                phase(nc, normed_transposed, X, nT, ident, "r")
                phase(nc, route, nT, combine, a)
                phase(nc, experts, nT, Y, combine, a)
            phase(nc, experts_out, X, Y, a)


def kernel(**inputs):
    import concourse.bacc as bacc
    from concourse.bass_utils import run_bass_kernel_spmd

    nc = bacc.Bacc("TRN2", target_bir_lowering=False, num_devices=1)
    arrays = host_arrays({name: np.asarray(value) for name, value in inputs.items()})
    a = {name: nc.dram_tensor(f"in_{name}", v.shape, mybir.dt.from_np(v.dtype), kind="ExternalInput").ap()
         for name, v in arrays.items()}
    a["out"] = nc.dram_tensor("out", (1, T, DM), F32, kind="ExternalOutput").ap()
    program(nc, a)
    ran = run_bass_kernel_spmd(nc, [{f"in_{name}": v for name, v in arrays.items()}], core_ids=[0])
    return ran.results[0]["out"]
```

```python
import numpy as np
from contextlib import ExitStack
import concourse.bass as bass
from concourse import mybir

F32 = mybir.dt.float32
BF16 = mybir.dt.bfloat16
ALU = mybir.AluOpType
ACT = mybir.ActivationFunctionType
AX = mybir.AxisListType

P = 128
T = 4096
DM = 256
NT = T // P
CH = 512
NCH = T // CH
TPC = CH // P
KD = DM // P
DI = 512
ND = DI // P
DS = 16
DTR = 16
DC = 4
SPLIT = 3
BC = 2 * DS
XP = SPLIT * BC + DTR
LN_EPS = 1e-5
MAMBA_EPS = 1e-12
FREE = 1


class Order:

    def __init__(self, eng, sem, base=0):
        self.eng, self.sem, self.base, self.n = eng, sem, base, 0

    def close(self, per_pass):
        assert self.n == per_pass, (self.n, per_pass)

    def done(self, ins):
        ins.then_inc(self.sem, 1)
        self.n += 1
        self.eng.wait_ge(self.sem, self.base + self.n)


def peeled(eng, count, first, second):
    first(0)
    with eng.Fori(0, count - 1) as i:
        first(i + 1)
        second(i)
    second(count - 1)


def tok(c, t):
    return c * TPC + t


def mamba(nc, sem, X, ident, a):
    with ExitStack() as ctx:
        def sb(name, shape, dt=F32):
            return ctx.enter_context(nc.sbuf_tensor(name, shape, dt))

        NH = 3
        w_in = sb("w_in", [P, KD, 2 * DI])
        w_out = sb("w_out", [P, ND, DM])
        w_xp = sb("w_xp", [P, ND, XP])
        w_dt = sb("w_dt", [P, DI])
        conv_w = sb("conv_w", [P, ND, DC])
        conv_b = sb("conv_b", [P, ND])
        dt_b = sb("dt_b", [P, ND])
        skip_d = sb("skip_d", [P, ND])
        a_neg = sb("m_a_neg", [P, ND, DS])
        spread = sb("spread", [SPLIT * BC, BC, P], BF16)
        stats = sb("m_stats", [P, TPC, 6])
        mv = sb("m_mv", [P, TPC, 2])
        var = sb("m_var", [P, TPC])
        spare = sb("m_spare", [P, 1])
        rstd = sb("m_rstd", [P, TPC])
        half = sb("m_half", [P, TPC])
        xn = sb("m_xn", [P, TPC, DM])
        xnT = sb("m_xnT", [P, KD, CH])
        raw = sb("m_raw", [P, ND, CH + DC - 1])
        conv = sb("m_conv", [P, ND, CH])
        u = conv
        xs = sb("m_xs", [P, ND, CH])
        zs = sb("m_zs", [P, ND, CH])
        soft = sb("m_soft", [P, ND, CH])
        yg = soft
        dt = sb("m_dt", [P, ND, CH])
        bc3 = sb("m_bc3", [SPLIT * BC, CH], BF16)
        mid = sb("m_mid", [SPLIT * BC, CH], BF16)
        low = sb("m_low", [SPLIT * BC, CH], BF16)
        rest = sb("m_rest", [SPLIT * BC, CH])
        dtr = sb("m_dtr", [P, CH])
        dA = sb("m_dA", [P, 2, ND, CH])
        spread_f = dA[0:SPLIT * BC].rearrange("p a b t -> p (a b t)")
        dBx = sb("m_dBx", [P, ND, CH])
        h = sb("m_h", [P, NH, ND, CH])
        crep = sb("m_crep", [P, NH, CH])
        h_end = sb("m_h_end", [P, DS, ND])
        bank = [ctx.enter_context(nc.psum_tensor(f"m_bank{b}", [P, CH], F32)) for b in range(8)]
        YB, BB, CB = 0, 4, 6

        w_ready, x_ready = sem("m_w_ready"), sem("m_x_ready")
        const_ready, spread_ready = sem("m_const_ready"), sem("m_spread_ready")
        var_ready, rstd_ready = sem("m_var_ready"), sem("m_rstd_ready")
        xn_ready, xT_ready, xnT_ready = sem("m_xn_ready"), sem("m_xT_ready"), sem("m_xnT_ready")
        proj_ready, raw_ready, conv_ready = sem("m_proj_ready"), sem("m_raw_ready"), sem("m_conv_ready")
        z_ready, xs_ready, xp_ready = sem("m_z_ready"), sem("m_xs_ready"), sem("m_xp_ready")
        bc_ready, dtr_ready, dtp_ready = sem("m_bc_ready"), sem("m_dtr_ready"), sem("m_dtp_ready")
        soft_ready, dt_ready = sem("m_soft_ready"), sem("m_dt_ready")
        b_spread, c_spread, crep_ready = sem("m_b_spread"), sem("m_c_spread"), sem("m_crep_ready")
        dA_ready, b_used = sem("m_dA_ready"), sem("m_b_used")
        h_ready, h_kept, g_ready, g_summed = sem("m_h_ready"), sem("m_h_kept"), sem("m_g_ready"), sem("m_g_summed")
        yg_ready, out_ready = sem("m_yg_ready"), sem("m_out_ready")
        v_own, s_own = sem("m_v_own"), sem("m_s_own")
        NW = 10
        V_OWN, S_OWN = 12, 4

        with nc.Block() as block:
            @block.sync
            def _(sp):
                for q in range(4):
                    sp.dma_start(X[:, q * 8:(q + 1) * 8, :],
                                 a["L0_attn_x"][0, q * 8 * P:(q + 1) * 8 * P, :].rearrange("(j p) d -> p j d", p=P)
                                 ).then_inc(x_ready, 16)
                    if q == 0:
                        sp.dma_start(ident[:], a["ident"]).then_inc(w_ready, 16)
                        sp.dma_start(w_in[:], a["in_proj_t"]).then_inc(w_ready, 16)
                sp.dma_start(w_xp[:], a["x_proj_t"]).then_inc(w_ready, 16)
                sp.dma_start(w_dt[SPLIT * BC:XP, :], a["dt_proj_t"]).then_inc(w_ready, 16)
                sp.dma_start(w_out[:], a["out_proj_t"]).then_inc(w_ready, 16)
                sp.dma_start(spread_f, a["spread"]).then_inc(w_ready, 16)

            @block.gpsimd
            def _(pool):
                nc.gpsimd.memset(half[:], -0.5).then_inc(const_ready, 1)
                nc.gpsimd.memset(h_end[:], 0.0).then_inc(const_ready, 1)
                nc.gpsimd.memset(raw[:, :, CH:], 0.0).then_inc(const_ready, 1)
                pool.wait_ge(const_ready, 3)
                with pool.Fori(0, NCH) as i:
                    pool.wait_ge(var_ready, i + 1)
                    nc.gpsimd.tensor_tensor(rstd[:], var[:], half[:], ALU.pow).then_inc(rstd_ready, 1)
                    for n in range(DS):
                        pool.wait_ge(crep_ready, i * DS + n + 1)
                        pool.wait_ge(h_kept, i * DS + n + 1)
                        nc.gpsimd.tensor_tensor(h[:, n % NH], h[:, n % NH],
                                                crep[:, n % NH:n % NH + 1, :].broadcast_to([P, ND, CH]),
                                                ALU.mult).then_inc(g_ready, 1)

            @block.scalar
            def _(act):
                act.dma_start(conv_w[:], a["conv_w"]).then_inc(w_ready, 16)
                act.dma_start(conv_b[:], a["conv_b"]).then_inc(w_ready, 16)
                act.dma_start(dt_b[:], a["dt_b"]).then_inc(w_ready, 16)
                act.dma_start(skip_d[:], a["skip_d"]).then_inc(w_ready, 16)
                act.dma_start(a_neg[:], a["a_log"]).then_inc(w_ready, 16)
                act.wait_ge(w_ready, 16 * (NW + 1))
                act.wait_ge(spread_ready, 1)
                setup = Order(act, s_own)
                setup.done(nc.scalar.activation(a_neg[:], a_neg[:], ACT.Exp))
                setup.done(nc.scalar.mul(a_neg[:], a_neg[:], -1.0))
                act.wait_ge(const_ready, 3)
                with act.Fori(0, NCH) as i:
                    own = Order(act, s_own, i * S_OWN + 2)
                    act.wait_ge(xT_ready, i + 1)
                    for k in range(KD):
                        last = nc.scalar.copy(xnT[:, k, :], bank[BB + k][:])
                    last.then_inc(xnT_ready, 1)
                    own.done(nc.scalar.copy(raw[:, :, 0:DC - 1], raw[:, :, CH:]))
                    for m in range(ND):
                        act.wait_ge(proj_ready, i * 2 * ND + m + 1)
                        nc.scalar.copy(raw[:, m, DC - 1:], bank[YB + m][:]).then_inc(raw_ready, 1)
                    for m in range(ND):
                        act.wait_ge(proj_ready, i * 2 * ND + ND + m + 1)
                        nc.scalar.activation(zs[:, m, :], bank[BB + m][:], ACT.Silu).then_inc(z_ready, 1)
                    for m in range(ND):
                        act.wait_ge(conv_ready, i * ND + m + 1)
                        nc.scalar.activation(xs[:, m, :], conv[:, m, :], ACT.Silu,
                                             bias=conv_b[:, m:m + 1]).then_inc(xs_ready, 1)
                    act.wait_ge(xp_ready, i + 1)
                    nc.scalar.copy(dtr[SPLIT * BC:XP, :], bank[CB][SPLIT * BC:XP, :]).then_inc(dtr_ready, 1)
                    for m in range(ND):
                        act.wait_ge(dtp_ready, i * ND + m + 1)
                        last = nc.scalar.activation(dt[:, m, :], bank[YB + m][:], ACT.Identity, bias=dt_b[:, m:m + 1])
                    own.done(last)
                    own.done(nc.scalar.activation(soft[:], dt[:], ACT.Abs))
                    own.done(nc.scalar.activation(soft[:], soft[:], ACT.Exp, scale=-1.0))
                    nc.scalar.activation(soft[:], soft[:], ACT.Ln, bias=1.0).then_inc(soft_ready, 1)
                    act.wait_ge(dt_ready, i + 1)

                    def keep_end(n):
                        act.wait_ge(h_ready, i * DS + n + 1)
                        nc.scalar.copy(h_end[:, n, :], h[:, n % NH, :, CH - 1]).then_inc(h_kept, 1)

                    for n in range(DS):
                        for m in range(ND):
                            last = nc.scalar.activation(dA[:, n % 2, m, :], dt[:, m, :], ACT.Exp,
                                                        scale=a_neg[:, m, n:n + 1])
                        last.then_inc(dA_ready, 1)
                        act.wait_ge(c_spread, i * DS + n + 1)
                        if n >= NH:
                            act.wait_ge(g_ready, i * DS + n - NH + 1)
                        nc.scalar.copy(crep[:, n % NH, :], bank[CB + n % 2][:]).then_inc(crep_ready, 1)
                        if n >= 1:
                            keep_end(n - 1)
                    keep_end(DS - 1)
                    own.close(S_OWN)

            @block.vector
            def _(dve):
                dve.wait_ge(w_ready, 16 * (NW + 1))
                nc.vector.tensor_copy(spread[:].rearrange("p r c -> p (r c)"), spread_f).then_inc(spread_ready, 1)
                dve.wait_ge(x_ready, 16 * 4)
                with dve.Fori(0, NCH) as i:
                    own = Order(dve, v_own, i * V_OWN)
                    for t in range(TPC):
                        last = nc.vector.bn_stats(stats[:, t, :], X[:, tok(i, t), :])
                    own.done(last)
                    nc.vector.memset(spare[:], 0.0)
                    for t in range(TPC):
                        last = nc.vector.bn_aggr(mv[:, t, :], stats[:, t, :])
                    own.done(last)
                    nc.vector.tensor_scalar(var[:], mv[:, :, 1], LN_EPS, None, ALU.add).then_inc(var_ready, 1)
                    dve.wait_ge(rstd_ready, i + 1)
                    for t in range(TPC):
                        last = nc.vector.tensor_scalar(xn[:, t, :], X[:, tok(i, t), :], mv[:, t, 0:1], rstd[:, t:t + 1],
                                                       ALU.subtract, ALU.mult)
                    last.then_inc(xn_ready, 1)
                    for k in range(DC):
                        for m in range(ND):
                            if k == 0:
                                dve.wait_ge(raw_ready, i * ND + m + 1)
                                last = nc.vector.tensor_scalar(conv[:, m, :], raw[:, m, 0:CH], conv_w[:, m, 0:1],
                                                               None, ALU.mult)
                            else:
                                last = nc.vector.scalar_tensor_tensor(conv[:, m, :], raw[:, m, k:k + CH],
                                                                      conv_w[:, m, k:k + 1], conv[:, m, :],
                                                                      ALU.mult, ALU.add)
                                if k == DC - 1:
                                    last.then_inc(conv_ready, 1)
                        if k < DC - 1:
                            own.done(last)
                    dve.wait_ge(xp_ready, i + 1)
                    dve.wait_ge(dtr_ready, i + 1)
                    own.done(nc.vector.tensor_copy(bc3[:], bank[CB][0:SPLIT * BC, :]))
                    own.done(nc.vector.tensor_tensor(rest[:], bank[CB][0:SPLIT * BC, :], bc3[:], ALU.subtract))
                    own.done(nc.vector.tensor_copy(mid[:], rest[:]))
                    nc.vector.tensor_copy(bc3[BC:2 * BC, :], mid[BC:2 * BC, :])
                    own.done(nc.vector.tensor_tensor(low[:], rest[:], mid[:], ALU.subtract))
                    nc.vector.tensor_copy(bc3[2 * BC:, :], low[2 * BC:, :]).then_inc(bc_ready, 1)
                    dve.wait_ge(soft_ready, i + 1)
                    nc.vector.scalar_tensor_tensor(dt[:], dt[:], 0.0, soft[:], ALU.max, ALU.add).then_inc(dt_ready, 1)
                    dve.wait_ge(dt_ready, i + 1)
                    dve.wait_ge(xs_ready, i * ND + ND)
                    own.done(nc.vector.tensor_tensor(u[:], dt[:], xs[:], ALU.mult))
                    for n in range(DS):
                        dve.wait_ge(b_spread, i * DS + n + 1)
                        if n >= 1:
                            dve.wait_ge(h_ready, i * DS + n)
                        nc.vector.tensor_tensor(dBx[:], u[:],
                                                bank[BB + n % 2][:].rearrange("p (o t) -> p o t", o=1)
                                                .broadcast_to([P, ND, CH]), ALU.mult).then_inc(b_used, 1)
                        dve.wait_ge(b_used, i * DS + n + 1)
                        dve.wait_ge(dA_ready, i * DS + n + 1)
                        if n >= NH:
                            dve.wait_ge(g_summed, i * DS + n - NH + 1)
                        for m in range(ND):
                            last = nc.vector.tensor_tensor_scan(h[:, n % NH, m, :], dA[:, n % 2, m, :], dBx[:, m, :],
                                                                h_end[:, n, m:m + 1], ALU.mult, ALU.add)
                        last.then_inc(h_ready, 1)
                    dve.wait_ge(g_summed, i * DS + DS)
                    for m in range(ND):
                        last = nc.vector.scalar_tensor_tensor(yg[:, m, :], xs[:, m, :], skip_d[:, m:m + 1],
                                                              bank[YB + m][:], ALU.mult, ALU.add)
                    own.done(last)
                    dve.wait_ge(z_ready, i * ND + ND)
                    nc.vector.tensor_tensor(yg[:], yg[:], zs[:], ALU.mult).then_inc(yg_ready, 1)
                    for t in range(TPC):
                        dve.wait_ge(out_ready, i * TPC + t + 1)
                        last = nc.vector.tensor_tensor(X[:, tok(i, t), :], bank[BB + t][:, 0:DM], xn[:, t, :], ALU.add)
                    own.done(last)
                    own.close(V_OWN)

            @block.tensor
            def _(pe):
                pe.wait_ge(w_ready, 16 * (NW + 1))
                pe.wait_ge(spread_ready, 1)
                with pe.Fori(0, NCH) as i:
                    pe.wait_ge(xn_ready, i + 1)
                    for t in range(TPC):
                        for k in range(KD):
                            last = nc.tensor.transpose(bank[BB + k][:, t * P:(t + 1) * P],
                                                       xn[:, t, k * P:(k + 1) * P], ident[:])
                    last.then_inc(xT_ready, 1)
                    pe.wait_ge(xnT_ready, i + 1)
                    for m in range(2 * ND):
                        for k in range(KD):
                            last = nc.tensor.matmul(bank[m][:], w_in[:, k, m * P:(m + 1) * P], xnT[:, k, :],
                                                    start=(k == 0), stop=(k == KD - 1))
                        last.then_inc(proj_ready, 1)
                    pe.wait_ge(z_ready, i * ND + ND)
                    for m in range(ND):
                        pe.wait_ge(xs_ready, i * ND + m + 1)
                        last = nc.tensor.matmul(bank[CB][0:XP, :], w_xp[:, m, :], xs[:, m, :],
                                                start=(m == 0), stop=(m == ND - 1))
                    last.then_inc(xp_ready, 1)
                    pe.wait_ge(dtr_ready, i + 1)
                    for m in range(ND):
                        nc.tensor.matmul(bank[YB + m][:], w_dt[SPLIT * BC:XP, m * P:(m + 1) * P],
                                         dtr[SPLIT * BC:XP, :], start=True, stop=True).then_inc(dtp_ready, 1)
                    pe.wait_ge(bc_ready, i + 1)

                    def spread_bc(n):
                        if n >= 2:
                            pe.wait_ge(b_used, i * DS + n - 1)
                        nc.tensor.matmul(bank[BB + n % 2][:], spread[:, n, :], bc3[:],
                                         start=True, stop=True).then_inc(b_spread, 1)
                        if n >= 2:
                            pe.wait_ge(crep_ready, i * DS + n - 1)
                        nc.tensor.matmul(bank[CB + n % 2][:], spread[:, DS + n, :], bc3[:],
                                         start=True, stop=True).then_inc(c_spread, 1)

                    spread_bc(0)
                    spread_bc(1)
                    for n in range(DS):
                        if n + 2 < DS:
                            spread_bc(n + 2)
                        pe.wait_ge(g_ready, i * DS + n + 1)
                        for m in range(ND):
                            last = nc.tensor.matmul(bank[YB + m][:], ident[:], h[:, n % NH, m, :],
                                                    start=(n == 0), stop=(n == DS - 1))
                        last.then_inc(g_summed, 1)
                    pe.wait_ge(yg_ready, i + 1)
                    for t in range(TPC):
                        for m in range(ND):
                            last = nc.tensor.matmul(bank[BB + t][:, 0:DM], yg[:, m, t * P:(t + 1) * P], w_out[:, m, :],
                                                    start=(m == 0), stop=(m == ND - 1))
                        last.then_inc(out_ready, 1)


def staged(eng, stages):
    ahead = max(lead for lead, _ in stages)

    def step(s, at):
        for lead, run in stages:
            if not isinstance(s, int) or 0 <= s + lead < NCH:
                run(s + lead, (at + lead) % 2)

    for s in range(-ahead, 2):
        step(s, s)
    passes = (NCH - ahead - 2) // 2
    with eng.Fori(1, 1 + passes) as j:
        step(2 * j, 0)
        step(2 * j + 1, 1)
    for s in range(2 + 2 * passes, NCH):
        step(s, s)


def before(c, lag):
    return not isinstance(c, int) or c >= lag


class Norm:

    ORDERS = 2

    def __init__(self, nc, ctx, sem, name, eps):
        def sb(part, shape):
            return ctx.enter_context(nc.sbuf_tensor(f"{name}_{part}", shape, F32))

        self.nc, self.eps = nc, eps
        self.stats, self.mv = sb("stats", [P, TPC, 6]), sb("mv", [P, TPC, 2])
        self.var, self.rstd, self.spare = sb("var", [P, TPC]), sb("rstd", [P, TPC]), sb("spare", [P, 1])
        self.var_ready, self.rstd_ready = sem(f"{name}_var_ready"), sem(f"{name}_rstd_ready")

    def begin(self, own, src):
        for t in range(TPC):
            last = self.nc.vector.bn_stats(self.stats[:, t, :], src(t))
        own.done(last)
        self.nc.vector.memset(self.spare[:], 0.0)
        for t in range(TPC):
            last = self.nc.vector.bn_aggr(self.mv[:, t, :], self.stats[:, t, :])
        own.done(last)
        self.nc.vector.tensor_scalar(self.var[:], self.mv[:, :, 1], self.eps, None, ALU.add).then_inc(self.var_ready, 1)

    def power(self, pool, half, c):
        pool.wait_ge(self.var_ready, c + 1)
        self.nc.gpsimd.tensor_tensor(self.rstd[:], self.var[:], half[:], ALU.pow).then_inc(self.rstd_ready, 1)

    def scale(self, dve, c, out, src):
        dve.wait_ge(self.rstd_ready, c + 1)
        for t in range(TPC):
            last = self.nc.vector.tensor_scalar(out(t), src(t), self.mv[:, t, 0:1], self.rstd[:, t:t + 1],
                                                ALU.subtract, ALU.mult)
        return last


def feed_forward(nc, sem, X, ident, a, name, hidden, tail):
    NM = hidden // P
    with ExitStack() as ctx:
        def sb(part, shape, dt=F32):
            return ctx.enter_context(nc.sbuf_tensor(f"{name}_{part}", shape, dt))

        def sig(part):
            return sem(f"{name}_{part}")

        w1 = sb("w1", [P, KD, hidden])
        w2 = sb("w2", [P, NM, DM])
        b1 = sb("b1", [P, NM])
        b2 = sb("b2", [1, DM])
        ones = sb("ones", [P, P])
        half = sb("half", [P, TPC])
        n = sb("n", [P, 2, TPC, DM])
        hT = sb("hT", [P, 2, KD, CH])
        fT = sb("fT", [P, 2, NM, CH])
        f = sb("f", [P, 2, TPC, DM])
        norm_in = Norm(nc, ctx, sem, f"{name}_in", MAMBA_EPS if tail else LN_EPS)
        norm_out = Norm(nc, ctx, sem, f"{name}_out", LN_EPS)
        if tail:
            norm_mid = Norm(nc, ctx, sem, f"{name}_mid", MAMBA_EPS)
            in_w, in_b = sb("in_w", [P, KD]), sb("in_b", [P, KD])
            mid_w, mid_b = sb("mid_w", [P, 1, DM]), sb("mid_b", [P, 1, DM])
            x = sb("x", [P, TPC, DM])
        else:
            gamma = sb("gamma", [P, 2])
            bound = sb("bound", [P, 2, 2])
            below = sb("below", [P, KD * hidden])
        bank = [ctx.enter_context(nc.psum_tensor(f"{name}_bank{b}", [P, CH], F32)) for b in range(8)]
        TB, FB, OB = 0, 2, 6

        w_ready, const_ready, q_ready = sig("w_ready"), sig("const_ready"), sig("q_ready")
        n_ready, nT_ready, hT_ready = sig("n_ready"), sig("nT_ready"), sig("hT_ready")
        up_ready, up_read, down_ready, f_ready = sig("up_ready"), sig("up_read"), sig("down_ready"), sig("f_ready")
        f_used, x_ready = sig("f_used"), sig("x_ready")
        mid_ready, mid_affine, mid_own = sig("mid_ready"), sig("mid_affine"), sig("mid_own")
        first_own, second_own, setup_own = sig("first_own"), sig("second_own"), sig("setup_own")
        abs_ready, sum_ready = sig("abs_ready"), sig("sum_ready")
        loads = [(w1, "w1"), (w2, "w2"), (b1, "b1"), (b2, "b2")]
        if tail:
            loads += [(in_w, "in_w"), (in_b, "in_b"), (mid_w, "mid_w"), (mid_b, "mid_b")]
        N_LOADS = 16 * len(loads)
        leaked = sig("leaked") if tail else None
        fT_ready = leaked if tail else up_read
        FIRST, SECOND = Norm.ORDERS, (2 if tail else 1) * Norm.ORDERS + 1

        with nc.Block() as block:
            @block.sync
            def _(sp):
                for dst, src in loads:
                    sp.dma_start(dst[:], a[f"{name}_{src}"]).then_inc(w_ready, 16)
                if tail:
                    with sp.Fori(0, NCH) as c:
                        sp.wait_ge(f_used, c + 1)
                        sp.dma_start(x[:], a["x_tiles"][bass.ds(c, 1)].rearrange("o (t p) d -> p (o t) d", p=P)
                                     ).then_inc(x_ready, 16)

            @block.gpsimd
            def _(pool):
                nc.gpsimd.memset(half[:], -0.5).then_inc(const_ready, 1)
                nc.gpsimd.memset(ones[:], 1.0).then_inc(const_ready, 1)
                pool.wait_ge(const_ready, 2)
                pool.wait_ge(w_ready, N_LOADS)

                def first(c, b):
                    norm_in.power(pool, half, c)

                def second(c, b):
                    if tail:
                        norm_mid.power(pool, half, c)
                        pool.wait_ge(mid_ready, c + 1)
                        nc.gpsimd.tensor_tensor(f[:, b], f[:, b], mid_w[:].broadcast_to([P, TPC, DM]),
                                                ALU.mult).then_inc(mid_own, 1)
                        pool.wait_ge(mid_own, c + 1)
                        nc.gpsimd.tensor_tensor(f[:, b], f[:, b], mid_b[:].broadcast_to([P, TPC, DM]),
                                                ALU.add).then_inc(mid_affine, 1)
                    norm_out.power(pool, half, c)

                staged(pool, [(2, first), (0, second)])

            @block.scalar
            def _(act):
                act.wait_ge(w_ready, N_LOADS)
                if not tail:
                    nc.scalar.activation(below[:], w1[:].rearrange("p k e -> p (k e)"), ACT.Abs,
                                         accum_out=gamma[:, 0:1]).then_inc(abs_ready, 1)
                    act.wait_ge(abs_ready, 1)
                    nc.scalar.activation(below[:], w2[:].rearrange("p k e -> p (k e)"), ACT.Abs,
                                         accum_out=gamma[:, 1:2]).then_inc(abs_ready, 1)

                def transposed(c, b):
                    act.wait_ge(nT_ready, c + 1)
                    for k in range(KD):
                        if tail:
                            last = nc.scalar.activation(hT[:, b, k, :], bank[TB + k][:], ACT.Identity,
                                                        bias=in_b[:, k:k + 1], scale=in_w[:, k:k + 1])
                        else:
                            last = nc.scalar.copy(hT[:, b, k, :], bank[TB + k][:])
                    last.then_inc(hT_ready, 1)

                def up(c, b):
                    for m in range(NM):
                        act.wait_ge(up_ready, c * NM + m + 1)
                        if tail:
                            last = nc.scalar.activation(fT[:, b, m, :], bank[FB + m % 4][:], ACT.Identity,
                                                        bias=b1[:, m:m + 1])
                        else:
                            last = nc.scalar.activation(fT[:, b, m, :], bank[FB + m % 4][:], ACT.Relu,
                                                        bias=b1[:, m:m + 1])
                        last.then_inc(up_read, 1)

                def down(c, b):
                    act.wait_ge(f_used, c)
                    for t in range(TPC):
                        act.wait_ge(down_ready, c * TPC + t + 1)
                        nc.scalar.copy(f[:, b, t, :], bank[OB + t % 2][:, 0:DM]).then_inc(f_ready, 1)

                staged(act, [(1, transposed), (0, down), (1, up)])

            @block.vector
            def _(dve):
                nc.vector.memset(norm_out.stats[:], 0.0).then_inc(f_used, 1)
                dve.wait_ge(w_ready, N_LOADS)
                if not tail:
                    setup = Order(dve, setup_own)
                    dve.wait_ge(sum_ready, 1)
                    setup.done(nc.vector.tensor_scalar(bound[:, 0, :], bank[TB][:, 0:2], 0.5 / (hidden * DM),
                                                       0.5 * LN_EPS, ALU.mult, ALU.add))
                    setup.done(nc.vector.tensor_scalar(bound[:, 1, :], bound[:, 0, :], -1.0, None, ALU.mult))
                    for q, w in enumerate((w1, w2)):
                        flat = w[:].rearrange("p k e -> p (k e)")
                        setup.done(nc.vector.tensor_scalar(below[:], flat, bound[:, 1, q:q + 1], None, ALU.is_lt))
                        last = nc.vector.scalar_tensor_tensor(flat, flat, bound[:, 0, q:q + 1], below[:],
                                                              ALU.is_gt, ALU.subtract)
                        setup.done(last)
                    nc.vector.tensor_scalar(bound[:, 1, :], bound[:, 0, :], -1.0, None, ALU.mult).then_inc(q_ready, 1)

                def first(c, b):
                    own = Order(dve, first_own, c * FIRST)
                    norm_in.begin(own, lambda t: X[:, tok(c, t), :])
                    if before(c, 2):
                        dve.wait_ge(nT_ready, c - 1)
                    norm_in.scale(dve, c, lambda t: n[:, b, t, :], lambda t: X[:, tok(c, t), :]).then_inc(n_ready, 1)
                    own.close(FIRST)

                def second(c, b):
                    own = Order(dve, second_own, c * SECOND)
                    dve.wait_ge(f_ready, c * TPC + TPC)
                    part = lambda t: f[:, b, t, :]
                    if tail:
                        norm_mid.begin(own, part)
                        norm_mid.scale(dve, c, part, part).then_inc(mid_ready, 1)
                        dve.wait_ge(mid_affine, c + 1)
                    norm_out.begin(own, part)
                    own.done(norm_out.scale(dve, c, part, part))
                    if tail:
                        dve.wait_ge(x_ready, 16 * c + 16)
                    for t in range(TPC):
                        last = nc.vector.tensor_tensor(X[:, tok(c, t), :], x[:, t, :] if tail else X[:, tok(c, t), :],
                                                       part(t), ALU.add)
                    last.then_inc(f_used, 1)
                    own.close(SECOND)

                def leak(c, b):
                    for m in range(NM):
                        dve.wait_ge(up_read, c * NM + m + 1)
                        nc.vector.scalar_tensor_tensor(fT[:, b, m, :], fT[:, b, m, :], 0.01, fT[:, b, m, :],
                                                       ALU.mult, ALU.max).then_inc(leaked, 1)

                staged(dve, [(2, first), (0, second)] + ([(1, leak)] if tail else []))

            @block.tensor
            def _(pe):
                pe.wait_ge(w_ready, N_LOADS)
                pe.wait_ge(const_ready, 2)
                if not tail:
                    pe.wait_ge(abs_ready, 2)
                    nc.tensor.matmul(bank[TB][:, 0:2], ones[:], gamma[:], start=True, stop=True).then_inc(sum_ready, 1)
                    pe.wait_ge(q_ready, 1)

                def transposes(c, b):
                    pe.wait_ge(n_ready, c + 1)
                    pe.wait_ge(hT_ready, c)
                    for t in range(TPC):
                        for k in range(KD):
                            last = nc.tensor.transpose(bank[TB + k][:, t * P:(t + 1) * P], n[:, b, t, k * P:(k + 1) * P],
                                                       ident[:])
                    last.then_inc(nT_ready, 1)

                def up(c, b):
                    pe.wait_ge(hT_ready, c + 1)
                    for m in range(NM):
                        pe.wait_ge(up_read, c * NM + max(0, m - 3))
                        for k in range(KD):
                            last = nc.tensor.matmul(bank[FB + m % 4][:], w1[:, k, m * P:(m + 1) * P], hT[:, b, k, :],
                                                    start=(k == 0), stop=(k == KD - 1))
                        last.then_inc(up_ready, 1)

                def down(c, b):
                    pe.wait_ge(fT_ready, c * NM + NM)
                    for t in range(TPC):
                        pe.wait_ge(f_ready, c * TPC + max(0, t - 1))
                        out = bank[OB + t % 2]
                        for m in range(NM):
                            nc.tensor.matmul(out[:, 0:DM], fT[:, b, m, t * P:(t + 1) * P], w2[:, m, :],
                                             start=(m == 0), stop=False)
                        if tail:
                            for k in range(KD):
                                nc.tensor.matmul(out[:, k * P:(k + 1) * P], hT[:, b, k, t * P:(t + 1) * P], ident[:],
                                                 start=False, stop=False)
                        nc.tensor.matmul(out[:, 0:DM], ones[0:1, :], b2[:], start=False,
                                         stop=True).then_inc(down_ready, 1)

                staged(pe, [(1, transposes), (0, down), (1, up)])


H = 16
HD = DM // H
SLOTS = ((0, 0), (0, 1), (1, 0), (1, 1), (0, 2), (2, 0))
QK_ROWS = len(SLOTS) * HD
ROWS = QK_ROWS + SPLIT
QS = 1.0 / 64
KC = CH
NKC = T // KC
RING = 12
NS = 4
NB = 2

TAIL = 4
QUAD = TPC
VW = 32


def project(nc, sem, X, V, ident, a, parts_dram):
    with ExitStack() as ctx:
        def sb(part, shape, dt=F32):
            return ctx.enter_context(nc.sbuf_tensor(f"p_{part}", shape, dt))

        def sig(part):
            return sem(f"p_{part}")

        w = sb("w", [P, KD, 3 * DM])
        qk_b = sb("qk_b", [P, 2, KD])
        v_b = sb("v_b", [1, DM])
        ones, half = sb("ones", [1, P]), sb("half", [P, TPC])
        n = sb("n", [P, 2, TPC, DM])
        nT = sb("nT", [P, 2, KD, CH])
        full = sb("full", [P, 2, 2, KD, CH])
        parts = sb("parts", [P, 2, 2, SPLIT, KD, CH], BF16)
        norm = Norm(nc, ctx, sem, "p_norm", LN_EPS)
        bank = [ctx.enter_context(nc.psum_tensor(f"p_bank{b}", [P, CH], F32)) for b in range(8)]
        TB, QB, VB = 0, 2, 6

        w_ready, const_ready, bias_ready = sig("w_ready"), sig("const_ready"), sig("bias_ready")
        n_ready, nT_ps, nT_ready = sig("n_ready"), sig("nT_ps"), sig("nT_ready")
        qk_ps, full_ready, v_ps, v_ready = sig("qk_ps"), sig("full_ready"), sig("v_ps"), sig("v_ready")
        split_ready, norm_own, split_own = sig("split_ready"), sig("norm_own"), sig("split_own")
        stored = [sig(f"stored{b}") for b in range(2)]
        loads = [(w, "w"), (qk_b, "qk_b"), (v_b, "v_b")]
        N_LOADS = 16 * len(loads)
        STORES = 16 * 2 * SPLIT
        SPLITS = 3

        with nc.Block() as block:
            @block.sync
            def _(sp):
                for dst, src in loads:
                    sp.dma_start(dst[:], a[f"attn_{src}"]).then_inc(w_ready, 16)

                def store(c, b):
                    for x in range(2):
                        sp.wait_ge(split_ready, 2 * c + x + 1)
                        for s in range(SPLIT):
                            sp.dma_start(parts_dram[x, s, :, :, bass.ds(c * CH, CH)].rearrange("m p t -> p m t"),
                                         parts[:, b, x, s]).then_inc(stored[b], 16)

                staged(sp, [(0, store), (1, lambda c, b: None)])
                for b in range(2):
                    sp.wait_ge(stored[b], NCH // 2 * STORES)

            @block.gpsimd
            def _(pool):
                nc.gpsimd.memset(half[:], -0.5).then_inc(const_ready, 1)
                nc.gpsimd.memset(ones[:], 1.0).then_inc(const_ready, 1)
                pool.wait_ge(const_ready, 2)
                staged(pool, [(2, lambda c, b: norm.power(pool, half, c))])

            @block.scalar
            def _(act):
                act.wait_ge(w_ready, N_LOADS)
                nc.scalar.mul(qk_b[:, 0, :], qk_b[:, 0, :], QS).then_inc(bias_ready, 1)
                act.wait_ge(bias_ready, 1)

                def transposed(c, b):
                    act.wait_ge(nT_ps, c + 1)
                    for k in range(KD):
                        last = nc.scalar.copy(nT[:, b, k, :], bank[TB + k][:])
                    last.then_inc(nT_ready, 1)

                def projected(c, b):
                    if before(c, 2):
                        act.wait_ge(split_ready, 2 * c - 2)
                    for x in range(2):
                        for m in range(KD):
                            act.wait_ge(qk_ps, c * 2 * KD + x * KD + m + 1)
                            nc.scalar.activation(full[:, b, x, m, :], bank[QB + x * KD + m][:], ACT.Identity,
                                                 bias=qk_b[:, x, m:m + 1],
                                                 scale=QS if x == 0 else 1.0).then_inc(full_ready, 1)
                    for t in range(TPC):
                        act.wait_ge(v_ps, c * TPC + t + 1)
                        nc.scalar.copy(V[:, tok(c, t), :], bank[VB + t % 2][:, 0:DM]).then_inc(v_ready, 1)

                staged(act, [(1, transposed), (0, projected)])

            @block.vector
            def _(dve):
                def normed(c, b):
                    own = Order(dve, norm_own, c * Norm.ORDERS)
                    norm.begin(own, lambda t: X[:, tok(c, t), :])
                    if before(c, 2):
                        dve.wait_ge(nT_ps, c - 1)
                    norm.scale(dve, c, lambda t: n[:, b, t, :], lambda t: X[:, tok(c, t), :]).then_inc(n_ready, 1)

                def split(c, b):
                    own = Order(dve, split_own, c * 2 * SPLITS)
                    if before(c, 2):
                        dve.wait_ge(stored[b], (c - b) * (STORES // 2))
                    for x in range(2):
                        f = full[:, b, x]
                        dve.wait_ge(full_ready, c * 2 * KD + x * KD + KD)
                        own.done(nc.vector.tensor_copy(parts[:, b, x, 0], f))
                        own.done(nc.vector.tensor_tensor(f, f, parts[:, b, x, 0], ALU.subtract))
                        own.done(nc.vector.tensor_copy(parts[:, b, x, 1], f))
                        nc.vector.tensor_tensor(parts[:, b, x, 2], f, parts[:, b, x, 1],
                                                ALU.subtract).then_inc(split_ready, 1)
                    own.close(2 * SPLITS)

                staged(dve, [(2, normed), (0, split)])

            @block.tensor
            def _(pe):
                pe.wait_ge(w_ready, N_LOADS)
                pe.wait_ge(const_ready, 2)

                def transposes(c, b):
                    pe.wait_ge(n_ready, c + 1)
                    pe.wait_ge(nT_ready, c)
                    for t in range(TPC):
                        for k in range(KD):
                            last = nc.tensor.transpose(bank[TB + k][:, t * P:(t + 1) * P], n[:, b, t, k * P:(k + 1) * P],
                                                       ident[:])
                    last.then_inc(nT_ps, 1)

                def projections(c, b):
                    pe.wait_ge(nT_ready, c + 1)
                    for x in range(2):
                        pe.wait_ge(full_ready, c * 2 * KD)
                        for m in range(KD):
                            for k in range(KD):
                                last = nc.tensor.matmul(bank[QB + x * KD + m][:],
                                                        w[:, k, x * DM + m * P:x * DM + (m + 1) * P], nT[:, b, k, :],
                                                        start=(k == 0), stop=(k == KD - 1))
                            last.then_inc(qk_ps, 1)
                    for t in range(TPC):
                        pe.wait_ge(v_ready, c * TPC + max(0, t - 1))
                        out = bank[VB + t % 2][:, 0:DM]
                        for k in range(KD):
                            nc.tensor.matmul(out, nT[:, b, k, t * P:(t + 1) * P], w[:, k, 2 * DM:3 * DM],
                                             start=(k == 0), stop=False)
                        nc.tensor.matmul(out, ones[:], v_b[:], start=False, stop=True).then_inc(v_ps, 1)

                staged(pe, [(1, transposes), (0, projections)])


def group_blocks(g):
    return [(kb, None) for kb in range(TPC * (g + 1), NT)] + [(TPC * g + r, r) for r in range(TPC)]


BLOCKS = [(g, kb, r) for g in range(NCH) for kb, r in group_blocks(g)]
UNITS = [(i, c) for i in range(NT) for c in range(NKC)]


def low_width(i, c):
    return max(0, min(KC, P * (i + 1) - KC * c))


def lows_upto(u):
    return sum(low_width(*UNITS[n]) > 0 for n in range(u + 1)) if u >= 0 else u + 1


def head_order():
    G0, G1 = [(0, g) for g in range(NCH)], [(1, g) for g in range(NCH)]
    rows = G1[-1:] + G0[:-1]
    turns = G1[-TAIL:] + G0[:-TAIL]
    blocks = [(p, j) for p, g in turns for j, b in enumerate(BLOCKS) if b[0] == g]
    quads = [(p, j // QUAD) for p, j in blocks[::QUAD]]
    units = [(0, u) for u in range(len(UNITS))]
    items = {"unit": units, "max": units, "low": [u for u in units if low_width(*UNITS[u[1]])],
             "negate": G0, "weight": G0, "row": rows, "rowcopy": rows, "block": blocks, "exp": blocks,
             "value": quads, "zcopy": turns, "turn": turns, "zout": turns}
    kinds = {"pe": ("unit", "row", "turn", "block", "value"), "act": ("low", "weight", "exp"),
             "dve": ("negate", "rowcopy", "zcopy", "zout", "max")}
    latency = {"pe": 300, "act": 100, "dve": 150}
    length = {"unit": 216, "max": 598, "negate": 1300, "weight": 300, "row": 250, "rowcopy": 600, "value": 940,
              "zcopy": 600, "turn": 300, "zout": 1200}

    def width(j):
        return CH if BLOCKS[j][2] is None else (BLOCKS[j][2] + 1) * P

    def long(kind, x):
        if kind == "low":
            return 240 + 0.833 * low_width(*UNITS[x])
        if kind in ("block", "exp"):
            return width(x) * 0.42 if kind == "block" else 50 + 0.833 * width(x)
        return length[kind]

    index = {kind: {x: n for n, x in enumerate(xs)} for kind, xs in items.items()}
    finish = {kind: [] for kind in items}

    def at(kind, p, x, back=0):
        n = index[kind].get((p, x), 0 if kind == "low" or back else -1)
        if (p, x) not in index[kind] or n - back < 0:
            return 0
        return finish[kind][n - back] if n - back < len(finish[kind]) else None

    def lows_last(g):
        return max(u for u in range((g + 1) * TPC * NKC) if low_width(*UNITS[u]))

    def needs(kind, p, x):
        if kind == "unit":
            v = x - NS
            return [at("low" if low_width(*UNITS[v]) else "max", p, v)] if v >= 0 else []
        if kind == "max":
            return [at("unit", p, x)]
        if kind == "low":
            return [at("max", p, x)]
        if kind == "negate":
            return [at("max", p, (x + 1) * TPC * NKC - 1), at("weight", p, x - 1), at("rowcopy", p, x - 1)]
        if kind == "weight":
            return [at("negate", p, x)]
        if kind == "row":
            return [at("negate", p, x)]
        if kind == "rowcopy":
            return [at("row", p, x)]
        if kind == "block":
            return [at("rowcopy", p, BLOCKS[x][0]), at("exp", p, x, NB)]
        if kind == "exp":
            back = index["exp"][(p, x)] - RING
            return [at("block", p, x), at("value", *quads[back // QUAD]) if back >= 0 else 0]
        if kind == "value":
            g = BLOCKS[x * QUAD][0]
            free = at("zout", p, g - 1) if g else at("zout", 1, NCH - 1)
            return [at("exp", p, x * QUAD + QUAD - 1), free]
        if kind == "zcopy":
            return [at("value", p, len([b for b in BLOCKS if b[0] <= x]) // QUAD - 1)]
        if kind == "turn":
            return [at("zcopy", p, x)]
        if kind == "zout":
            return [at("turn", p, x), at("low", p, lows_last(x)) if p == 0 else 0,
                    at("weight", p, x)]

    free, order = dict.fromkeys(kinds, 0), []
    while True:
        first = None
        for eng, own in kinds.items():
            for rank, kind in enumerate(own):
                if len(finish[kind]) == len(items[kind]):
                    continue
                p, x = items[kind][len(finish[kind])]
                ready = needs(kind, p, x)
                if None not in ready and (first is None or (max([free[eng], *ready]), rank) < first[:2]):
                    first = (max([free[eng], *ready]), rank, eng, kind, p, x)
        if first is None:
            return order
        start, _, eng, kind, p, x = first
        free[eng] = start + long(kind, x)
        finish[kind].append(free[eng] + latency[eng])
        order.append((kind, p, x))


def attend(nc, sem, V, ident, a, parts_dram, z_dram):
    with ExitStack() as ctx:
        def sb(part, shape, dt=F32):
            return ctx.enter_context(nc.sbuf_tensor(f"a_{part}", shape, dt))

        def sig(part):
            return sem(f"a_{part}")

        q = sb("q", [ROWS, 2, T], BF16)
        k = sb("k", [ROWS, 2, T], BF16)
        vh = sb("vh", [P, 2, NT, VW])
        sel = sb("sel", [P, VW])
        identb = sb("identb", [P, P], BF16)
        prob = sb("prob", [P, RING, CH])
        zeros = sb("zeros", [P, CH])
        keep = sb("keep", [P, P])
        neg_c = sb("neg_c", [P, 2, NT, NKC])
        sums_c = sb("sums_c", [P, 2, NT, NKC])
        neg = sb("neg", [P, TPC])
        neg_rest = sb("neg_rest", [P, TPC])
        neg3 = sb("neg3", [P, TPC, ROWS], BF16)
        lift = sb("lift", [P, TPC, NKC])
        weight = sb("weight", [P, 2, NCH, TPC, NKC])
        part_l = sb("part_l", [P, TPC, NKC])
        total = sb("total", [P, TPC])
        zT = sb("zT", [P, CH])
        z = sb("z", [P, 2, NT, HD])
        S = [ctx.enter_context(nc.psum_tensor(f"a_S{b}", [P, KC], F32)) for b in range(NS)]
        B = [ctx.enter_context(nc.psum_tensor(f"a_B{b}", [P, CH], F32)) for b in range(NB)]
        zacc = ctx.enter_context(nc.psum_tensor("a_zacc", [P, CH], F32))
        row_ps = ctx.enter_context(nc.psum_tensor("a_row", [P, CH], F32))

        const_ready, const_loaded, identb_ready, pool_own, vh_ready = (
            sig("const_ready"), sig("const_loaded"), sig("identb_ready"), sig("pool_own"), sig("vh_ready"))
        loaded = [sig(f"loaded{b}") for b in range(2)]
        z_stored = [sig(f"z_stored{b}") for b in range(2)]
        scored, unit_max, low_summed = sig("scored"), sig("unit_max"), sig("low_summed")
        neg_ready, neg_T, row_ready, weight_ready = sig("neg_ready"), sig("neg_T"), sig("row_ready"), sig("weight_ready")
        block_scored, prob_ready, masked, valued = sig("block_scored"), sig("prob_ready"), sig("masked"), sig("valued")
        z_copied, z_T, z_out, own_sem = sig("z_copied"), sig("z_T"), sig("z_out"), sig("own")

        order = head_order()
        assert all(len(s) % n == 0 for s, n in ((UNITS, NS), (BLOCKS, NB), (BLOCKS, RING)))
        NU, NBL, NQ = len(UNITS), len(BLOCKS), len(BLOCKS) // QUAD
        LOWS = lows_upto(NU - 1)
        NEGATE, ZOUT = 4, 4
        OWN = NCH * (NEGATE + ZOUT)
        OWN_FIRST = OWN - TAIL * ZOUT
        LOADS = 16 * 2 * len(SLOTS)
        for s in (unit_max, low_summed, z_out, prob_ready, valued, z_copied, weight_ready, z_T, *z_stored):
            nc.sync.sem_inc(s, FREE)

        def upto(h, per_head, n):
            return FREE + (max(0, h * per_head + n) if isinstance(h, int) else h * per_head + n)

        def blocks_upto(g):
            return sum(b[0] <= g for b in BLOCKS)

        def every_pass(run):
            def one_pass(h, b, parts=(0, 1)):
                for kind, p, x in order:
                    if p in parts:
                        run(kind, h - p, b ^ p, x)

            def both(eng, begin=lambda h, b: None):
                begin(0, 0)
                one_pass(0, 0, (0,))
                with eng.Fori(0, H // 2 - 1) as j:
                    for b in (1, 0):
                        begin(2 * j + 2 - b, b)
                        one_pass(2 * j + 2 - b, b)
                begin(H - 1, 1)
                one_pass(H - 1, 1)
                one_pass(H, 0, (1,))

            return both

        with nc.Block() as block:
            @block.sync
            def _(sp):
                sp.dma_start(sel[:], a["sel"]).then_inc(const_loaded, 16)

                def load(h, b):
                    for s, (pq, pk) in enumerate(SLOTS):
                        for dst, x, part in ((q, 0, pq), (k, 1, pk)):
                            src = parts_dram[x, part].rearrange("m p t -> (m p) t")
                            sp.dma_start(dst[s * HD:(s + 1) * HD, b, :], src[bass.ds(h * HD, HD), :]
                                         ).then_inc(loaded[b], 16)

                load(0, 0)
                load(1, 1)

                def store(h, b):
                    sp.wait_ge(z_out, FREE + (h + 1) * NCH)
                    sp.dma_start(z_dram[bass.ds(h, 1)].rearrange("o (i p) d -> p (o i) d", p=P),
                                 z[:, b]).then_inc(z_stored[b], 16)

                with sp.Fori(0, H // 2 - 1) as j:
                    for b in range(2):
                        h = 2 * j + b
                        sp.wait_ge(valued, FREE + (h + 1) * NQ)
                        load(h + 2, b)
                        store(h, b)
                store(H - 2, 0)
                store(H - 1, 1)
                for b in range(2):
                    sp.wait_ge(z_stored[b], FREE + H // 2 * 16)

            @block.gpsimd
            def _(pool):
                own = Order(pool, pool_own)
                for tile, value in ((vh[:], 0.0), (k[QK_ROWS:, :, :], 1.0), (zeros[:], 0.0), (neg3[:], 0.0),
                                    (sums_c[:], 0.0), (neg_c[:], 0.0)):
                    own.done(nc.gpsimd.memset(tile, value))
                own.done(nc.gpsimd.memset(keep[:], 1.0))
                own.done(nc.gpsimd.affine_select(out=keep[:], in_=keep[:], pattern=[[-1, P]], compare_op=ALU.is_ge,
                                                 fill=0.0, base=0, channel_multiplier=1))
                nc.gpsimd.memset(vh[:, :, :, HD:HD + 1], 1.0).then_inc(const_ready, 1)
                pool.wait_ge(const_ready, 1)

                def head(h, b, first=False):
                    if not first:
                        pool.wait_ge(valued, FREE + (h - 1) * NQ)
                    nc.gpsimd.tensor_copy(vh[:, b, :, 0:HD], V[:, :, bass.ds(h * HD, HD)]).then_inc(vh_ready, 1)
                    for j, (g, kb, r) in enumerate(BLOCKS):
                        if r is not None:
                            pool.wait_ge(prob_ready, FREE + h * NBL + j + 1)
                            blk = prob[:, j % RING, r * P:(r + 1) * P]
                            nc.gpsimd.tensor_tensor(blk, blk, keep[:], ALU.mult).then_inc(masked, 1)

                head(0, 0, True)
                head(1, 1, True)
                with pool.Fori(1, H // 2) as pair:
                    head(2 * pair, 0)
                    head(2 * pair + 1, 1)

            @block.scalar
            def _(act):
                act.wait_ge(const_ready, 1)

                def run(kind, h, b, x):
                    if kind == "low":
                        i, c = UNITS[x]
                        w = low_width(i, c)
                        act.wait_ge(unit_max, FREE + h * NU + x + 1)
                        nc.scalar.activation(S[x % NS][:, 0:w], S[x % NS][:, 0:w], ACT.Exp, bias=neg_c[:, b, i, c:c + 1],
                                             accum_out=sums_c[:, b, i, c:c + 1]).then_inc(low_summed, 1)
                    elif kind == "weight":
                        act.wait_ge(neg_ready, h * NCH + x + 1)
                        nc.scalar.activation(weight[:, b, x], lift[:], ACT.Exp).then_inc(weight_ready, 1)
                    elif kind == "exp":
                        g, kb, r = BLOCKS[x]
                        w = CH if r is None else (r + 1) * P
                        act.wait_ge(block_scored, h * NBL + x + 1)
                        act.wait_ge(valued, upto(h, NQ, (x - RING) // QUAD + 1))
                        nc.scalar.activation(prob[:, x % RING, 0:w], B[x % NB][:, 0:w], ACT.Exp).then_inc(prob_ready, 1)

                every_pass(run)(act)

            @block.vector
            def _(dve):
                dve.wait_ge(const_ready, 1)
                nc.vector.tensor_copy(identb[:], ident[:]).then_inc(identb_ready, 1)
                own = None

                def begin(h, b):
                    nonlocal own
                    own = Order(dve, own_sem, (h - 1) * OWN + OWN_FIRST if not isinstance(h, int) or h else 0)

                def run(kind, h, b, x):
                    if kind == "max":
                        i, c = UNITS[x]
                        dve.wait_ge(scored, h * NU + x + 1)
                        nc.vector.tensor_reduce(neg_c[:, b, i, c:c + 1], S[x % NS][:], AX.X, ALU.max,
                                                negate=True).then_inc(unit_max, 1)
                        return
                    rows = slice(x * TPC, (x + 1) * TPC)
                    if kind == "negate":
                        units = neg_c[:, b, rows, :]
                        dve.wait_ge(unit_max, FREE + h * NU + (x + 1) * TPC * NKC)
                        own.done(nc.vector.tensor_reduce(neg[:], units, AX.X, ALU.min))
                        dve.wait_ge(weight_ready, FREE + h * NCH + x)
                        nc.vector.tensor_tensor(lift[:], neg[:].rearrange("p (t o) -> p t o", o=1)
                                                .broadcast_to([P, TPC, NKC]), units, ALU.subtract)
                        own.done(nc.vector.tensor_copy(neg3[:, :, QK_ROWS], neg[:]))
                        own.done(nc.vector.tensor_tensor(neg_rest[:], neg[:], neg3[:, :, QK_ROWS], ALU.subtract))
                        own.done(nc.vector.tensor_copy(neg3[:, :, QK_ROWS + 1], neg_rest[:]))
                        nc.vector.tensor_tensor(neg3[:, :, QK_ROWS + 2], neg_rest[:], neg3[:, :, QK_ROWS + 1],
                                                ALU.subtract).then_inc(neg_ready, 1)
                    elif kind == "rowcopy":
                        dve.wait_ge(neg_T, h * NCH + x + 1)
                        nc.vector.tensor_copy(q[QK_ROWS:, b, x * CH:(x + 1) * CH],
                                              row_ps[QK_ROWS:ROWS, :]).then_inc(row_ready, 1)
                    elif kind == "zcopy":
                        dve.wait_ge(valued, FREE + h * NQ + blocks_upto(x) // QUAD)
                        dve.wait_ge(z_T, FREE + h * NCH + x)
                        nc.vector.tensor_copy(zT[:], zacc[:]).then_inc(z_copied, 1)
                    elif kind == "zout":
                        dve.wait_ge(low_summed, FREE + h * LOWS + lows_upto((x + 1) * TPC * NKC - 1))
                        dve.wait_ge(weight_ready, FREE + h * NCH + x + 1)
                        own.done(nc.vector.tensor_tensor(part_l[:], weight[:, b, x], sums_c[:, b, rows, :], ALU.mult))
                        own.done(nc.vector.tensor_reduce(total[:], part_l[:], AX.X, ALU.add))
                        dve.wait_ge(z_T, FREE + h * NCH + x + 1)
                        zt = zacc[:, 0:TPC * VW].rearrange("p (t v) -> p t v", v=VW)
                        own.done(nc.vector.tensor_tensor(total[:], total[:], zt[:, :, HD], ALU.add))
                        own.done(nc.vector.reciprocal(total[:], total[:]))
                        if x == 0:
                            dve.wait_ge(z_stored[b], FREE + (h - b) * 8)
                        nc.vector.tensor_tensor(z[:, b, rows, :], zt[:, :, 0:HD],
                                                total[:].rearrange("p (t o) -> p t o", o=1)
                                                .broadcast_to([P, TPC, HD]), ALU.mult).then_inc(z_out, 1)
                        dve.wait_ge(z_out, FREE + h * NCH + x + 1)

                every_pass(run)(dve, begin)

            @block.tensor
            def _(pe):
                pe.wait_ge(const_ready, 1)
                pe.wait_ge(const_loaded, 16)
                pe.wait_ge(identb_ready, 1)

                def begin(h, b):
                    pe.wait_ge(loaded[b], (h - b) * (LOADS // 2) + LOADS)

                def run(kind, h, b, x):
                    if kind == "unit":
                        i, c = UNITS[x]
                        pe.wait_ge(unit_max, upto(h, NU, x - NS + 1))
                        pe.wait_ge(low_summed, upto(h, LOWS, lows_upto(x - NS)))
                        nc.tensor.matmul(S[x % NS][:], q[0:QK_ROWS, b, i * P:(i + 1) * P],
                                         k[0:QK_ROWS, b, c * KC:(c + 1) * KC], start=True, stop=True).then_inc(scored, 1)
                    elif kind == "row":
                        pe.wait_ge(neg_ready, h * NCH + x + 1)
                        pe.wait_ge(row_ready, h * NCH + x)
                        for t in range(TPC):
                            last = nc.tensor.matmul(row_ps[0:ROWS, t * P:(t + 1) * P], neg3[:, t, :], identb[:],
                                                    start=True, stop=True)
                        last.then_inc(neg_T, 1)
                    elif kind == "block":
                        g, kb, r = BLOCKS[x]
                        w = CH if r is None else (r + 1) * P
                        pe.wait_ge(row_ready, h * NCH + g + 1)
                        pe.wait_ge(prob_ready, upto(h, NBL, x - NB + 1))
                        nc.tensor.matmul(B[x % NB][:, 0:w], k[:, b, kb * P:(kb + 1) * P],
                                         q[:, b, g * CH:g * CH + w], start=True, stop=True).then_inc(block_scored, 1)
                    elif kind == "value":
                        quad = [(j, *BLOCKS[j]) for j in range(x * QUAD, (x + 1) * QUAD)]
                        g, on_diagonal = quad[0][1], quad[0][3] is not None
                        if x * QUAD == blocks_upto(g - 1):
                            pe.wait_ge(z_out, FREE + h * NCH + g)
                            pe.wait_ge(vh_ready, h + 1)
                        if not on_diagonal:
                            pe.wait_ge(prob_ready, FREE + h * NBL + (x + 1) * QUAD)
                            for j, g, kb, r in quad:
                                col = kb % TPC * VW
                                last = nc.tensor.matmul(zacc[col:col + VW, :], vh[:, b, kb, :], prob[:, j % RING, :],
                                                        start=(kb < TPC * (g + 2)), stop=False)
                        else:
                            pe.wait_ge(masked, h * NT + TPC * (g + 1))
                            if g == NCH - 1:
                                for j, g, kb, r in quad:
                                    col = kb % TPC * VW
                                    nc.tensor.matmul(zacc[col:col + VW, :], vh[:, b, kb, :], zeros[:],
                                                     start=True, stop=False)
                            for j, g, kb, r in quad:
                                col = kb % TPC * VW
                                if r > 0:
                                    nc.tensor.matmul(zacc[col:col + VW, 0:r * P], vh[:, b, kb, :],
                                                     prob[:, j % RING, 0:r * P], start=False, stop=False)
                                last = nc.tensor.matmul(zacc[col:col + HD, r * P:(r + 1) * P], vh[:, b, kb, 0:HD],
                                                        prob[:, j % RING, r * P:(r + 1) * P], start=False, stop=True)
                        last.then_inc(valued, 1)
                    elif kind == "turn":
                        pe.wait_ge(z_copied, FREE + h * NCH + x + 1)
                        for t in range(TPC):
                            last = nc.tensor.matmul(zacc[:, t * VW:(t + 1) * VW], zT[:, t * P:(t + 1) * P], sel[:],
                                                    start=True, stop=True)
                        last.then_inc(z_T, 1)

                every_pass(run)(pe, begin)


def attention_out(nc, sem, X, a, z_dram):
    with ExitStack() as ctx:
        def sb(part, shape, dt=F32):
            return ctx.enter_context(nc.sbuf_tensor(f"o_{part}", shape, dt))

        def sig(part):
            return sem(f"o_{part}")

        gamma, beta, half = sb("gamma", [P, 1, DM]), sb("beta", [P, 1, DM]), sb("half", [P, TPC])
        f = sb("f", [P, 2, TPC, DM])
        z = sb("z", [P, 2, TPC, DM])
        z_tiles = z_dram.rearrange("h q d -> (h q d)").rearrange("(j p d) -> p j d", p=P, d=DM)
        z_ready = [sig(f"z_ready{b}") for b in range(2)]
        norm_in, norm_mid, norm_out = (Norm(nc, ctx, sem, f"o_{x}", LN_EPS) for x in ("in", "mid", "out"))
        w_ready, const_ready = sig("w_ready"), sig("const_ready")
        mid_ready, mid_own, mid_affine, first_own, second_own = (
            sig("mid_ready"), sig("mid_own"), sig("mid_affine"), sig("first_own"), sig("second_own"))
        FIRST, SECOND = 2 * Norm.ORDERS + 2, Norm.ORDERS + 2

        with nc.Block() as block:
            @block.sync
            def _(sp):
                sp.dma_start(gamma[:], a["attn_gamma"]).then_inc(w_ready, 16)
                sp.dma_start(beta[:], a["attn_beta"]).then_inc(w_ready, 16)

                def load(c, b):
                    if before(c, 2):
                        sp.wait_ge(mid_ready, c - 1)
                    sp.dma_start(z[:, b], z_tiles[:, bass.ds(c * TPC, TPC), :]).then_inc(z_ready[b], 16)

                staged(sp, [(2, load), (0, lambda c, b: None)])

            @block.gpsimd
            def _(pool):
                nc.gpsimd.memset(half[:], -0.5).then_inc(const_ready, 1)
                pool.wait_ge(const_ready, 1)
                pool.wait_ge(w_ready, 32)

                def first(c, b):
                    norm_in.power(pool, half, c)
                    norm_mid.power(pool, half, c)
                    pool.wait_ge(mid_ready, c + 1)
                    nc.gpsimd.tensor_tensor(f[:, b], f[:, b], gamma[:].broadcast_to([P, TPC, DM]),
                                            ALU.mult).then_inc(mid_own, 1)
                    pool.wait_ge(mid_own, c + 1)
                    nc.gpsimd.tensor_tensor(f[:, b], f[:, b], beta[:].broadcast_to([P, TPC, DM]),
                                            ALU.add).then_inc(mid_affine, 1)

                staged(pool, [(1, first), (0, lambda c, b: norm_out.power(pool, half, c))])

            @block.vector
            def _(dve):
                def first(c, b):
                    own = Order(dve, first_own, c * FIRST)
                    part = lambda t: f[:, b, t, :]
                    norm_in.begin(own, lambda t: X[:, tok(c, t), :])
                    own.done(norm_in.scale(dve, c, part, lambda t: X[:, tok(c, t), :]))
                    dve.wait_ge(z_ready[b], (c - b) * 8 + 16)
                    own.done(nc.vector.tensor_tensor(f[:, b], f[:, b], z[:, b], ALU.add))
                    norm_mid.begin(own, part)
                    norm_mid.scale(dve, c, part, part).then_inc(mid_ready, 1)
                    own.close(FIRST)

                def second(c, b):
                    own = Order(dve, second_own, c * SECOND)
                    part = lambda t: f[:, b, t, :]
                    dve.wait_ge(mid_affine, c + 1)
                    norm_out.begin(own, part)
                    own.done(norm_out.scale(dve, c, part, part))
                    for t in range(TPC):
                        last = nc.vector.tensor_tensor(X[:, tok(c, t), :], X[:, tok(c, t), :], part(t), ALU.add)
                    own.done(last)
                    own.close(SECOND)

                staged(dve, [(1, first), (0, second)])


NE = 16
NG = 4
GE = NE // NG
TOP_K = 4
TOP_G = 2
SCALE = 2.5
ME = 128
NX = NE + 2 * ME // ME


def normed_transposed(nc, sem, X, nT, ident, name, extra=None):
    with ExitStack() as ctx:
        def sb(part, shape, dt=F32):
            return ctx.enter_context(nc.sbuf_tensor(f"{name}_{part}", shape, dt))

        def sig(part):
            return sem(f"{name}_{part}")

        half = sb("half", [P, TPC])
        n = sb("n", [P, 2, TPC, DM])
        norm = Norm(nc, ctx, sem, f"{name}_norm", LN_EPS)
        bank = [ctx.enter_context(nc.psum_tensor(f"{name}_bank{b}", [P, CH], F32)) for b in range(4)]
        const_ready, n_ready, nT_ps, nT_ready, own_sem = (
            sig("const_ready"), sig("n_ready"), sig("nT_ps"), sig("nT_ready"), sig("own"))

        with nc.Block() as block:
            @block.gpsimd
            def _(pool):
                nc.gpsimd.memset(half[:], -0.5).then_inc(const_ready, 1)
                pool.wait_ge(const_ready, 1)
                staged(pool, [(1, lambda c, b: norm.power(pool, half, c))])

            @block.vector
            def _(dve):
                def normed(c, b):
                    own = Order(dve, own_sem, c * Norm.ORDERS)
                    norm.begin(own, lambda t: X[:, tok(c, t), :])
                    if before(c, 2):
                        dve.wait_ge(nT_ps, c - 1)
                    norm.scale(dve, c, lambda t: n[:, b, t, :], lambda t: X[:, tok(c, t), :]).then_inc(n_ready, 1)

                staged(dve, [(2, normed)])

            @block.tensor
            def _(pe):
                def transposes(c, b):
                    pe.wait_ge(n_ready, c + 1)
                    if before(c, 2):
                        pe.wait_ge(nT_ready, c - 1)
                    for t in range(TPC):
                        for k in range(KD):
                            last = nc.tensor.transpose(bank[b * KD + k][:, t * P:(t + 1) * P],
                                                       n[:, b, t, k * P:(k + 1) * P], ident[:])
                    last.then_inc(nT_ps, 1)

                staged(pe, [(2, transposes)])

            @block.scalar
            def _(act):
                def copied(c, b):
                    act.wait_ge(nT_ps, c + 1)
                    for k in range(KD):
                        last = nc.scalar.copy(nT[:, k, bass.ds(c * CH, CH)], bank[b * KD + k][:])
                    last.then_inc(nT_ready, 1)

                staged(act, [(1, copied)])


def route(nc, sem, nT, combine, a):
    with ExitStack() as ctx:
        def sb(part, shape, dt=F32):
            return ctx.enter_context(nc.sbuf_tensor(f"g_{part}", shape, dt))

        def sig(part):
            return sem(f"g_{part}")

        w = sb("w", [P, KD, NE])
        bias = sb("bias", [P, 1, NE])
        score = sb("score", [P, NT, NE])
        group = sb("group", [P, NT, NG])
        pair = sb("pair", [P, NT, NG])
        g_rank = sb("g_rank", [P, NT, NG])
        wins = sb("wins", [P, NT, 1])
        rank = sb("rank", [P, NT, NE])
        beaten = sb("beaten", [P, NT, NE])
        total = sb("total", [P, NT, 1])
        logits = ctx.enter_context(nc.psum_tensor("g_logits", [P, NT, NE], F32))
        w_ready, logit_ready, score_ready, own_sem = sig("w_ready"), sig("logit_ready"), sig("score_ready"), sig("own")
        nT3 = nT[:].rearrange("p k (j t) -> p k j t", t=P)

        with nc.Block() as block:
            @block.sync
            def _(sp):
                sp.dma_start(w[:], a["gate_w"]).then_inc(w_ready, 16)
                sp.dma_start(bias[:], a["gate_b"]).then_inc(w_ready, 16)

            @block.tensor
            def _(pe):
                pe.wait_ge(w_ready, 32)
                for i in range(NT):
                    for k in range(KD):
                        last = nc.tensor.matmul(logits[:, i, :], nT3[:, k, i, :], w[:, k, :],
                                                start=(k == 0), stop=(k == KD - 1))
                last.then_inc(logit_ready, 1)

            @block.scalar
            def _(act):
                act.wait_ge(logit_ready, 1)
                nc.scalar.activation(score[:], logits[:], ACT.Sigmoid).then_inc(score_ready, 1)

            @block.vector
            def _(dve):
                own = Order(dve, own_sem)
                tt = nc.vector.tensor_tensor
                dve.wait_ge(w_ready, 32)
                dve.wait_ge(score_ready, 1)
                own.done(tt(score[:], score[:], bias[:].broadcast_to([P, NT, NE]), ALU.add))
                member = score[:].rearrange("p i (g e) -> p i g e", e=GE)
                pairs = [(x, y) for x in range(GE) for y in range(x + 1, GE)]
                for n, (x, y) in enumerate(pairs):
                    dst = pair if n else group
                    own.done(tt(dst[:], member[:, :, :, x], member[:, :, :, y], ALU.add))
                    if n:
                        own.done(tt(group[:], group[:], pair[:], ALU.max))
                own.done(nc.vector.memset(g_rank[:], 0.0))
                for x in range(NG):
                    for y in range(x + 1, NG):
                        gx, gy = group[:, :, x:x + 1], group[:, :, y:y + 1]
                        own.done(tt(wins[:], gx, gy, ALU.is_ge))
                        own.done(tt(g_rank[:, :, y:y + 1], g_rank[:, :, y:y + 1], wins[:], ALU.add))
                        own.done(tt(wins[:], gx, gy, ALU.is_lt))
                        own.done(tt(g_rank[:, :, x:x + 1], g_rank[:, :, x:x + 1], wins[:], ALU.add))
                own.done(nc.vector.tensor_scalar(g_rank[:], g_rank[:], float(TOP_G), None, ALU.is_lt))
                for x in range(GE):
                    last = tt(member[:, :, :, x], member[:, :, :, x], g_rank[:], ALU.mult)
                own.done(last)
                own.done(nc.vector.memset(rank[:], 0.0))
                for x in range(NE):
                    one = score[:, :, x:x + 1]
                    if x:
                        last = tt(beaten[:, :, 0:x], one.broadcast_to([P, NT, x]), score[:, :, 0:x], ALU.is_gt)
                    if x < NE - 1:
                        last = tt(beaten[:, :, x + 1:], one.broadcast_to([P, NT, NE - 1 - x]), score[:, :, x + 1:],
                                  ALU.is_ge)
                    own.done(last)
                    if x:
                        last = tt(rank[:, :, 0:x], rank[:, :, 0:x], beaten[:, :, 0:x], ALU.add)
                    if x < NE - 1:
                        last = tt(rank[:, :, x + 1:], rank[:, :, x + 1:], beaten[:, :, x + 1:], ALU.add)
                    own.done(last)
                own.done(nc.vector.tensor_scalar(rank[:], rank[:], float(TOP_K), None, ALU.is_lt))
                own.done(tt(score[:], score[:], rank[:], ALU.mult))
                own.done(nc.vector.tensor_reduce(total[:].rearrange("p i o -> p (i o)"), score[:], AX.X, ALU.add))
                own.done(nc.vector.tensor_scalar(total[:], total[:], 1e-20, None, ALU.add))
                own.done(nc.vector.reciprocal(total[:], total[:]))
                own.done(tt(score[:], score[:], total[:].broadcast_to([P, NT, NE]), ALU.mult))
                nc.vector.memset(combine[:, :, NE:], 1.0)
                own.done(nc.vector.tensor_scalar(combine[:, :, 0:NE], score[:], SCALE, None, ALU.mult))


def experts(nc, sem, nT, Y, combine, a):
    with ExitStack() as ctx:
        def sb(part, shape, dt=F32):
            return ctx.enter_context(nc.sbuf_tensor(f"e_{part}", shape, dt))

        def sig(part):
            return sem(f"e_{part}")

        wg, wu = sb("wg", [P, 2, KD, ME]), sb("wu", [P, 2, KD, ME])
        wd = sb("wd", [P, 2, DM])
        gate = sb("gate", [P, 2, CH])
        inter = sb("inter", [P, 2, CH])
        G = [ctx.enter_context(nc.psum_tensor(f"e_G{b}", [P, CH], F32)) for b in range(2)]
        U = [ctx.enter_context(nc.psum_tensor(f"e_U{b}", [P, CH], F32)) for b in range(2)]
        O = [ctx.enter_context(nc.psum_tensor(f"e_O{b}", [P, TPC, DM], F32)) for b in range(2)]
        gu_ps, gate_ready, inter_ready, out_ps, out_used, own_sem = (
            sig("gu_ps"), sig("gate_ready"), sig("inter_ready"), sig("out_ps"), sig("out_used"), sig("own"))
        loaded = [sig(f"loaded{b}") for b in range(2)]
        DONE = 2
        for s in (inter_ready, out_ps, out_used):
            nc.sync.sem_inc(s, DONE)


        def every(eng, step, ahead=None):
            STEPS = 2 * NCH

            def at(x, m):
                eb, c = m % STEPS // NCH, m % NCH
                return x * STEPS + m, (x + m // STEPS) * 2 + eb, eb, c, c % 2

            def one_pass(x, last=False):
                for m in range(STEPS):
                    if ahead and not (last and m == STEPS - 1):
                        ahead(*at(x, m + 1))
                    step(*at(x, m))

            if ahead:
                ahead(*at(0, 0))
            with eng.Fori(0, NX // 2 - 1) as x:
                one_pass(x)
            one_pass(NX // 2 - 1, True)

        with nc.Block() as block:
            @block.sync
            def _(sp):
                def load(e, eb):
                    for dst, src in ((wg, "wg"), (wu, "wu"), (wd, "wd")):
                        sp.dma_start(dst[:, eb], a[f"moe_{src}"][:, bass.ds(e, 1)].rearrange(
                            "p o k m -> p (o k) m" if src != "wd" else "p o m -> p (o m)")).then_inc(loaded[eb], 16)

                load(0, 0)
                load(1, 1)
                with sp.Fori(0, NX // 2 - 1) as x:
                    for eb in range(2):
                        e = 2 * x + eb
                        sp.wait_ge(out_ps, DONE + (e + 1) * NCH)
                        load(e + 2, eb)

            @block.scalar
            def _(act):
                def step(n, e, eb, c, b):
                    act.wait_ge(gu_ps, n + 1)
                    act.wait_ge(inter_ready, DONE + n - 1)
                    nc.scalar.activation(gate[:, b], G[b][:], ACT.Silu).then_inc(gate_ready, 1)

                every(act, step)

            @block.vector
            def _(dve):
                nc.vector.memset(Y[:], 0.0).then_inc(own_sem, 1)
                dve.wait_ge(own_sem, 1)

                def gated(n, e, eb, c, b):
                    dve.wait_ge(gate_ready, n + 1)
                    dve.wait_ge(out_ps, DONE + n - 1)
                    nc.vector.tensor_tensor(inter[:, b], gate[:, b], U[b][:], ALU.mult).then_inc(inter_ready, 1)

                def weighted(n, e, eb, c, b):
                    dve.wait_ge(out_ps, DONE + n + 1)
                    dve.wait_ge(out_used, DONE + n - 1)
                    for t in range(TPC):
                        last = nc.vector.scalar_tensor_tensor(Y[:, tok(c, t), :], O[b][:, t, :],
                                                              combine[:, tok(c, t), bass.ds(e, 1)],
                                                              Y[:, tok(c, t), :], ALU.mult, ALU.add)
                    last.then_inc(out_used, 1)

                every(dve, weighted, gated)

            @block.tensor
            def _(pe):
                def gate_up(n, e, eb, c, b):
                    pe.wait_ge(loaded[eb], (e - eb) * 24 + 48)
                    pe.wait_ge(inter_ready, DONE + n - 1)
                    for ps, w in ((G, wg), (U, wu)):
                        for k in range(KD):
                            last = nc.tensor.matmul(ps[b][:], w[:, eb, k, :], nT[:, k, c * CH:(c + 1) * CH],
                                                    start=(k == 0), stop=(k == KD - 1))
                    last.then_inc(gu_ps, 1)

                def down(n, e, eb, c, b):
                    pe.wait_ge(inter_ready, DONE + n + 1)
                    pe.wait_ge(out_used, DONE + n - 1)
                    for t in range(TPC):
                        last = nc.tensor.matmul(O[b][:, t, :], inter[:, b, t * P:(t + 1) * P], wd[:, eb, :],
                                                start=True, stop=True)
                    last.then_inc(out_ps, 1)

                every(pe, down, gate_up)


def experts_out(nc, sem, X, Y, a):
    with ExitStack() as ctx:
        half = ctx.enter_context(nc.sbuf_tensor("f_half", [P, TPC], F32))
        norm = Norm(nc, ctx, sem, "f_norm", LN_EPS)
        const_ready, x_done, own_sem, stored = sem("f_const_ready"), sem("f_x_done"), sem("f_own"), sem("f_stored")
        out_tiles = a["out"][0].rearrange("(j p) d -> p j d", p=P)
        with nc.Block() as block:
            @block.sync
            def _(sp):
                def store(c, b):
                    sp.wait_ge(x_done, c + 1)
                    sp.dma_start(out_tiles[:, bass.ds(c * TPC, TPC), :], X[:, bass.ds(c * TPC, TPC), :]
                                 ).then_inc(stored, 16)

                staged(sp, [(0, store)])
                sp.wait_ge(stored, NCH * 16)

            @block.gpsimd
            def _(pool):
                nc.gpsimd.memset(half[:], -0.5).then_inc(const_ready, 1)
                pool.wait_ge(const_ready, 1)
                staged(pool, [(0, lambda c, b: norm.power(pool, half, c))])

            @block.vector
            def _(dve):
                def step(c, b):
                    own = Order(dve, own_sem, c * (Norm.ORDERS + 1))
                    norm.begin(own, lambda t: Y[:, tok(c, t), :])
                    own.done(norm.scale(dve, c, lambda t: Y[:, tok(c, t), :], lambda t: Y[:, tok(c, t), :]))
                    for t in range(TPC):
                        last = nc.vector.tensor_tensor(X[:, tok(c, t), :], X[:, tok(c, t), :], Y[:, tok(c, t), :],
                                                       ALU.add)
                    last.then_inc(x_done, 1)

                staged(dve, [(0, step)])


def host_arrays(g):
    c = np.ascontiguousarray
    spread = np.zeros((SPLIT * BC, BC, P), np.float32)
    for r in range(BC):
        for s in range(SPLIT):
            spread[s * BC + r, r, :] = 1
    xp = g["L0_attn_x_proj_w"].T

    def rows(w):
        return c(np.moveaxis(w.reshape(-1, P, *w.shape[1:]), 0, 1))

    def every(v):
        return c(np.broadcast_to(v, (P, 1, v.size)))

    def ffn(name, w1, b1, w2, b2):
        return {f"{name}_w1": rows(w1.T), f"{name}_b1": rows(b1), f"{name}_w2": rows(w2.T), f"{name}_b2": c(b2[None])}

    def up(w, shared):
        both = np.concatenate([w, shared.reshape(DM, -1, ME).transpose(1, 0, 2)], 0)
        return c(both.reshape(NX, KD, P, ME).transpose(2, 0, 1, 3))

    return {
        "L0_attn_x": c(g["L0_attn_x"]),
        "in_proj_t": rows(g["L0_attn_in_proj_w"].T),
        "x_proj_t": rows(np.concatenate([xp[:, DTR:]] * SPLIT + [xp[:, :DTR]], 1)),
        "dt_proj_t": c(g["L0_attn_dt_proj_w"].T),
        "out_proj_t": rows(g["L0_attn_out_proj_w"].T),
        "conv_w": rows(g["L0_attn_conv_w"]),
        "conv_b": rows(g["L0_attn_conv_b"]),
        "dt_b": rows(g["L0_attn_dt_proj_b"]),
        "skip_d": rows(g["L0_attn_D"]),
        "a_log": rows(g["L0_attn_A_log"]),
        "x_tiles": c(g["L0_attn_x"].reshape(NCH, CH, DM)),
        **ffn("tail", g["L0_attn_ffn_w1"], g["L0_attn_ffn_b1"], g["L0_attn_ffn_w2"], g["L0_attn_ffn_b2"]),
        "tail_in_w": rows(g["L0_attn_ln1_w"]), "tail_in_b": rows(g["L0_attn_ln1_b"]),
        "tail_mid_w": every(g["L0_attn_ln2_w"]), "tail_mid_b": every(g["L0_attn_ln2_b"]),
        **ffn("bit", g["L0_ffn_W1"], g["L0_ffn_b1"], g["L0_ffn_W2"], g["L0_ffn_b2"]),
        "attn_w": np.concatenate([rows(g[f"L1_attn_W{x}"].T) for x in "qkv"], 2),
        "attn_qk_b": np.stack([rows(g["L1_attn_bq"]), rows(g["L1_attn_bk"])], 1),
        "attn_v_b": c(g["L1_attn_bv"][None]),
        "attn_gamma": every(g["L1_attn_gamma"]), "attn_beta": every(g["L1_attn_beta"]),
        "gate_w": rows(g["L1_ffn_gate_kernel"]), "gate_b": every(g["L1_ffn_gate_bias"]),
        "moe_wg": up(g["L1_ffn_w_gate"], g["L1_ffn_sw_gate"]), "moe_wu": up(g["L1_ffn_w_up"], g["L1_ffn_sw_up"]),
        "moe_wd": c(np.concatenate([g["L1_ffn_w_down"], g["L1_ffn_sw_down"].reshape(-1, ME, DM)], 0).transpose(1, 0, 2)),
        "sel": np.tile(np.eye(VW, dtype=np.float32), (P // VW, 1)),
        "ident": np.eye(P, dtype=np.float32),
        "spread": spread.reshape(SPLIT * BC, BC * P),
    }


def phase(nc, build, *args):
    held = []

    def sem(name):
        held.append(nc.alloc_semaphore(name=name))
        return held[-1]

    build(nc, sem, *args)
    nc.clear_and_free_semaphores(held)
    nc.all_engine_barrier()


def program(nc, a):
    with ExitStack() as ctx:
        parts_dram = nc.dram_tensor("parts", (2, SPLIT, KD, P, T), BF16, kind="Internal").ap()
        z_dram = nc.dram_tensor("z", (H, T, HD), F32, kind="Internal").ap()
        X = ctx.enter_context(nc.sbuf_tensor("X", [P, NT, DM], F32))
        ident = ctx.enter_context(nc.sbuf_tensor("ident", [P, P], F32))
        phase(nc, mamba, X, ident, a)
        phase(nc, feed_forward, X, ident, a, "tail", 2 * DM, True)
        phase(nc, feed_forward, X, ident, a, "bit", 4 * DM, False)
        with nc.sbuf_tensor("V", [P, NT, DM], F32) as V:
            phase(nc, project, X, V, ident, a, parts_dram)
            phase(nc, attend, V, ident, a, parts_dram, z_dram)
        phase(nc, attention_out, X, a, z_dram)
        with nc.sbuf_tensor("combine", [P, NT, NX], F32) as combine, nc.sbuf_tensor("Y", [P, NT, DM], F32) as Y:
            with nc.sbuf_tensor("nT", [P, KD, T], F32) as nT:
                phase(nc, normed_transposed, X, nT, ident, "r")
                phase(nc, route, nT, combine, a)
                phase(nc, experts, nT, Y, combine, a)
            phase(nc, experts_out, X, Y, a)


def kernel(**inputs):
    import concourse.bacc as bacc
    from concourse.bass_utils import run_bass_kernel_spmd

    nc = bacc.Bacc("TRN2", target_bir_lowering=False, num_devices=1)
    arrays = host_arrays({name: np.asarray(value) for name, value in inputs.items()})
    a = {name: nc.dram_tensor(f"in_{name}", v.shape, mybir.dt.from_np(v.dtype), kind="ExternalInput").ap()
         for name, v in arrays.items()}
    a["out"] = nc.dram_tensor("out", (1, T, DM), F32, kind="ExternalOutput").ap()
    program(nc, a)
    ran = run_bass_kernel_spmd(nc, [{f"in_{name}": v for name, v in arrays.items()}], core_ids=[0])
    return ran.results[0]["out"]
```

```python
import numpy as np
from contextlib import ExitStack
import concourse.bass as bass
from concourse import mybir

F32 = mybir.dt.float32
BF16 = mybir.dt.bfloat16
F32R = mybir.dt.float32r
ALU = mybir.AluOpType
ACT = mybir.ActivationFunctionType
AX = mybir.AxisListType

P = 128
T = 4096
DM = 256
NT = T // P
CH = 512
NCH = T // CH
TPC = CH // P
KD = DM // P
DI = 512
ND = DI // P
DS = 16
DTR = 16
DC = 4
SPLIT = 3
BC = 2 * DS
XP = SPLIT * BC + DTR
LN_EPS = 1e-5
MAMBA_EPS = 1e-12
FREE = 1


class Order:

    def __init__(self, eng, sem, base=0):
        self.eng, self.sem, self.base, self.n = eng, sem, base, 0

    def close(self, per_pass):
        assert self.n == per_pass, (self.n, per_pass)

    def done(self, ins):
        ins.then_inc(self.sem, 1)
        self.n += 1
        self.eng.wait_ge(self.sem, self.base + self.n)


def peeled(eng, count, first, second):
    first(0)
    with eng.Fori(0, count - 1) as i:
        first(i + 1)
        second(i)
    second(count - 1)


def tok(c, t):
    return c * TPC + t


NH = 3
SLOT = [[(n + b) % NH for n in range(DS)] for b in range(2)]


def lap(b, n):
    earlier = SLOT[1 - b] + SLOT[b][:n]
    return next(d for d in range(1, DS) if earlier[-d] == SLOT[b][n])


def wait_past(eng, sem, value):
    if not isinstance(value, int) or value > 0:
        eng.wait_ge(sem, value)


def mamba_chunks(eng, spread_first, state, pre, post, begin=None):
    def chunk(i, b, before=True, after=True):
        if begin:
            begin(i, b)
        for n in range(DS):
            state(n, i, b)
            if before:
                post(n, i - 1, 1 - b)
            if after:
                pre(n, i + 1, 1 - b)
        if after:
            spread_first(i + 1, 1 - b)

    for s in range(DS):
        pre(s, 0, 0)
    spread_first(0, 0)
    chunk(0, 0, before=False)
    with eng.Fori(0, NCH // 2 - 1) as j:
        chunk(2 * j + 1, 1)
        chunk(2 * j + 2, 0)
    chunk(NCH - 1, 1, after=False)
    for s in range(-1, DS):
        post(s, NCH - 1, 1)


def mamba(nc, sem, X, ident, a):
    with ExitStack() as ctx:
        def sb(name, shape, dt=F32):
            return ctx.enter_context(nc.sbuf_tensor(name, shape, dt))

        w_in = sb("w_in", [P, KD, 2 * DI])
        w_out = sb("w_out", [P, ND, DM])
        w_xp = sb("w_xp", [P, ND, XP])
        w_dt = sb("w_dt", [P, DI])
        conv_w = sb("conv_w", [P, ND, DC])
        conv_b = sb("conv_b", [P, ND])
        dt_b = sb("dt_b", [P, ND])
        skip_d = sb("skip_d", [P, ND])
        a_neg = sb("m_a_neg", [P, ND, DS])
        spread = sb("spread", [SPLIT * BC, BC, P], BF16)
        stats = sb("m_stats", [P, TPC, 6])
        mv = sb("m_mv", [P, TPC, 2])
        var = sb("m_var", [P, TPC])
        spare = sb("m_spare", [P, 1])
        rstd = sb("m_rstd", [P, TPC])
        half = sb("m_half", [P, TPC])
        xn = sb("m_xn", [P, TPC, DM])
        xnT = sb("m_xnT", [P, KD, CH])
        raw = sb("m_raw", [P, ND, CH + DC - 1])
        xs = sb("m_xs", [P, 2, ND, CH])
        zs = sb("m_zs", [P, 2, ND, CH])
        dt = sb("m_dt", [P, 2, ND, CH])
        soft = sb("m_soft", [P, ND, CH])
        u = sb("m_u", [P, ND, CH])
        bc3 = sb("m_bc3", [SPLIT * BC, 2, CH], BF16)
        mid = sb("m_mid", [SPLIT * BC, CH], BF16)
        low = sb("m_low", [SPLIT * BC, CH], BF16)
        rest = sb("m_rest", [SPLIT * BC, CH])
        dtr = sb("m_dtr", [P, CH])
        dA = sb("m_dA", [P, NH, ND, CH])
        spread_f = dA[0:SPLIT * BC, 0:2].rearrange("p a b t -> p (a b t)")
        dBx = sb("m_dBx", [P, ND, CH])
        h = sb("m_h", [P, NH, ND, CH])
        crep = sb("m_crep", [P, NH, CH])
        h_end = sb("m_h_end", [P, DS, ND])
        Y = [ctx.enter_context(nc.psum_tensor(f"m_Y{m}", [P, CH], F32)) for m in range(ND)]
        B = ctx.enter_context(nc.psum_tensor("m_B", [P, CH], F32))
        C = ctx.enter_context(nc.psum_tensor("m_C", [P, CH], F32))
        W = [ctx.enter_context(nc.psum_tensor(f"m_W{b}", [P, CH], F32)) for b in range(2)]

        w_ready, w_first, conv_loaded = sem("m_w_ready"), sem("m_w_first"), sem("m_conv_loaded")
        x_first, x_ready = sem("m_x_first"), sem("m_x_ready")
        const_ready, spread_ready = sem("m_const_ready"), sem("m_spread_ready")
        var_ready, rstd_ready = sem("m_var_ready"), sem("m_rstd_ready")
        xn_ready, xT_ready, xnT_ready = sem("m_xn_ready"), sem("m_xT_ready"), sem("m_xnT_ready")
        proj_ready, raw_ready, conv_ready = sem("m_proj_ready"), sem("m_raw_ready"), sem("m_conv_ready")
        z_copied, z_ready, xs_ready, xp_ready = sem("m_z_copied"), sem("m_z_ready"), sem("m_xs_ready"), sem("m_xp_ready")
        bc_ready, dtr_ready, dtp_ready = sem("m_bc_ready"), sem("m_dtr_ready"), sem("m_dtp_ready")
        v_ready, soft_ready, dt_ready = sem("m_v_ready"), sem("m_soft_ready"), sem("m_dt_ready")
        b_spread, c_spread, crep_ready = sem("m_b_spread"), sem("m_c_spread"), sem("m_crep_ready")
        dA_ready, b_used = sem("m_dA_ready"), sem("m_b_used")
        h_ready, h_kept, g_ready, g_summed = sem("m_h_ready"), sem("m_h_kept"), sem("m_g_ready"), sem("m_g_summed")
        y_read, yg_ready, out_ready, out_added = sem("m_y_read"), sem("m_yg_ready"), sem("m_out_ready"), sem("m_out_added")
        v_pre, v_u, s_own = sem("m_v_pre"), sem("m_v_u"), sem("m_s_own")
        V_PRE, S_PRE = 12, 3

        def nothing(*_):
            pass

        with nc.Block() as block:
            @block.sync
            def _(sp):
                XQ = NT // 4

                def load_x(q, ready):
                    sp.dma_start(X[:, q * XQ:(q + 1) * XQ, :],
                                 a["L0_attn_x"][0, q * XQ * P:(q + 1) * XQ * P, :].rearrange("(j p) d -> p j d", p=P)
                                 ).then_inc(ready, 16)

                load_x(0, x_first)
                sp.dma_start(ident[:], a["ident"]).then_inc(w_first, 16)
                sp.dma_start(w_in[:], a["in_proj_t"]).then_inc(w_first, 16)
                sp.dma_start(w_xp[:], a["x_proj_t"]).then_inc(w_ready, 16)
                sp.dma_start(w_dt[SPLIT * BC:XP, :], a["dt_proj_t"]).then_inc(w_ready, 16)
                sp.dma_start(spread_f, a["spread"]).then_inc(w_ready, 16)
                for q in range(1, 4):
                    load_x(q, x_ready)
                sp.dma_start(w_out[:], a["out_proj_t"]).then_inc(w_ready, 16)

            @block.gpsimd
            def _(pool):
                nc.gpsimd.memset(half[:], -0.5).then_inc(const_ready, 1)
                nc.gpsimd.memset(h_end[:], 0.0).then_inc(const_ready, 1)
                nc.gpsimd.memset(raw[:, :, CH:], 0.0).then_inc(const_ready, 1)
                pool.wait_ge(const_ready, 3)

                def pre(s, c, b):
                    if s == 1:
                        pool.wait_ge(var_ready, c + 1)
                        nc.gpsimd.tensor_tensor(rstd[:], var[:], half[:], ALU.pow).then_inc(rstd_ready, 1)

                def state(n, i, b):
                    slot = SLOT[b][n]
                    pool.wait_ge(crep_ready, i * DS + n + 1)
                    pool.wait_ge(h_kept, i * DS + n + 1)
                    nc.gpsimd.tensor_tensor(h[:, slot], h[:, slot],
                                            crep[:, slot:slot + 1, :].broadcast_to([P, ND, CH]),
                                            ALU.mult).then_inc(g_ready, 1)

                mamba_chunks(pool, nothing, state, pre, nothing)

            @block.scalar
            def _(act):
                for to, src in ((conv_w, "conv_w"), (conv_b, "conv_b"), (dt_b, "dt_b"), (skip_d, "skip_d"),
                                (a_neg, "a_log")):
                    act.dma_start(to[:], a[src]).then_inc(conv_loaded, 16)
                act.wait_ge(conv_loaded, 16 * 5)
                setup = Order(act, s_own)
                setup.done(nc.scalar.activation(a_neg[:], a_neg[:], ACT.Exp))
                setup.done(nc.scalar.mul(a_neg[:], a_neg[:], -1.0))
                act.wait_ge(const_ready, 3)
                own = None

                def pre(s, c, b):
                    nonlocal own
                    if s == 4:
                        act.wait_ge(xT_ready, c + 1)
                        for k in range(KD):
                            last = nc.scalar.copy(xnT[:, k, :], W[k][:])
                        last.then_inc(xnT_ready, 1)
                    elif s in (5, 6):
                        if s == 5:
                            own = Order(act, s_own, c * S_PRE + 2)
                            own.done(nc.scalar.copy(raw[:, :, 0:DC - 1], raw[:, :, CH:]))
                        for m in (0, 1) if s == 5 else (2, 3):
                            act.wait_ge(proj_ready, c * 2 * ND + m + 1)
                            nc.scalar.copy(raw[:, m, DC - 1:], W[m % 2][:]).then_inc(raw_ready, 1)
                    elif s in (7, 8):
                        wait_past(act, yg_ready, c - 1)
                        for m in (0, 1) if s == 7 else (2, 3):
                            act.wait_ge(proj_ready, c * 2 * ND + ND + m + 1)
                            nc.scalar.copy(zs[:, b, m, :], W[m % 2][:]).then_inc(z_copied, 1)
                        if s == 8:
                            act.wait_ge(conv_ready, c * ND + ND)
                            for m in range(ND):
                                last = nc.scalar.activation(xs[:, b, m, :], xs[:, b, m, :], ACT.Silu,
                                                            bias=conv_b[:, m:m + 1])
                            last.then_inc(xs_ready, 1)
                    elif s == 9:
                        act.wait_ge(xp_ready, c + 1)
                        nc.scalar.copy(dtr[SPLIT * BC:XP, :], W[0][SPLIT * BC:XP, :]).then_inc(dtr_ready, 1)
                    elif s == 10:
                        act.wait_ge(z_copied, c * ND + ND)
                        nc.scalar.activation(zs[:, b], zs[:, b], ACT.Silu).then_inc(z_ready, 1)
                    elif s in (11, 12):
                        for m in (0, 1) if s == 11 else (2, 3):
                            act.wait_ge(dtp_ready, c * ND + m + 1)
                            nc.scalar.activation(dt[:, b, m, :], W[(m + 1) % 2][:], ACT.Identity,
                                                 bias=dt_b[:, m:m + 1]).then_inc(v_ready, 1)
                    elif s == 13:
                        act.wait_ge(v_ready, c * ND + ND)
                        wait_past(act, dt_ready, c)
                        own.done(nc.scalar.activation(soft[:], dt[:, b], ACT.Abs))
                        own.done(nc.scalar.activation(soft[:], soft[:], ACT.Exp, scale=-1.0))
                    elif s == 14:
                        nc.scalar.activation(soft[:], soft[:], ACT.Ln, bias=1.0).then_inc(soft_ready, 1)
                        own.close(S_PRE)

                def decay(n, b):
                    for m in range(ND):
                        last = nc.scalar.activation(dA[:, SLOT[b][n], m, :], dt[:, b, m, :], ACT.Exp,
                                                    scale=a_neg[:, m, n:n + 1])
                    last.then_inc(dA_ready, 1)

                def begin(i, b):
                    if isinstance(i, int) and i == 0:
                        act.wait_ge(spread_ready, 1)
                    act.wait_ge(dt_ready, i + 1)
                    decay(0, b)

                def keep_end(n, i, b):
                    act.wait_ge(h_ready, i * DS + n + 1)
                    nc.scalar.copy(h_end[:, n, :], h[:, SLOT[b][n], :, CH - 1]).then_inc(h_kept, 1)

                def state(n, i, b):
                    if n >= 1:
                        keep_end(n - 1, i, b)
                    act.wait_ge(c_spread, i * DS + n + 1)
                    wait_past(act, g_ready, i * DS + n - lap(b, n) + 1)
                    nc.scalar.copy(crep[:, SLOT[b][n], :], C[:]).then_inc(crep_ready, 1)
                    if n + 1 < DS:
                        decay(n + 1, b)
                    if n == DS - 1:
                        keep_end(n, i, b)

                mamba_chunks(act, nothing, state, pre, nothing, begin)

            @block.vector
            def _(dve):
                dve.wait_ge(x_first, 16)
                own = None

                def pre(s, c, b):
                    nonlocal own
                    if s == 1:
                        own = Order(dve, v_pre, c * V_PRE)
                        for t in range(TPC):
                            last = nc.vector.bn_stats(stats[:, t, :], X[:, tok(c, t), :])
                        own.done(last)
                        nc.vector.memset(spare[:], 0.0)
                        for t in range(TPC):
                            last = nc.vector.bn_aggr(mv[:, t, :], stats[:, t, :])
                        own.done(last)
                        nc.vector.tensor_scalar(var[:], mv[:, :, 1], LN_EPS, None, ALU.add).then_inc(var_ready, 1)
                    elif s == 2:
                        dve.wait_ge(rstd_ready, c + 1)
                        for to, each in ((xn, lambda t: t), (X, lambda t: tok(c, t))):
                            for t in range(TPC):
                                last = nc.vector.tensor_scalar(to[:, each(t), :], X[:, tok(c, t), :], mv[:, t, 0:1],
                                                               rstd[:, t:t + 1], ALU.subtract, ALU.mult)
                            if to is xn:
                                last.then_inc(xn_ready, 1)
                    elif s == 3 and isinstance(c, int) and c == 0:
                        dve.wait_ge(conv_loaded, 16 * 5)
                    elif s == 8 and isinstance(c, int) and c == 0:
                        dve.wait_ge(w_ready, 16 * 4)
                        nc.vector.tensor_copy(spread[:].rearrange("p r c -> p (r c)"), spread_f).then_inc(spread_ready, 1)
                        dve.wait_ge(x_ready, 16 * 3)
                    elif s in (5, 6):
                        pair = (0, 1) if s == 5 else (2, 3)
                        for k in range(DC):
                            for m in pair:
                                if k == 0:
                                    dve.wait_ge(raw_ready, c * ND + m + 1)
                                    last = nc.vector.tensor_scalar(xs[:, b, m, :], raw[:, m, 0:CH], conv_w[:, m, 0:1],
                                                                   None, ALU.mult)
                                else:
                                    last = nc.vector.scalar_tensor_tensor(xs[:, b, m, :], raw[:, m, k:k + CH],
                                                                          conv_w[:, m, k:k + 1], xs[:, b, m, :],
                                                                          ALU.mult, ALU.add)
                                    if k == DC - 1:
                                        last.then_inc(conv_ready, 1)
                            if k < DC - 1:
                                own.done(last)
                    elif s == 9:
                        dve.wait_ge(xp_ready, c + 1)
                        dve.wait_ge(dtr_ready, c + 1)
                        own.done(nc.vector.tensor_copy(bc3[:, b], W[0][0:SPLIT * BC, :]))
                        own.done(nc.vector.tensor_tensor(rest[:], W[0][0:SPLIT * BC, :], bc3[:, b], ALU.subtract))
                        own.done(nc.vector.tensor_copy(mid[:], rest[:]))
                        nc.vector.tensor_copy(bc3[BC:2 * BC, b], mid[BC:2 * BC, :])
                        own.done(nc.vector.tensor_tensor(low[:], rest[:], mid[:], ALU.subtract))
                        nc.vector.tensor_copy(bc3[2 * BC:, b], low[2 * BC:, :]).then_inc(bc_ready, 1)
                        own.close(V_PRE)

                def begin(i, b):
                    dve.wait_ge(soft_ready, i + 1)
                    nc.vector.scalar_tensor_tensor(dt[:, b], dt[:, b], 0.0, soft[:],
                                                   ALU.max, ALU.add).then_inc(dt_ready, 1)
                    dve.wait_ge(dt_ready, i + 1)
                    dve.wait_ge(xs_ready, i + 1)
                    nc.vector.tensor_tensor(u[:], dt[:, b], xs[:, b], ALU.mult).then_inc(v_u, 1)
                    dve.wait_ge(v_u, i + 1)

                def state(n, i, b):
                    slot = SLOT[b][n]
                    dve.wait_ge(b_spread, i * DS + n + 1)
                    wait_past(dve, h_ready, i * DS + n)
                    nc.vector.tensor_tensor(dBx[:], u[:], B[:].rearrange("p (o t) -> p o t", o=1)
                                            .broadcast_to([P, ND, CH]), ALU.mult).then_inc(b_used, 1)
                    dve.wait_ge(b_used, i * DS + n + 1)
                    dve.wait_ge(dA_ready, i * DS + n + 1)
                    wait_past(dve, g_summed, i * DS + n - lap(b, n) + 1)
                    for m in range(ND):
                        last = nc.vector.tensor_tensor_scan(h[:, slot, m, :], dA[:, slot, m, :], dBx[:, m, :],
                                                            h_end[:, n, m:m + 1], ALU.mult, ALU.add)
                    last.then_inc(h_ready, 1)

                def post(s, i, b):
                    if s == 0:
                        dve.wait_ge(g_summed, i * DS + DS)
                        for m in range(ND):
                            last = nc.vector.scalar_tensor_tensor(xs[:, b, m, :], xs[:, b, m, :], skip_d[:, m:m + 1],
                                                                  Y[m][:], ALU.mult, ALU.add)
                        last.then_inc(y_read, 1)
                        dve.wait_ge(y_read, i + 1)
                        dve.wait_ge(z_ready, i + 1)
                        nc.vector.tensor_tensor(xs[:, b], xs[:, b], zs[:, b], ALU.mult).then_inc(yg_ready, 1)
                    elif s in (2, 3):
                        q = s - 2
                        dve.wait_ge(out_ready, i * 2 + q + 1)
                        rows = bass.ds(i * TPC + 2 * q, 2)
                        nc.vector.tensor_tensor(X[:, rows, :], X[:, rows, :], W[q][:].rearrange("p (t d) -> p t d", d=DM),
                                                ALU.add).then_inc(out_added, 1)

                mamba_chunks(dve, nothing, state, pre, post, begin)
                dve.wait_ge(out_added, NCH * 2)

            @block.tensor
            def _(pe):
                pe.wait_ge(w_first, 16 * 2)

                def into_work(c, m, half):
                    for k in range(KD):
                        last = nc.tensor.matmul(W[m % 2][:], w_in[:, k, (half * ND + m) * P:(half * ND + m + 1) * P],
                                                xnT[:, k, :], start=(k == 0), stop=(k == KD - 1))
                    last.then_inc(proj_ready, 1)

                def pre(s, c, b):
                    if s == 3:
                        pe.wait_ge(xn_ready, c + 1)
                        wait_past(pe, v_ready, c * ND)
                        for k in range(KD):
                            wait_past(pe, out_added, (c - 2) * 2 + k + 1)
                            for t in range(TPC):
                                last = nc.tensor.transpose(W[k][:, t * P:(t + 1) * P], xn[:, t, k * P:(k + 1) * P],
                                                           ident[:])
                        last.then_inc(xT_ready, 1)
                    elif s in (4, 5):
                        for m in (0, 1) if s == 4 else (2, 3):
                            if m == 0:
                                pe.wait_ge(xnT_ready, c + 1)
                            if m >= 2:
                                pe.wait_ge(raw_ready, c * ND + m - 1)
                            into_work(c, m, 0)
                    elif s in (6, 7):
                        for m in (0, 1) if s == 6 else (2, 3):
                            if m < 2:
                                pe.wait_ge(raw_ready, c * ND + m + 3)
                            else:
                                pe.wait_ge(z_copied, c * ND + m - 1)
                            into_work(c, m, 1)
                    elif s == 8:
                        pe.wait_ge(xs_ready, c + 1)
                        pe.wait_ge(w_ready, 16 * 4)
                        pe.wait_ge(z_copied, c * ND + ND - 1)
                        for m in range(ND):
                            last = nc.tensor.matmul(W[0][0:XP, :], w_xp[:, m, :], xs[:, b, m, :],
                                                    start=(m == 0), stop=(m == ND - 1))
                        last.then_inc(xp_ready, 1)
                    elif s in (10, 11):
                        for m in (0, 1) if s == 10 else (2, 3):
                            if m == 0:
                                pe.wait_ge(dtr_ready, c + 1)
                                pe.wait_ge(z_copied, c * ND + ND)
                            elif m == 1:
                                pe.wait_ge(bc_ready, c + 1)
                            else:
                                pe.wait_ge(v_ready, c * ND + m - 1)
                            nc.tensor.matmul(W[(m + 1) % 2][:], w_dt[SPLIT * BC:XP, m * P:(m + 1) * P],
                                             dtr[SPLIT * BC:XP, :], start=True, stop=True).then_inc(dtp_ready, 1)

                def spread_bc(n, c, b):
                    pe.wait_ge(bc_ready, c + 1)
                    wait_past(pe, b_used, c * DS + n)
                    nc.tensor.matmul(B[:], spread[:, n, :], bc3[:, b], start=True, stop=True).then_inc(b_spread, 1)
                    wait_past(pe, crep_ready, c * DS + n)
                    nc.tensor.matmul(C[:], spread[:, DS + n, :], bc3[:, b], start=True, stop=True).then_inc(c_spread, 1)

                def spread_first(c, b):
                    pe.wait_ge(spread_ready, 1)
                    spread_bc(0, c, b)

                def add_up(n, i, b):
                    pe.wait_ge(g_ready, i * DS + n + 1)
                    if n == 0:
                        wait_past(pe, y_read, i)
                    for m in range(ND):
                        last = nc.tensor.matmul(Y[m][:], ident[:], h[:, SLOT[b][n], m, :],
                                                start=(n == 0), stop=(n == DS - 1))
                    last.then_inc(g_summed, 1)

                def state(n, i, b):
                    late = (n - 1, i, b) if n else (DS - 1, i - 1, 1 - b)
                    summed = n > 0 or not isinstance(i, int) or i > 0
                    if n + 1 < DS:
                        spread_bc(n + 1, i, b)
                    if summed:
                        add_up(*late)

                def post(s, i, b):
                    if s == -1:
                        add_up(DS - 1, i, b)
                    elif s in (1, 2):
                        q = s - 1
                        pe.wait_ge(yg_ready, i + 1)
                        pe.wait_ge(v_ready, NCH * ND if isinstance(i, int) and i == NCH - 1 else (i + 2) * ND)
                        for t in (2 * q, 2 * q + 1):
                            for m in range(ND):
                                last = nc.tensor.matmul(W[q][:, t % 2 * DM:(t % 2 + 1) * DM],
                                                        xs[:, b, m, t * P:(t + 1) * P], w_out[:, m, :],
                                                        start=(m == 0), stop=(m == ND - 1))
                        last.then_inc(out_ready, 1)

                mamba_chunks(pe, spread_first, state, pre, post)


def staged(eng, stages):
    ahead = max(lead for lead, _ in stages)

    def step(s, at):
        for lead, run in stages:
            if not isinstance(s, int) or 0 <= s + lead < NCH:
                run(s + lead, (at + lead) % 2)

    for s in range(-ahead, 2):
        step(s, s)
    passes = (NCH - ahead - 2) // 2
    with eng.Fori(1, 1 + passes) as j:
        step(2 * j, 0)
        step(2 * j + 1, 1)
    for s in range(2 + 2 * passes, NCH):
        step(s, s)


def before(c, lag):
    return not isinstance(c, int) or c >= lag


class Norm:

    ORDERS = 2

    def __init__(self, nc, ctx, sem, name, eps):
        def sb(part, shape):
            return ctx.enter_context(nc.sbuf_tensor(f"{name}_{part}", shape, F32))

        self.nc, self.eps = nc, eps
        self.stats, self.mv = sb("stats", [P, TPC, 6]), sb("mv", [P, TPC, 2])
        self.var, self.rstd, self.spare = sb("var", [P, TPC]), sb("rstd", [P, TPC]), sb("spare", [P, 1])
        self.var_ready, self.rstd_ready = sem(f"{name}_var_ready"), sem(f"{name}_rstd_ready")

    def begin(self, own, src):
        for t in range(TPC):
            last = self.nc.vector.bn_stats(self.stats[:, t, :], src(t))
        own.done(last)
        self.nc.vector.memset(self.spare[:], 0.0)
        for t in range(TPC):
            last = self.nc.vector.bn_aggr(self.mv[:, t, :], self.stats[:, t, :])
        own.done(last)
        self.nc.vector.tensor_scalar(self.var[:], self.mv[:, :, 1], self.eps, None, ALU.add).then_inc(self.var_ready, 1)

    def power(self, pool, half, c):
        pool.wait_ge(self.var_ready, c + 1)
        self.nc.gpsimd.tensor_tensor(self.rstd[:], self.var[:], half[:], ALU.pow).then_inc(self.rstd_ready, 1)

    def scale(self, dve, c, out, src):
        dve.wait_ge(self.rstd_ready, c + 1)
        for t in range(TPC):
            last = self.nc.vector.tensor_scalar(out(t), src(t), self.mv[:, t, 0:1], self.rstd[:, t:t + 1],
                                                ALU.subtract, ALU.mult)
        return last


def weight_tiles(nc, ctx, name, shapes):
    return [(ctx.enter_context(nc.sbuf_tensor(f"{name}_{src}", shape, F32)), f"{name}_{src}")
            for src, shape in shapes]


def ffn_shapes(hidden):
    return [("w1", [P, KD, hidden]), ("w2", [P, hidden // P, DM]), ("b1", [P, hidden // P]), ("b2", [1, DM])]


def fetch(sp, a, tiles, fetched):
    for tile, src in tiles:
        sp.dma_start(tile[:], a[src]).then_inc(fetched, 16)


def feed_forward(nc, sem, X, ident, a, name, hidden, tail, own_tiles, next_tiles):
    NM = hidden // P
    with ExitStack() as ctx:
        def sb(part, shape, dt=F32):
            return ctx.enter_context(nc.sbuf_tensor(f"{name}_{part}", shape, dt))

        def sig(part):
            return sem(f"{name}_{part}")

        w1, w2, b1, b2 = (tile for tile, _ in own_tiles)
        ones = sb("ones", [P, P])
        half = sb("half", [P, TPC])
        n = sb("n", [P, 2, TPC, DM])
        if tail:
            hT = sb("hT", [P, 2, KD, CH])
            fT = sb("fT", [P, 2, NM, CH])
        else:
            w1_t, w2_t = sb("w1_t", [P, KD, hidden], F32R), sb("w2_t", [P, NM, DM], F32R)
            hT_part = {x: sb(f"hT_{x}", [P, 2, KD, CH], F32R) for x in ("high", "low")}
            fT = sb("fT", [P, NM, CH])
            fT_part = {x: sb(f"fT_{x}", [P, NM, CH], F32R) for x in ("high", "low")}
        f = sb("f", [P, 2, TPC, DM])
        norm_in = Norm(nc, ctx, sem, f"{name}_in", MAMBA_EPS if tail else LN_EPS)
        norm_out = Norm(nc, ctx, sem, f"{name}_out", LN_EPS)
        if tail:
            norm_mid = Norm(nc, ctx, sem, f"{name}_mid", MAMBA_EPS)
            in_w, in_b = sb("in_w", [P, KD]), sb("in_b", [P, KD])
            mid_w, mid_b = sb("mid_w", [P, 1, DM]), sb("mid_b", [P, 1, DM])
            x = sb("x", [P, 2, TPC, DM])
        else:
            gamma = sb("gamma", [P, 2])
            bound = sb("bound", [P, 2, 2])
            below = sb("below", [P, KD * hidden])
        bank = [ctx.enter_context(nc.psum_tensor(f"{name}_bank{b}", [P, CH], F32)) for b in range(8)]
        TB, FB, OB = 0, 2, 6

        w_ready, const_ready, q_ready = sig("w_ready"), sig("const_ready"), sig("q_ready")
        n_ready, nT_ready, hT_ready = sig("n_ready"), sig("nT_ready"), sig("hT_ready")
        up_ready, up_read, down_ready, f_ready = sig("up_ready"), sig("up_read"), sig("down_ready"), sig("f_ready")
        f_used, x_ready = sig("f_used"), [sig(f"x_ready{b}") for b in range(2)]
        mid_ready, mid_affine, mid_own = sig("mid_ready"), sig("mid_affine"), sig("mid_own")
        v_in, v_mid, v_out, setup_own = sig("v_in"), sig("v_mid"), sig("v_out"), sig("setup_own")
        abs_ready, sum_ready = sig("abs_ready"), sig("sum_ready")
        fetched = sig("fetched")
        loads = own_tiles + [(in_w, "tail_in_w"), (in_b, "tail_in_b"), (mid_w, "tail_mid_w"), (mid_b, "tail_mid_b")
                             ] if tail else []
        N_LOADS = 16 * len(loads)
        leaked, h_split, f_split = sig("leaked"), sig("h_split"), sig("f_split")
        IN, UP, DOWN, OUT = 3, 2, 1, 0

        with nc.Block() as block:
            @block.sync
            def _(sp):
                for dst, src in loads:
                    sp.dma_start(dst[:], a[src]).then_inc(w_ready, 16)
                fetch(sp, a, next_tiles, fetched)
                if tail:
                    def load(c, b):
                        if before(c, 2):
                            sp.wait_ge(f_used, c)
                        sp.dma_start(x[:, b], a["x_tiles"][bass.ds(c, 1)].rearrange("o (t p) d -> p (o t) d", p=P)
                                     ).then_inc(x_ready[b], 16)

                    staged(sp, [(0, load)])
                sp.wait_ge(fetched, 16 * len(next_tiles))

            @block.gpsimd
            def _(pool):
                nc.gpsimd.memset(half[:], -0.5).then_inc(const_ready, 1)
                nc.gpsimd.memset(ones[:], 1.0).then_inc(const_ready, 1)
                pool.wait_ge(const_ready, 2)
                wait_past(pool, w_ready, N_LOADS)

                def mid(c, b):
                    norm_mid.power(pool, half, c)
                    pool.wait_ge(mid_ready, c + 1)
                    nc.gpsimd.tensor_tensor(f[:, b], f[:, b], mid_w[:].broadcast_to([P, TPC, DM]),
                                            ALU.mult).then_inc(mid_own, 1)
                    pool.wait_ge(mid_own, c + 1)
                    nc.gpsimd.tensor_tensor(f[:, b], f[:, b], mid_b[:].broadcast_to([P, TPC, DM]),
                                            ALU.add).then_inc(mid_affine, 1)

                staged(pool, [(IN, lambda c, b: norm_in.power(pool, half, c)),
                              (OUT, lambda c, b: norm_out.power(pool, half, c))] + ([(DOWN, mid)] if tail else []))

            @block.scalar
            def _(act):
                wait_past(act, w_ready, N_LOADS)
                if not tail:
                    nc.scalar.activation(below[:], w1[:].rearrange("p k e -> p (k e)"), ACT.Abs,
                                         accum_out=gamma[:, 0:1]).then_inc(abs_ready, 1)
                    act.wait_ge(abs_ready, 1)
                    nc.scalar.activation(below[:], w2[:].rearrange("p k e -> p (k e)"), ACT.Abs,
                                         accum_out=gamma[:, 1:2]).then_inc(abs_ready, 1)

                def transposed(c, b):
                    act.wait_ge(nT_ready, c + 1)
                    if not tail and before(c, 2):
                        act.wait_ge(up_ready, (c - 1) * NM)
                    for k in range(KD):
                        if tail:
                            last = nc.scalar.activation(hT[:, b, k, :], bank[TB + k][:], ACT.Identity,
                                                        bias=in_b[:, k:k + 1], scale=in_w[:, k:k + 1])
                        else:
                            last = nc.scalar.copy(hT_part["high"][:, b, k, :], bank[TB + k][:])
                    last.then_inc(hT_ready, 1)

                def up(c, b):
                    if not tail:
                        act.wait_ge(down_ready, c * TPC)
                        act.wait_ge(f_split, c * NM)
                    for m in range(NM):
                        act.wait_ge(up_ready, c * NM + m + 1)
                        if tail:
                            last = nc.scalar.activation(fT[:, b, m, :], bank[FB + m % 4][:], ACT.Identity,
                                                        bias=b1[:, m:m + 1])
                        else:
                            for to in (fT, fT_part["high"]):
                                last = nc.scalar.activation(to[:, m, :], bank[FB + m % 4][:], ACT.Relu,
                                                            bias=b1[:, m:m + 1])
                        last.then_inc(up_read, 1)

                def down(c, b):
                    act.wait_ge(f_used, c)
                    for t in range(TPC):
                        act.wait_ge(down_ready, c * TPC + t + 1)
                        nc.scalar.copy(f[:, b, t, :], bank[OB + t % 2][:, 0:DM]).then_inc(f_ready, 1)

                staged(act, [(UP, transposed), (DOWN, down), (UP, up)])

            @block.vector
            def _(dve):
                nc.vector.memset(norm_out.stats[:], 0.0).then_inc(f_used, 1)
                wait_past(dve, w_ready, N_LOADS)
                if not tail:
                    setup = Order(dve, setup_own)
                    dve.wait_ge(sum_ready, 1)
                    setup.done(nc.vector.tensor_scalar(bound[:, 0, :], bank[TB][:, 0:2], 0.5 / (hidden * DM),
                                                       0.5 * LN_EPS, ALU.mult, ALU.add))
                    setup.done(nc.vector.tensor_scalar(bound[:, 1, :], bound[:, 0, :], -1.0, None, ALU.mult))
                    for q, (w, ternary) in enumerate(((w1, w1_t), (w2, w2_t))):
                        flat = w[:].rearrange("p k e -> p (k e)")
                        setup.done(nc.vector.tensor_scalar(below[:], flat, bound[:, 1, q:q + 1], None, ALU.is_lt))
                        last = nc.vector.scalar_tensor_tensor(ternary[:].rearrange("p k e -> p (k e)"), flat,
                                                              bound[:, 0, q:q + 1], below[:], ALU.is_gt, ALU.subtract)
                        setup.done(last)
                    nc.vector.tensor_scalar(bound[:, 1, :], bound[:, 0, :], -1.0, None, ALU.mult).then_inc(q_ready, 1)

                def in_begin(c, b):
                    norm_in.begin(Order(dve, v_in, c * Norm.ORDERS), lambda t: X[:, tok(c, t), :])

                def in_scale(c, b):
                    if before(c, 2):
                        dve.wait_ge(nT_ready, c - 1)
                    norm_in.scale(dve, c, lambda t: n[:, b, t, :], lambda t: X[:, tok(c, t), :]).then_inc(n_ready, 1)

                def mid_begin(c, b):
                    dve.wait_ge(f_ready, c * TPC + TPC)
                    norm_mid.begin(Order(dve, v_mid, c * Norm.ORDERS), lambda t: f[:, b, t, :])

                def mid_scale(c, b):
                    norm_mid.scale(dve, c, lambda t: f[:, b, t, :], lambda t: f[:, b, t, :]).then_inc(mid_ready, 1)

                def out_begin(c, b):
                    if tail:
                        dve.wait_ge(mid_affine, c + 1)
                    else:
                        dve.wait_ge(f_ready, c * TPC + TPC)
                    norm_out.begin(Order(dve, v_out, c * (Norm.ORDERS + 1)), lambda t: f[:, b, t, :])

                def out_scale(c, b):
                    own = Order(dve, v_out, c * (Norm.ORDERS + 1) + Norm.ORDERS)
                    own.done(norm_out.scale(dve, c, lambda t: f[:, b, t, :], lambda t: f[:, b, t, :]))
                    if tail:
                        dve.wait_ge(x_ready[b], (c - b) * 8 + 16)
                    for t in range(TPC):
                        last = nc.vector.tensor_tensor(X[:, tok(c, t), :], x[:, b, t, :] if tail else X[:, tok(c, t), :],
                                                       f[:, b, t, :], ALU.add)
                    last.then_inc(f_used, 1)

                def leak(c, b):
                    for m in range(NM):
                        dve.wait_ge(up_read, c * NM + m + 1)
                        nc.vector.scalar_tensor_tensor(fT[:, b, m, :], fT[:, b, m, :], 0.01, fT[:, b, m, :],
                                                       ALU.mult, ALU.max).then_inc(leaked, 1)

                def low_h(c, b):
                    dve.wait_ge(hT_ready, c + 1)
                    for k in range(KD):
                        last = nc.vector.tensor_tensor(hT_part["low"][:, b, k, :], bank[TB + k][:],
                                                       hT_part["high"][:, b, k, :].bitcast(F32), ALU.subtract)
                    last.then_inc(h_split, 1)

                def low_f(c, b):
                    dve.wait_ge(down_ready, c * TPC)
                    for m in range(NM):
                        dve.wait_ge(up_read, c * NM + m + 1)
                        nc.vector.tensor_tensor(fT_part["low"][:, m, :], fT[:, m, :],
                                                fT_part["high"][:, m, :].bitcast(F32), ALU.subtract).then_inc(f_split, 1)

                if tail:
                    staged(dve, [(IN, in_begin), (OUT, out_begin), (IN, in_scale), (OUT, out_scale),
                                 (DOWN, mid_begin), (UP, leak), (DOWN, mid_scale)])
                else:
                    staged(dve, [(IN, in_begin), (OUT, out_begin), (UP, low_h), (IN, in_scale), (OUT, out_scale),
                                 (UP, low_f)])

            @block.tensor
            def _(pe):
                wait_past(pe, w_ready, N_LOADS)
                pe.wait_ge(const_ready, 2)
                if not tail:
                    pe.wait_ge(abs_ready, 2)
                    nc.tensor.matmul(bank[TB][:, 0:2], ones[:], gamma[:], start=True, stop=True).then_inc(sum_ready, 1)
                    pe.wait_ge(q_ready, 1)

                def transposes(c, b):
                    pe.wait_ge(n_ready, c + 1)
                    pe.wait_ge(hT_ready if tail else h_split, c)
                    for t in range(TPC):
                        for k in range(KD):
                            last = nc.tensor.transpose(bank[TB + k][:, t * P:(t + 1) * P], n[:, b, t, k * P:(k + 1) * P],
                                                       ident[:])
                    last.then_inc(nT_ready, 1)

                def up(c, b):
                    pe.wait_ge(hT_ready if tail else h_split, c + 1)
                    for m in range(NM):
                        pe.wait_ge(up_read, c * NM + max(0, m - 3))
                        out, cols = bank[FB + m % 4], slice(m * P, (m + 1) * P)
                        if tail:
                            for k in range(KD):
                                last = nc.tensor.matmul(out[:], w1[:, k, cols], hT[:, b, k, :],
                                                        start=(k == 0), stop=(k == KD - 1))
                        else:
                            for k in range(KD):
                                nc.tensor.matmul(out[:], w1_t[:, k, cols], hT_part["low"][:, b, k, :],
                                                 start=(k == 0), stop=False)
                                last = nc.tensor.matmul(out[:], w1_t[:, k, cols], hT_part["high"][:, b, k, :],
                                                        start=False, stop=(k == KD - 1))
                        last.then_inc(up_ready, 1)

                def down(c, b):
                    pe.wait_ge(leaked if tail else f_split, c * NM + NM)
                    for t in range(TPC):
                        pe.wait_ge(f_ready, c * TPC + max(0, t - 1))
                        out = bank[OB + t % 2]
                        for m in range(NM):
                            if tail:
                                nc.tensor.matmul(out[:, 0:DM], fT[:, b, m, t * P:(t + 1) * P], w2[:, m, :],
                                                 start=(m == 0), stop=False)
                            else:
                                for x in ("low", "high"):
                                    nc.tensor.matmul(out[:, 0:DM], fT_part[x][:, m, t * P:(t + 1) * P], w2_t[:, m, :],
                                                     start=(m == 0 and x == "low"), stop=False)
                        if tail:
                            for k in range(KD):
                                nc.tensor.matmul(out[:, k * P:(k + 1) * P], hT[:, b, k, t * P:(t + 1) * P], ident[:],
                                                 start=False, stop=False)
                        nc.tensor.matmul(out[:, 0:DM], ones[0:1, :], b2[:], start=False,
                                         stop=True).then_inc(down_ready, 1)

                staged(pe, [(UP, transposes), (DOWN, down), (UP, up)])


PROJECT_SHAPES = [("w", [P, KD, 3 * DM]), ("qk_b", [P, 2, KD]), ("v_b", [1, DM])]
H = 16
HD = DM // H
SLOTS = ((0, 0), (0, 1), (1, 0), (1, 1), (0, 2), (2, 0))
QK_ROWS = len(SLOTS) * HD
ROWS = QK_ROWS + SPLIT
QS = 1.0 / 64
KC = CH
NKC = T // KC
RING = 12
NS = 4
NB = 2

TAIL = 4
QUAD = TPC
VW = 32


def project(nc, sem, X, V, ident, own_tiles, parts_dram):
    with ExitStack() as ctx:
        def sb(part, shape, dt=F32):
            return ctx.enter_context(nc.sbuf_tensor(f"p_{part}", shape, dt))

        def sig(part):
            return sem(f"p_{part}")

        w, qk_b, v_b = (tile for tile, _ in own_tiles)
        ones, half = sb("ones", [1, P]), sb("half", [P, TPC])
        n = sb("n", [P, 2, TPC, DM])
        nT = sb("nT", [P, 2, KD, CH])
        full = sb("full", [P, 2, 2, KD, CH])
        parts = sb("parts", [P, 2, 2, SPLIT, KD, CH], BF16)
        norm = Norm(nc, ctx, sem, "p_norm", LN_EPS)
        bank = [ctx.enter_context(nc.psum_tensor(f"p_bank{b}", [P, CH], F32)) for b in range(8)]
        TB, QB, VB = 0, 2, 6

        const_ready, bias_ready = sig("const_ready"), sig("bias_ready")
        n_ready, nT_ps, nT_ready = sig("n_ready"), sig("nT_ps"), sig("nT_ready")
        qk_ps, full_ready, v_ps, v_ready = sig("qk_ps"), sig("full_ready"), sig("v_ps"), sig("v_ready")
        split_ready, norm_own, split_own = sig("split_ready"), sig("norm_own"), sig("split_own")
        stored = [sig(f"stored{b}") for b in range(2)]
        STORES = 16 * 2 * SPLIT
        SPLITS = 3

        with nc.Block() as block:
            @block.sync
            def _(sp):
                def store(c, b):
                    for x in range(2):
                        sp.wait_ge(split_ready, 2 * c + x + 1)
                        for s in range(SPLIT):
                            sp.dma_start(parts_dram[x, s, :, :, bass.ds(c * CH, CH)].rearrange("m p t -> p m t"),
                                         parts[:, b, x, s]).then_inc(stored[b], 16)

                staged(sp, [(0, store), (1, lambda c, b: None)])
                for b in range(2):
                    sp.wait_ge(stored[b], NCH // 2 * STORES)

            @block.gpsimd
            def _(pool):
                nc.gpsimd.memset(half[:], -0.5).then_inc(const_ready, 1)
                nc.gpsimd.memset(ones[:], 1.0).then_inc(const_ready, 1)
                pool.wait_ge(const_ready, 2)
                staged(pool, [(2, lambda c, b: norm.power(pool, half, c))])

            @block.scalar
            def _(act):
                nc.scalar.mul(qk_b[:, 0, :], qk_b[:, 0, :], QS).then_inc(bias_ready, 1)
                act.wait_ge(bias_ready, 1)

                def transposed(c, b):
                    act.wait_ge(nT_ps, c + 1)
                    for k in range(KD):
                        last = nc.scalar.copy(nT[:, b, k, :], bank[TB + k][:])
                    last.then_inc(nT_ready, 1)

                def projected(c, b):
                    if before(c, 2):
                        act.wait_ge(split_ready, 2 * c - 2)
                    for x in range(2):
                        for m in range(KD):
                            act.wait_ge(qk_ps, c * 2 * KD + x * KD + m + 1)
                            nc.scalar.activation(full[:, b, x, m, :], bank[QB + x * KD + m][:], ACT.Identity,
                                                 bias=qk_b[:, x, m:m + 1],
                                                 scale=QS if x == 0 else 1.0).then_inc(full_ready, 1)
                    for t in range(TPC):
                        act.wait_ge(v_ps, c * TPC + t + 1)
                        nc.scalar.copy(V[:, tok(c, t), :], bank[VB + t % 2][:, 0:DM]).then_inc(v_ready, 1)

                staged(act, [(1, transposed), (0, projected)])

            @block.vector
            def _(dve):
                def normed(c, b):
                    own = Order(dve, norm_own, c * Norm.ORDERS)
                    norm.begin(own, lambda t: X[:, tok(c, t), :])
                    if before(c, 2):
                        dve.wait_ge(nT_ps, c - 1)
                    norm.scale(dve, c, lambda t: n[:, b, t, :], lambda t: X[:, tok(c, t), :]).then_inc(n_ready, 1)

                def split(c, b):
                    own = Order(dve, split_own, c * 2 * SPLITS)
                    if before(c, 2):
                        dve.wait_ge(stored[b], (c - b) * (STORES // 2))
                    for x in range(2):
                        f = full[:, b, x]
                        dve.wait_ge(full_ready, c * 2 * KD + x * KD + KD)
                        own.done(nc.vector.tensor_copy(parts[:, b, x, 0], f))
                        own.done(nc.vector.tensor_tensor(f, f, parts[:, b, x, 0], ALU.subtract))
                        own.done(nc.vector.tensor_copy(parts[:, b, x, 1], f))
                        nc.vector.tensor_tensor(parts[:, b, x, 2], f, parts[:, b, x, 1],
                                                ALU.subtract).then_inc(split_ready, 1)
                    own.close(2 * SPLITS)

                staged(dve, [(2, normed), (0, split)])

            @block.tensor
            def _(pe):
                pe.wait_ge(const_ready, 2)

                def transposes(c, b):
                    pe.wait_ge(n_ready, c + 1)
                    pe.wait_ge(nT_ready, c)
                    for t in range(TPC):
                        for k in range(KD):
                            last = nc.tensor.transpose(bank[TB + k][:, t * P:(t + 1) * P], n[:, b, t, k * P:(k + 1) * P],
                                                       ident[:])
                    last.then_inc(nT_ps, 1)

                def projections(c, b):
                    pe.wait_ge(nT_ready, c + 1)
                    for x in range(2):
                        pe.wait_ge(full_ready, c * 2 * KD)
                        for m in range(KD):
                            for k in range(KD):
                                last = nc.tensor.matmul(bank[QB + x * KD + m][:],
                                                        w[:, k, x * DM + m * P:x * DM + (m + 1) * P], nT[:, b, k, :],
                                                        start=(k == 0), stop=(k == KD - 1))
                            last.then_inc(qk_ps, 1)
                    for t in range(TPC):
                        pe.wait_ge(v_ready, c * TPC + max(0, t - 1))
                        out = bank[VB + t % 2][:, 0:DM]
                        for k in range(KD):
                            nc.tensor.matmul(out, nT[:, b, k, t * P:(t + 1) * P], w[:, k, 2 * DM:3 * DM],
                                             start=(k == 0), stop=False)
                        nc.tensor.matmul(out, ones[:], v_b[:], start=False, stop=True).then_inc(v_ps, 1)

                staged(pe, [(1, transposes), (0, projections)])


def group_blocks(g):
    return [(kb, None) for kb in range(TPC * (g + 1), NT)] + [(TPC * g + r, r) for r in range(TPC)]


BLOCKS = [(g, kb, r) for g in range(NCH) for kb, r in group_blocks(g)]
UNITS = [(i, c) for i in range(NT) for c in range(NKC)]


def low_width(i, c):
    return max(0, min(KC, P * (i + 1) - KC * c))


def lows_upto(u):
    return sum(low_width(*UNITS[n]) > 0 for n in range(u + 1)) if u >= 0 else u + 1


def head_order():
    G0, G1 = [(0, g) for g in range(NCH)], [(1, g) for g in range(NCH)]
    rows = G1[-1:] + G0[:-1]
    turns = G1[-TAIL:] + G0[:-TAIL]
    blocks = [(p, j) for p, g in turns for j, b in enumerate(BLOCKS) if b[0] == g]
    quads = [(p, j // QUAD) for p, j in blocks[::QUAD]]
    units = [(0, u) for u in range(len(UNITS))]
    items = {"unit": units, "max": units, "low": [u for u in units if low_width(*UNITS[u[1]])],
             "negate": G0, "weight": G0, "row": rows, "rowcopy": rows, "block": blocks, "exp": blocks,
             "value": quads, "zcopy": turns, "turn": turns, "zout": turns}
    kinds = {"pe": ("unit", "row", "turn", "block", "value"), "act": ("low", "weight", "exp"),
             "dve": ("negate", "rowcopy", "zcopy", "zout", "max")}
    latency = {"pe": 300, "act": 100, "dve": 150}
    length = {"unit": 216, "max": 598, "negate": 1300, "weight": 300, "row": 250, "rowcopy": 600, "value": 940,
              "zcopy": 600, "turn": 300, "zout": 1200}

    def width(j):
        return CH if BLOCKS[j][2] is None else (BLOCKS[j][2] + 1) * P

    def long(kind, x):
        if kind == "low":
            return 240 + 0.833 * low_width(*UNITS[x])
        if kind in ("block", "exp"):
            return width(x) * 0.42 if kind == "block" else 50 + 0.833 * width(x)
        return length[kind]

    index = {kind: {x: n for n, x in enumerate(xs)} for kind, xs in items.items()}
    finish = {kind: [] for kind in items}

    def at(kind, p, x, back=0):
        n = index[kind].get((p, x), 0 if kind == "low" or back else -1)
        if (p, x) not in index[kind] or n - back < 0:
            return 0
        return finish[kind][n - back] if n - back < len(finish[kind]) else None

    def lows_last(g):
        return max(u for u in range((g + 1) * TPC * NKC) if low_width(*UNITS[u]))

    def needs(kind, p, x):
        if kind == "unit":
            v = x - NS
            return [at("low" if low_width(*UNITS[v]) else "max", p, v)] if v >= 0 else []
        if kind == "max":
            return [at("unit", p, x)]
        if kind == "low":
            return [at("max", p, x)]
        if kind == "negate":
            return [at("max", p, (x + 1) * TPC * NKC - 1), at("weight", p, x - 1), at("rowcopy", p, x - 1)]
        if kind == "weight":
            return [at("negate", p, x)]
        if kind == "row":
            return [at("negate", p, x)]
        if kind == "rowcopy":
            return [at("row", p, x)]
        if kind == "block":
            return [at("rowcopy", p, BLOCKS[x][0]), at("exp", p, x, NB)]
        if kind == "exp":
            back = index["exp"][(p, x)] - RING
            return [at("block", p, x), at("value", *quads[back // QUAD]) if back >= 0 else 0]
        if kind == "value":
            g = BLOCKS[x * QUAD][0]
            free = at("zout", p, g - 1) if g else at("zout", 1, NCH - 1)
            return [at("exp", p, x * QUAD + QUAD - 1), free]
        if kind == "zcopy":
            return [at("value", p, len([b for b in BLOCKS if b[0] <= x]) // QUAD - 1)]
        if kind == "turn":
            return [at("zcopy", p, x)]
        if kind == "zout":
            return [at("turn", p, x), at("low", p, lows_last(x)) if p == 0 else 0,
                    at("weight", p, x)]

    free, order = dict.fromkeys(kinds, 0), []
    while True:
        first = None
        for eng, own in kinds.items():
            for rank, kind in enumerate(own):
                if len(finish[kind]) == len(items[kind]):
                    continue
                p, x = items[kind][len(finish[kind])]
                ready = needs(kind, p, x)
                if None not in ready and (first is None or (max([free[eng], *ready]), rank) < first[:2]):
                    first = (max([free[eng], *ready]), rank, eng, kind, p, x)
        if first is None:
            return order
        start, _, eng, kind, p, x = first
        free[eng] = start + long(kind, x)
        finish[kind].append(free[eng] + latency[eng])
        order.append((kind, p, x))


def attend(nc, sem, V, ident, a, parts_dram, z_dram):
    with ExitStack() as ctx:
        def sb(part, shape, dt=F32):
            return ctx.enter_context(nc.sbuf_tensor(f"a_{part}", shape, dt))

        def sig(part):
            return sem(f"a_{part}")

        q = sb("q", [ROWS, 2, T], BF16)
        k = sb("k", [ROWS, 2, T], BF16)
        vh = sb("vh", [P, 2, NT, VW])
        sel = sb("sel", [P, VW])
        identb = sb("identb", [P, P], BF16)
        prob = sb("prob", [P, RING, CH])
        zeros = sb("zeros", [P, CH])
        keep = sb("keep", [P, P])
        neg_c = sb("neg_c", [P, 2, NT, NKC])
        sums_c = sb("sums_c", [P, 2, NT, NKC])
        neg = sb("neg", [P, TPC])
        neg_rest = sb("neg_rest", [P, TPC])
        neg3 = sb("neg3", [P, TPC, ROWS], BF16)
        lift = sb("lift", [P, TPC, NKC])
        weight = sb("weight", [P, 2, NCH, TPC, NKC])
        part_l = sb("part_l", [P, TPC, NKC])
        total = sb("total", [P, TPC])
        zT = sb("zT", [P, CH])
        z = sb("z", [P, 2, NT, HD])
        S = [ctx.enter_context(nc.psum_tensor(f"a_S{b}", [P, KC], F32)) for b in range(NS)]
        B = [ctx.enter_context(nc.psum_tensor(f"a_B{b}", [P, CH], F32)) for b in range(NB)]
        zacc = ctx.enter_context(nc.psum_tensor("a_zacc", [P, CH], F32))
        row_ps = ctx.enter_context(nc.psum_tensor("a_row", [P, CH], F32))

        const_ready, const_loaded, identb_ready, pool_own, vh_ready = (
            sig("const_ready"), sig("const_loaded"), sig("identb_ready"), sig("pool_own"), sig("vh_ready"))
        loaded = [sig(f"loaded{b}") for b in range(2)]
        z_stored = [sig(f"z_stored{b}") for b in range(2)]
        scored, unit_max, low_summed = sig("scored"), sig("unit_max"), sig("low_summed")
        neg_ready, neg_T, row_ready, weight_ready = sig("neg_ready"), sig("neg_T"), sig("row_ready"), sig("weight_ready")
        block_scored, prob_ready, masked, valued = sig("block_scored"), sig("prob_ready"), sig("masked"), sig("valued")
        z_copied, z_T, z_out, own_sem = sig("z_copied"), sig("z_T"), sig("z_out"), sig("own")

        order = head_order()
        assert all(len(s) % n == 0 for s, n in ((UNITS, NS), (BLOCKS, NB), (BLOCKS, RING)))
        NU, NBL, NQ = len(UNITS), len(BLOCKS), len(BLOCKS) // QUAD
        LOWS = lows_upto(NU - 1)
        NEGATE, ZOUT = 4, 4
        OWN = NCH * (NEGATE + ZOUT)
        OWN_FIRST = OWN - TAIL * ZOUT
        LOADS = 16 * 2 * len(SLOTS)
        for s in (unit_max, low_summed, z_out, prob_ready, valued, z_copied, weight_ready, z_T, *z_stored):
            nc.sync.sem_inc(s, FREE)

        def upto(h, per_head, n):
            return FREE + (max(0, h * per_head + n) if isinstance(h, int) else h * per_head + n)

        def blocks_upto(g):
            return sum(b[0] <= g for b in BLOCKS)

        def every_pass(run):
            def one_pass(h, b, parts=(0, 1)):
                for kind, p, x in order:
                    if p in parts:
                        run(kind, h - p, b ^ p, x)

            def both(eng, begin=lambda h, b: None):
                begin(0, 0)
                one_pass(0, 0, (0,))
                with eng.Fori(0, H // 2 - 1) as j:
                    for b in (1, 0):
                        begin(2 * j + 2 - b, b)
                        one_pass(2 * j + 2 - b, b)
                begin(H - 1, 1)
                one_pass(H - 1, 1)
                one_pass(H, 0, (1,))

            return both

        with nc.Block() as block:
            @block.sync
            def _(sp):
                sp.dma_start(sel[:], a["sel"]).then_inc(const_loaded, 16)

                def load(h, b):
                    for s, (pq, pk) in enumerate(SLOTS):
                        for dst, x, part in ((q, 0, pq), (k, 1, pk)):
                            src = parts_dram[x, part].rearrange("m p t -> (m p) t")
                            sp.dma_start(dst[s * HD:(s + 1) * HD, b, :], src[bass.ds(h * HD, HD), :]
                                         ).then_inc(loaded[b], 16)

                load(0, 0)
                load(1, 1)

                def store(h, b):
                    sp.wait_ge(z_out, FREE + (h + 1) * NCH)
                    sp.dma_start(z_dram[bass.ds(h, 1)].rearrange("o (i p) d -> p (o i) d", p=P),
                                 z[:, b]).then_inc(z_stored[b], 16)

                with sp.Fori(0, H // 2 - 1) as j:
                    for b in range(2):
                        h = 2 * j + b
                        sp.wait_ge(valued, FREE + (h + 1) * NQ)
                        load(h + 2, b)
                        store(h, b)
                store(H - 2, 0)
                store(H - 1, 1)
                for b in range(2):
                    sp.wait_ge(z_stored[b], FREE + H // 2 * 16)

            @block.gpsimd
            def _(pool):
                own = Order(pool, pool_own)
                for tile, value in ((vh[:], 0.0), (k[QK_ROWS:, :, :], 1.0), (zeros[:], 0.0), (neg3[:], 0.0),
                                    (sums_c[:], 0.0), (neg_c[:], 0.0)):
                    own.done(nc.gpsimd.memset(tile, value))
                own.done(nc.gpsimd.memset(keep[:], 1.0))
                own.done(nc.gpsimd.affine_select(out=keep[:], in_=keep[:], pattern=[[-1, P]], compare_op=ALU.is_ge,
                                                 fill=0.0, base=0, channel_multiplier=1))
                nc.gpsimd.memset(vh[:, :, :, HD:HD + 1], 1.0).then_inc(const_ready, 1)
                pool.wait_ge(const_ready, 1)

                def head(h, b, first=False):
                    if not first:
                        pool.wait_ge(valued, FREE + (h - 1) * NQ)
                    nc.gpsimd.tensor_copy(vh[:, b, :, 0:HD], V[:, :, bass.ds(h * HD, HD)]).then_inc(vh_ready, 1)
                    for j, (g, kb, r) in enumerate(BLOCKS):
                        if r is not None:
                            pool.wait_ge(prob_ready, FREE + h * NBL + j + 1)
                            blk = prob[:, j % RING, r * P:(r + 1) * P]
                            nc.gpsimd.tensor_tensor(blk, blk, keep[:], ALU.mult).then_inc(masked, 1)

                head(0, 0, True)
                head(1, 1, True)
                with pool.Fori(1, H // 2) as pair:
                    head(2 * pair, 0)
                    head(2 * pair + 1, 1)

            @block.scalar
            def _(act):
                act.wait_ge(const_ready, 1)

                def run(kind, h, b, x):
                    if kind == "low":
                        i, c = UNITS[x]
                        w = low_width(i, c)
                        act.wait_ge(unit_max, FREE + h * NU + x + 1)
                        nc.scalar.activation(S[x % NS][:, 0:w], S[x % NS][:, 0:w], ACT.Exp, bias=neg_c[:, b, i, c:c + 1],
                                             accum_out=sums_c[:, b, i, c:c + 1]).then_inc(low_summed, 1)
                    elif kind == "weight":
                        act.wait_ge(neg_ready, h * NCH + x + 1)
                        nc.scalar.activation(weight[:, b, x], lift[:], ACT.Exp).then_inc(weight_ready, 1)
                    elif kind == "exp":
                        g, kb, r = BLOCKS[x]
                        w = CH if r is None else (r + 1) * P
                        act.wait_ge(block_scored, h * NBL + x + 1)
                        act.wait_ge(valued, upto(h, NQ, (x - RING) // QUAD + 1))
                        nc.scalar.activation(prob[:, x % RING, 0:w], B[x % NB][:, 0:w], ACT.Exp).then_inc(prob_ready, 1)

                every_pass(run)(act)

            @block.vector
            def _(dve):
                dve.wait_ge(const_ready, 1)
                nc.vector.tensor_copy(identb[:], ident[:]).then_inc(identb_ready, 1)
                own = None

                def begin(h, b):
                    nonlocal own
                    own = Order(dve, own_sem, (h - 1) * OWN + OWN_FIRST if not isinstance(h, int) or h else 0)

                def run(kind, h, b, x):
                    if kind == "max":
                        i, c = UNITS[x]
                        dve.wait_ge(scored, h * NU + x + 1)
                        nc.vector.tensor_reduce(neg_c[:, b, i, c:c + 1], S[x % NS][:], AX.X, ALU.max,
                                                negate=True).then_inc(unit_max, 1)
                        return
                    rows = slice(x * TPC, (x + 1) * TPC)
                    if kind == "negate":
                        units = neg_c[:, b, rows, :]
                        dve.wait_ge(unit_max, FREE + h * NU + (x + 1) * TPC * NKC)
                        own.done(nc.vector.tensor_reduce(neg[:], units, AX.X, ALU.min))
                        dve.wait_ge(weight_ready, FREE + h * NCH + x)
                        nc.vector.tensor_tensor(lift[:], neg[:].rearrange("p (t o) -> p t o", o=1)
                                                .broadcast_to([P, TPC, NKC]), units, ALU.subtract)
                        own.done(nc.vector.tensor_copy(neg3[:, :, QK_ROWS], neg[:]))
                        own.done(nc.vector.tensor_tensor(neg_rest[:], neg[:], neg3[:, :, QK_ROWS], ALU.subtract))
                        own.done(nc.vector.tensor_copy(neg3[:, :, QK_ROWS + 1], neg_rest[:]))
                        nc.vector.tensor_tensor(neg3[:, :, QK_ROWS + 2], neg_rest[:], neg3[:, :, QK_ROWS + 1],
                                                ALU.subtract).then_inc(neg_ready, 1)
                    elif kind == "rowcopy":
                        dve.wait_ge(neg_T, h * NCH + x + 1)
                        nc.vector.tensor_copy(q[QK_ROWS:, b, x * CH:(x + 1) * CH],
                                              row_ps[QK_ROWS:ROWS, :]).then_inc(row_ready, 1)
                    elif kind == "zcopy":
                        dve.wait_ge(valued, FREE + h * NQ + blocks_upto(x) // QUAD)
                        dve.wait_ge(z_T, FREE + h * NCH + x)
                        nc.vector.tensor_copy(zT[:], zacc[:]).then_inc(z_copied, 1)
                    elif kind == "zout":
                        dve.wait_ge(low_summed, FREE + h * LOWS + lows_upto((x + 1) * TPC * NKC - 1))
                        dve.wait_ge(weight_ready, FREE + h * NCH + x + 1)
                        own.done(nc.vector.tensor_tensor(part_l[:], weight[:, b, x], sums_c[:, b, rows, :], ALU.mult))
                        own.done(nc.vector.tensor_reduce(total[:], part_l[:], AX.X, ALU.add))
                        dve.wait_ge(z_T, FREE + h * NCH + x + 1)
                        zt = zacc[:, 0:TPC * VW].rearrange("p (t v) -> p t v", v=VW)
                        own.done(nc.vector.tensor_tensor(total[:], total[:], zt[:, :, HD], ALU.add))
                        own.done(nc.vector.reciprocal(total[:], total[:]))
                        if x == 0:
                            dve.wait_ge(z_stored[b], FREE + (h - b) * 8)
                        nc.vector.tensor_tensor(z[:, b, rows, :], zt[:, :, 0:HD],
                                                total[:].rearrange("p (t o) -> p t o", o=1)
                                                .broadcast_to([P, TPC, HD]), ALU.mult).then_inc(z_out, 1)
                        dve.wait_ge(z_out, FREE + h * NCH + x + 1)

                every_pass(run)(dve, begin)

            @block.tensor
            def _(pe):
                pe.wait_ge(const_ready, 1)
                pe.wait_ge(const_loaded, 16)
                pe.wait_ge(identb_ready, 1)

                def begin(h, b):
                    pe.wait_ge(loaded[b], (h - b) * (LOADS // 2) + LOADS)

                def run(kind, h, b, x):
                    if kind == "unit":
                        i, c = UNITS[x]
                        pe.wait_ge(unit_max, upto(h, NU, x - NS + 1))
                        pe.wait_ge(low_summed, upto(h, LOWS, lows_upto(x - NS)))
                        nc.tensor.matmul(S[x % NS][:], q[0:QK_ROWS, b, i * P:(i + 1) * P],
                                         k[0:QK_ROWS, b, c * KC:(c + 1) * KC], start=True, stop=True).then_inc(scored, 1)
                    elif kind == "row":
                        pe.wait_ge(neg_ready, h * NCH + x + 1)
                        pe.wait_ge(row_ready, h * NCH + x)
                        for t in range(TPC):
                            last = nc.tensor.matmul(row_ps[0:ROWS, t * P:(t + 1) * P], neg3[:, t, :], identb[:],
                                                    start=True, stop=True)
                        last.then_inc(neg_T, 1)
                    elif kind == "block":
                        g, kb, r = BLOCKS[x]
                        w = CH if r is None else (r + 1) * P
                        pe.wait_ge(row_ready, h * NCH + g + 1)
                        pe.wait_ge(prob_ready, upto(h, NBL, x - NB + 1))
                        nc.tensor.matmul(B[x % NB][:, 0:w], k[:, b, kb * P:(kb + 1) * P],
                                         q[:, b, g * CH:g * CH + w], start=True, stop=True).then_inc(block_scored, 1)
                    elif kind == "value":
                        quad = [(j, *BLOCKS[j]) for j in range(x * QUAD, (x + 1) * QUAD)]
                        g, on_diagonal = quad[0][1], quad[0][3] is not None
                        if x * QUAD == blocks_upto(g - 1):
                            pe.wait_ge(z_out, FREE + h * NCH + g)
                            pe.wait_ge(vh_ready, h + 1)
                        if not on_diagonal:
                            pe.wait_ge(prob_ready, FREE + h * NBL + (x + 1) * QUAD)
                            for j, g, kb, r in quad:
                                col = kb % TPC * VW
                                last = nc.tensor.matmul(zacc[col:col + VW, :], vh[:, b, kb, :], prob[:, j % RING, :],
                                                        start=(kb < TPC * (g + 2)), stop=False)
                        else:
                            pe.wait_ge(masked, h * NT + TPC * (g + 1))
                            if g == NCH - 1:
                                for j, g, kb, r in quad:
                                    col = kb % TPC * VW
                                    nc.tensor.matmul(zacc[col:col + VW, :], vh[:, b, kb, :], zeros[:],
                                                     start=True, stop=False)
                            for j, g, kb, r in quad:
                                col = kb % TPC * VW
                                if r > 0:
                                    nc.tensor.matmul(zacc[col:col + VW, 0:r * P], vh[:, b, kb, :],
                                                     prob[:, j % RING, 0:r * P], start=False, stop=False)
                                last = nc.tensor.matmul(zacc[col:col + HD, r * P:(r + 1) * P], vh[:, b, kb, 0:HD],
                                                        prob[:, j % RING, r * P:(r + 1) * P], start=False, stop=True)
                        last.then_inc(valued, 1)
                    elif kind == "turn":
                        pe.wait_ge(z_copied, FREE + h * NCH + x + 1)
                        for t in range(TPC):
                            last = nc.tensor.matmul(zacc[:, t * VW:(t + 1) * VW], zT[:, t * P:(t + 1) * P], sel[:],
                                                    start=True, stop=True)
                        last.then_inc(z_T, 1)

                every_pass(run)(pe, begin)


def attention_out(nc, sem, X, a, z_dram):
    with ExitStack() as ctx:
        def sb(part, shape, dt=F32):
            return ctx.enter_context(nc.sbuf_tensor(f"o_{part}", shape, dt))

        def sig(part):
            return sem(f"o_{part}")

        gamma, beta, half = sb("gamma", [P, 1, DM]), sb("beta", [P, 1, DM]), sb("half", [P, TPC])
        e = sb("e", [P, 2, TPC, DM])
        f = sb("f", [P, 2, TPC, DM])
        z = sb("z", [P, 2, TPC, DM])
        z_tiles = z_dram.rearrange("h q d -> (h q d)").rearrange("(j p d) -> p j d", p=P, d=DM)
        z_ready = [sig(f"z_ready{b}") for b in range(2)]
        norm_in, norm_mid, norm_out = (Norm(nc, ctx, sem, f"o_{x}", LN_EPS) for x in ("in", "mid", "out"))
        w_ready, const_ready, x_done = sig("w_ready"), sig("const_ready"), sig("x_done")
        sum_ready, mid_ready, mid_own, mid_affine, v_in, v_mid, v_out = (
            sig("sum_ready"), sig("mid_ready"), sig("mid_own"), sig("mid_affine"), sig("v_in"), sig("v_mid"), sig("v_out"))
        IN, MID, OUT = 2, 1, 0

        with nc.Block() as block:
            @block.sync
            def _(sp):
                sp.dma_start(gamma[:], a["attn_gamma"]).then_inc(w_ready, 16)
                sp.dma_start(beta[:], a["attn_beta"]).then_inc(w_ready, 16)

                def load(c, b):
                    if before(c, 2):
                        sp.wait_ge(sum_ready, c - 1)
                    sp.dma_start(z[:, b], z_tiles[:, bass.ds(c * TPC, TPC), :]).then_inc(z_ready[b], 16)

                staged(sp, [(0, load)])

            @block.gpsimd
            def _(pool):
                nc.gpsimd.memset(half[:], -0.5).then_inc(const_ready, 1)
                pool.wait_ge(const_ready, 1)
                pool.wait_ge(w_ready, 32)

                def affine(c, b):
                    pool.wait_ge(mid_ready, c + 1)
                    nc.gpsimd.tensor_tensor(f[:, b], f[:, b], gamma[:].broadcast_to([P, TPC, DM]),
                                            ALU.mult).then_inc(mid_own, 1)
                    pool.wait_ge(mid_own, c + 1)
                    nc.gpsimd.tensor_tensor(f[:, b], f[:, b], beta[:].broadcast_to([P, TPC, DM]),
                                            ALU.add).then_inc(mid_affine, 1)

                staged(pool, [(IN, lambda c, b: norm_in.power(pool, half, c)),
                              (MID, lambda c, b: norm_mid.power(pool, half, c)),
                              (OUT, lambda c, b: norm_out.power(pool, half, c)), (MID, affine)])

            @block.vector
            def _(dve):
                IN_ORDERS, OUT_ORDERS = Norm.ORDERS + 1, Norm.ORDERS + 1

                def in_begin(c, b):
                    norm_in.begin(Order(dve, v_in, c * IN_ORDERS), lambda t: X[:, tok(c, t), :])

                def in_scale(c, b):
                    own = Order(dve, v_in, c * IN_ORDERS + Norm.ORDERS)
                    own.done(norm_in.scale(dve, c, lambda t: e[:, b, t, :], lambda t: X[:, tok(c, t), :]))
                    dve.wait_ge(z_ready[b], (c - b) * 8 + 16)
                    nc.vector.tensor_tensor(e[:, b], e[:, b], z[:, b], ALU.add).then_inc(sum_ready, 1)

                def mid_begin(c, b):
                    dve.wait_ge(sum_ready, c + 1)
                    norm_mid.begin(Order(dve, v_mid, c * Norm.ORDERS), lambda t: e[:, b, t, :])

                def mid_scale(c, b):
                    norm_mid.scale(dve, c, lambda t: f[:, b, t, :], lambda t: e[:, b, t, :]).then_inc(mid_ready, 1)

                def out_begin(c, b):
                    dve.wait_ge(mid_affine, c + 1)
                    norm_out.begin(Order(dve, v_out, c * OUT_ORDERS), lambda t: f[:, b, t, :])

                def out_scale(c, b):
                    own = Order(dve, v_out, c * OUT_ORDERS + Norm.ORDERS)
                    own.done(norm_out.scale(dve, c, lambda t: f[:, b, t, :], lambda t: f[:, b, t, :]))
                    for t in range(TPC):
                        last = nc.vector.tensor_tensor(X[:, tok(c, t), :], X[:, tok(c, t), :], f[:, b, t, :], ALU.add)
                    last.then_inc(x_done, 1)

                staged(dve, [(IN, in_begin), (MID, mid_begin), (IN, in_scale), (MID, mid_scale), (OUT, out_begin),
                             (OUT, out_scale)])
                dve.wait_ge(x_done, NCH)


NE = 16
NG = 4
GE = NE // NG
TOP_K = 4
TOP_G = 2
SCALE = 2.5
ME = 128
NX = NE + 2 * ME // ME


PRODUCTS = (("high", "high"), ("high", "low"), ("low", "high"))


def normed_transposed(nc, sem, X, nT, halves, ident, name):
    with ExitStack() as ctx:
        def sb(part, shape, dt=F32):
            return ctx.enter_context(nc.sbuf_tensor(f"{name}_{part}", shape, dt))

        def sig(part):
            return sem(f"{name}_{part}")

        half = sb("half", [P, TPC])
        n = sb("n", [P, 2, TPC, DM])
        norm = Norm(nc, ctx, sem, f"{name}_norm", LN_EPS)
        bank = [ctx.enter_context(nc.psum_tensor(f"{name}_bank{b}", [P, CH], F32)) for b in range(4)]
        const_ready, n_ready, nT_ps, nT_ready, low_ready, own_sem = (
            sig("const_ready"), sig("n_ready"), sig("nT_ps"), sig("nT_ready"), sig("low_ready"), sig("own"))

        with nc.Block() as block:
            @block.gpsimd
            def _(pool):
                nc.gpsimd.memset(half[:], -0.5).then_inc(const_ready, 1)
                pool.wait_ge(const_ready, 1)
                staged(pool, [(1, lambda c, b: norm.power(pool, half, c))])

            @block.vector
            def _(dve):
                def normed(c, b):
                    own = Order(dve, own_sem, c * Norm.ORDERS)
                    norm.begin(own, lambda t: X[:, tok(c, t), :])
                    if before(c, 2):
                        dve.wait_ge(nT_ps, c - 1)
                    norm.scale(dve, c, lambda t: n[:, b, t, :], lambda t: X[:, tok(c, t), :]).then_inc(n_ready, 1)

                def low(c, b):
                    dve.wait_ge(nT_ready, c + 1)
                    for k in range(KD):
                        cols = bass.ds(c * CH, CH)
                        last = nc.vector.tensor_tensor(halves["low"][:, k, cols], nT[:, k, cols],
                                                       halves["high"][:, k, cols].bitcast(F32), ALU.subtract)
                    last.then_inc(low_ready, 1)

                staged(dve, [(2, normed), (0, low)])
                dve.wait_ge(low_ready, NCH)

            @block.tensor
            def _(pe):
                def transposes(c, b):
                    pe.wait_ge(n_ready, c + 1)
                    if before(c, 2):
                        pe.wait_ge(nT_ready, c - 1)
                    for t in range(TPC):
                        for k in range(KD):
                            last = nc.tensor.transpose(bank[b * KD + k][:, t * P:(t + 1) * P],
                                                       n[:, b, t, k * P:(k + 1) * P], ident[:])
                    last.then_inc(nT_ps, 1)

                staged(pe, [(2, transposes)])

            @block.scalar
            def _(act):
                def copied(c, b):
                    act.wait_ge(nT_ps, c + 1)
                    for k in range(KD):
                        nc.scalar.copy(nT[:, k, bass.ds(c * CH, CH)], bank[b * KD + k][:])
                        last = nc.scalar.copy(halves["high"][:, k, bass.ds(c * CH, CH)], bank[b * KD + k][:])
                    last.then_inc(nT_ready, 1)

                staged(act, [(1, copied)])


def route(nc, sem, nT, combine, a):
    with ExitStack() as ctx:
        def sb(part, shape, dt=F32):
            return ctx.enter_context(nc.sbuf_tensor(f"g_{part}", shape, dt))

        def sig(part):
            return sem(f"g_{part}")

        w = sb("w", [P, KD, NE])
        bias = sb("bias", [P, 1, NE])
        score = sb("score", [P, NT, NE])
        group = sb("group", [P, NT, NG])
        pair = sb("pair", [P, NT, NG])
        g_rank = sb("g_rank", [P, NT, NG])
        wins = sb("wins", [P, NT, 1])
        rank = sb("rank", [P, NT, NE])
        beaten = sb("beaten", [P, NT, NE])
        total = sb("total", [P, NT, 1])
        logits = ctx.enter_context(nc.psum_tensor("g_logits", [P, NT, NE], F32))
        w_ready, logit_ready, score_ready, own_sem = sig("w_ready"), sig("logit_ready"), sig("score_ready"), sig("own")
        nT3 = nT[:].rearrange("p k (j t) -> p k j t", t=P)

        with nc.Block() as block:
            @block.sync
            def _(sp):
                sp.dma_start(w[:], a["gate_w"]).then_inc(w_ready, 16)
                sp.dma_start(bias[:], a["gate_b"]).then_inc(w_ready, 16)

            @block.tensor
            def _(pe):
                pe.wait_ge(w_ready, 32)
                for i in range(NT):
                    for k in range(KD):
                        last = nc.tensor.matmul(logits[:, i, :], nT3[:, k, i, :], w[:, k, :],
                                                start=(k == 0), stop=(k == KD - 1))
                last.then_inc(logit_ready, 1)

            @block.scalar
            def _(act):
                act.wait_ge(logit_ready, 1)
                nc.scalar.activation(score[:], logits[:], ACT.Sigmoid).then_inc(score_ready, 1)

            @block.vector
            def _(dve):
                own = Order(dve, own_sem)
                tt = nc.vector.tensor_tensor
                dve.wait_ge(w_ready, 32)
                dve.wait_ge(score_ready, 1)
                own.done(tt(score[:], score[:], bias[:].broadcast_to([P, NT, NE]), ALU.add))
                member = score[:].rearrange("p i (g e) -> p i g e", e=GE)
                pairs = [(x, y) for x in range(GE) for y in range(x + 1, GE)]
                for n, (x, y) in enumerate(pairs):
                    dst = pair if n else group
                    own.done(tt(dst[:], member[:, :, :, x], member[:, :, :, y], ALU.add))
                    if n:
                        own.done(tt(group[:], group[:], pair[:], ALU.max))
                own.done(nc.vector.memset(g_rank[:], 0.0))
                for x in range(NG):
                    for y in range(x + 1, NG):
                        gx, gy = group[:, :, x:x + 1], group[:, :, y:y + 1]
                        own.done(tt(wins[:], gx, gy, ALU.is_ge))
                        own.done(tt(g_rank[:, :, y:y + 1], g_rank[:, :, y:y + 1], wins[:], ALU.add))
                        own.done(tt(wins[:], gx, gy, ALU.is_lt))
                        own.done(tt(g_rank[:, :, x:x + 1], g_rank[:, :, x:x + 1], wins[:], ALU.add))
                own.done(nc.vector.tensor_scalar(g_rank[:], g_rank[:], float(TOP_G), None, ALU.is_lt))
                for x in range(GE):
                    last = tt(member[:, :, :, x], member[:, :, :, x], g_rank[:], ALU.mult)
                own.done(last)
                own.done(nc.vector.memset(rank[:], 0.0))
                for x in range(NE):
                    one = score[:, :, x:x + 1]
                    if x:
                        last = tt(beaten[:, :, 0:x], one.broadcast_to([P, NT, x]), score[:, :, 0:x], ALU.is_gt)
                    if x < NE - 1:
                        last = tt(beaten[:, :, x + 1:], one.broadcast_to([P, NT, NE - 1 - x]), score[:, :, x + 1:],
                                  ALU.is_ge)
                    own.done(last)
                    if x:
                        last = tt(rank[:, :, 0:x], rank[:, :, 0:x], beaten[:, :, 0:x], ALU.add)
                    if x < NE - 1:
                        last = tt(rank[:, :, x + 1:], rank[:, :, x + 1:], beaten[:, :, x + 1:], ALU.add)
                    own.done(last)
                own.done(nc.vector.tensor_scalar(rank[:], rank[:], float(TOP_K), None, ALU.is_lt))
                own.done(tt(score[:], score[:], rank[:], ALU.mult))
                own.done(nc.vector.tensor_reduce(total[:].rearrange("p i o -> p (i o)"), score[:], AX.X, ALU.add))
                own.done(nc.vector.tensor_scalar(total[:], total[:], 1e-20, None, ALU.add))
                own.done(nc.vector.reciprocal(total[:], total[:]))
                own.done(tt(score[:], score[:], total[:].broadcast_to([P, NT, NE]), ALU.mult))
                nc.vector.memset(combine[:, :, NE:], 1.0)
                own.done(nc.vector.tensor_scalar(combine[:, :, 0:NE], score[:], SCALE, None, ALU.mult))


def experts(nc, sem, halves, Y, combine, a):
    with ExitStack() as ctx:
        def sb(part, shape, dt=F32):
            return ctx.enter_context(nc.sbuf_tensor(f"e_{part}", shape, dt))

        def sig(part):
            return sem(f"e_{part}")

        w = sb("w", [P, 2, 3, DM])
        half, spare = sb("half", [P, 1]), sb("spare", [P, 1])
        w_part = {x: sb(f"w_{x}", [P, 2, 3, DM], F32R) for x in ("high", "low")}
        gate = sb("gate", [P, 2, CH])
        inter = sb("inter", [P, 2, CH])
        inter_part = {x: sb(f"inter_{x}", [P, 2, CH], F32R) for x in ("high", "low")}
        G = [ctx.enter_context(nc.psum_tensor(f"e_G{b}", [P, CH], F32)) for b in range(2)]
        U = [ctx.enter_context(nc.psum_tensor(f"e_U{b}", [P, CH], F32)) for b in range(2)]
        O = [ctx.enter_context(nc.psum_tensor(f"e_O{b}", [P, TPC, DM], F32)) for b in range(2)]
        gu_ps, gate_ready, inter_ready, out_ps, out_used, own_sem = (
            sig("gu_ps"), sig("gate_ready"), sig("inter_ready"), sig("out_ps"), sig("out_used"), sig("own"))
        high_ready, inter_split, w_high, w_split = sig("high_ready"), sig("inter_split"), sig("w_high"), sig("w_split")
        const_ready = sig("const_ready")
        loaded = [sig(f"loaded{b}") for b in range(2)]
        DONE = 2
        for s in (inter_ready, high_ready, out_ps, out_used):
            nc.sync.sem_inc(s, DONE)


        def every(eng, step, ahead=None):
            STEPS = 2 * NCH

            def at(x, m):
                eb, c = m % STEPS // NCH, m % NCH
                return x * STEPS + m, (x + m // STEPS) * 2 + eb, eb, c, c % 2

            def one_pass(x, last=False):
                for m in range(STEPS):
                    if ahead and not (last and m == STEPS - 1):
                        ahead(*at(x, m + 1))
                    step(*at(x, m))

            if ahead:
                ahead(*at(0, 0))
            with eng.Fori(0, NX // 2 - 1) as x:
                one_pass(x)
            one_pass(NX // 2 - 1, True)

        with nc.Block() as block:
            @block.sync
            def _(sp):
                def load(e, eb):
                    for n, src in enumerate(("wg", "wu", "wd")):
                        sp.dma_start(w[:, eb, n], a[f"moe_{src}"][:, bass.ds(e, 1)].rearrange(
                            "p o k m -> p (o k m)" if src != "wd" else "p o m -> p (o m)")).then_inc(loaded[eb], 16)

                load(0, 0)
                load(1, 1)
                with sp.Fori(0, NX // 2 - 1) as x:
                    for eb in range(2):
                        e = 2 * x + eb
                        sp.wait_ge(w_split, e + 1)
                        load(e + 2, eb)

            @block.gpsimd
            def _(pool):
                def split(e, eb):
                    pool.wait_ge(loaded[eb], (e - eb) * 24 + 48)
                    wait_past(pool, out_ps, DONE + (e - 1) * NCH if not isinstance(e, int) or e > 1 else 0)
                    nc.gpsimd.tensor_tensor(spare[:], half[:], half[:], ALU.add)
                    nc.gpsimd.tensor_copy(w_part["high"][:, eb], w[:, eb]).then_inc(w_high, 1)
                    pool.wait_ge(w_high, e + 1)
                    nc.gpsimd.tensor_tensor(w_part["low"][:, eb], w[:, eb], w_part["high"][:, eb].bitcast(F32),
                                            ALU.subtract).then_inc(w_split, 1)

                nc.gpsimd.memset(half[:], 0.5).then_inc(const_ready, 1)
                pool.wait_ge(const_ready, 1)
                split(0, 0)
                split(1, 1)
                with pool.Fori(1, NX // 2) as x:
                    split(2 * x, 0)
                    split(2 * x + 1, 1)

            @block.scalar
            def _(act):
                def step(n, e, eb, c, b):
                    act.wait_ge(gu_ps, n + 1)
                    act.wait_ge(inter_ready, DONE + n - 1)
                    nc.scalar.activation(gate[:, b], G[b][:], ACT.Silu).then_inc(gate_ready, 1)
                    act.wait_ge(inter_ready, DONE + n + 1)
                    act.wait_ge(out_ps, DONE + n - 1)
                    nc.scalar.copy(inter_part["high"][:, b], inter[:, b]).then_inc(high_ready, 1)

                every(act, step)

            @block.vector
            def _(dve):
                nc.vector.memset(Y[:], 0.0).then_inc(own_sem, 1)
                dve.wait_ge(own_sem, 1)

                def gated(n, e, eb, c, b):
                    dve.wait_ge(gate_ready, n + 1)
                    dve.wait_ge(high_ready, DONE + n - 1)
                    nc.vector.tensor_tensor(inter[:, b], gate[:, b], U[b][:], ALU.mult).then_inc(inter_ready, 1)
                    dve.wait_ge(inter_ready, DONE + n + 1)
                    dve.wait_ge(high_ready, DONE + n + 1)
                    dve.wait_ge(out_ps, DONE + n - 1)
                    nc.vector.tensor_tensor(inter_part["low"][:, b], inter[:, b],
                                            inter_part["high"][:, b].bitcast(F32), ALU.subtract).then_inc(inter_split, 1)

                def weighted(n, e, eb, c, b):
                    dve.wait_ge(out_ps, DONE + n + 1)
                    dve.wait_ge(out_used, DONE + n - 1)
                    for t in range(TPC):
                        last = nc.vector.scalar_tensor_tensor(Y[:, tok(c, t), :], O[b][:, t, :],
                                                              combine[:, tok(c, t), bass.ds(e, 1)],
                                                              Y[:, tok(c, t), :], ALU.mult, ALU.add)
                    last.then_inc(out_used, 1)

                every(dve, weighted, gated)

            @block.tensor
            def _(pe):
                def gate_up(n, e, eb, c, b):
                    pe.wait_ge(w_split, e + 1)
                    pe.wait_ge(inter_ready, DONE + n - 1)
                    for which, ps in enumerate((G, U)):
                        for k in range(KD):
                            for x, y in PRODUCTS:
                                last = nc.tensor.matmul(ps[b][:], w_part[x][:, eb, which, k * ME:(k + 1) * ME],
                                                        halves[y][:, k, c * CH:(c + 1) * CH],
                                                        start=(k == 0 and (x, y) == PRODUCTS[0]),
                                                        stop=(k == KD - 1 and (x, y) == PRODUCTS[-1]))
                    last.then_inc(gu_ps, 1)

                def down(n, e, eb, c, b):
                    pe.wait_ge(inter_split, n + 1)
                    pe.wait_ge(out_used, DONE + n - 1)
                    for t in range(TPC):
                        for x, y in PRODUCTS:
                            last = nc.tensor.matmul(O[b][:, t, :], inter_part[x][:, b, t * P:(t + 1) * P],
                                                    w_part[y][:, eb, 2, :], start=((x, y) == PRODUCTS[0]),
                                                    stop=((x, y) == PRODUCTS[-1]))
                    last.then_inc(out_ps, 1)

                every(pe, down, gate_up)


def experts_out(nc, sem, X, Y, a):
    with ExitStack() as ctx:
        half = ctx.enter_context(nc.sbuf_tensor("f_half", [P, TPC], F32))
        norm = Norm(nc, ctx, sem, "f_norm", LN_EPS)
        const_ready, x_done, own_sem, stored = sem("f_const_ready"), sem("f_x_done"), sem("f_own"), sem("f_stored")
        out_tiles = a["out"][0].rearrange("(j p) d -> p j d", p=P)
        with nc.Block() as block:
            @block.sync
            def _(sp):
                def store(c, b):
                    sp.wait_ge(x_done, c + 1)
                    sp.dma_start(out_tiles[:, bass.ds(c * TPC, TPC), :], X[:, bass.ds(c * TPC, TPC), :]
                                 ).then_inc(stored, 16)

                staged(sp, [(0, store)])
                sp.wait_ge(stored, NCH * 16)

            @block.gpsimd
            def _(pool):
                nc.gpsimd.memset(half[:], -0.5).then_inc(const_ready, 1)
                pool.wait_ge(const_ready, 1)
                staged(pool, [(0, lambda c, b: norm.power(pool, half, c))])

            @block.vector
            def _(dve):
                def step(c, b):
                    own = Order(dve, own_sem, c * (Norm.ORDERS + 1))
                    norm.begin(own, lambda t: Y[:, tok(c, t), :])
                    own.done(norm.scale(dve, c, lambda t: Y[:, tok(c, t), :], lambda t: Y[:, tok(c, t), :]))
                    for t in range(TPC):
                        last = nc.vector.tensor_tensor(X[:, tok(c, t), :], X[:, tok(c, t), :], Y[:, tok(c, t), :],
                                                       ALU.add)
                    last.then_inc(x_done, 1)

                staged(dve, [(0, step)])


def host_arrays(g):
    c = np.ascontiguousarray
    spread = np.zeros((SPLIT * BC, BC, P), np.float32)
    for r in range(BC):
        for s in range(SPLIT):
            spread[s * BC + r, r, :] = 1
    xp = g["L0_attn_x_proj_w"].T

    def rows(w):
        return c(np.moveaxis(w.reshape(-1, P, *w.shape[1:]), 0, 1))

    def every(v):
        return c(np.broadcast_to(v, (P, 1, v.size)))

    def ffn(name, w1, b1, w2, b2):
        return {f"{name}_w1": rows(w1.T), f"{name}_b1": rows(b1), f"{name}_w2": rows(w2.T), f"{name}_b2": c(b2[None])}

    def up(w, shared):
        both = np.concatenate([w, shared.reshape(DM, -1, ME).transpose(1, 0, 2)], 0)
        return c(both.reshape(NX, KD, P, ME).transpose(2, 0, 1, 3))

    return {
        "L0_attn_x": c(g["L0_attn_x"]),
        "in_proj_t": rows(g["L0_attn_in_proj_w"].T),
        "x_proj_t": rows(np.concatenate([xp[:, DTR:]] * SPLIT + [xp[:, :DTR]], 1)),
        "dt_proj_t": c(g["L0_attn_dt_proj_w"].T),
        "out_proj_t": rows(g["L0_attn_out_proj_w"].T),
        "conv_w": rows(g["L0_attn_conv_w"]),
        "conv_b": rows(g["L0_attn_conv_b"]),
        "dt_b": rows(g["L0_attn_dt_proj_b"]),
        "skip_d": rows(g["L0_attn_D"]),
        "a_log": rows(g["L0_attn_A_log"]),
        "x_tiles": c(g["L0_attn_x"].reshape(NCH, CH, DM)),
        **ffn("tail", g["L0_attn_ffn_w1"], g["L0_attn_ffn_b1"], g["L0_attn_ffn_w2"], g["L0_attn_ffn_b2"]),
        "tail_in_w": rows(g["L0_attn_ln1_w"]), "tail_in_b": rows(g["L0_attn_ln1_b"]),
        "tail_mid_w": every(g["L0_attn_ln2_w"]), "tail_mid_b": every(g["L0_attn_ln2_b"]),
        **ffn("bit", g["L0_ffn_W1"], g["L0_ffn_b1"], g["L0_ffn_W2"], g["L0_ffn_b2"]),
        "attn_w": np.concatenate([rows(g[f"L1_attn_W{x}"].T) for x in "qkv"], 2),
        "attn_qk_b": np.stack([rows(g["L1_attn_bq"]), rows(g["L1_attn_bk"])], 1),
        "attn_v_b": c(g["L1_attn_bv"][None]),
        "attn_gamma": every(g["L1_attn_gamma"]), "attn_beta": every(g["L1_attn_beta"]),
        "gate_w": rows(g["L1_ffn_gate_kernel"]), "gate_b": every(g["L1_ffn_gate_bias"]),
        "moe_wg": up(g["L1_ffn_w_gate"], g["L1_ffn_sw_gate"]), "moe_wu": up(g["L1_ffn_w_up"], g["L1_ffn_sw_up"]),
        "moe_wd": c(np.concatenate([g["L1_ffn_w_down"], g["L1_ffn_sw_down"].reshape(-1, ME, DM)], 0).transpose(1, 0, 2)),
        "sel": np.tile(np.eye(VW, dtype=np.float32), (P // VW, 1)),
        "ident": np.eye(P, dtype=np.float32),
        "spread": spread.reshape(SPLIT * BC, BC * P),
    }


def phase(nc, build, *args):
    held = []

    def sem(name):
        held.append(nc.alloc_semaphore(name=name))
        return held[-1]

    build(nc, sem, *args)
    nc.clear_and_free_semaphores(held)
    nc.all_engine_barrier()


def program(nc, a):
    with ExitStack() as ctx:
        parts_dram = nc.dram_tensor("parts", (2, SPLIT, KD, P, T), BF16, kind="Internal").ap()
        z_dram = nc.dram_tensor("z", (H, T, HD), F32, kind="Internal").ap()
        X = ctx.enter_context(nc.sbuf_tensor("X", [P, NT, DM], F32))
        ident = ctx.enter_context(nc.sbuf_tensor("ident", [P, P], F32))
        phase(nc, mamba, X, ident, a)
        with ExitStack() as attn_weights:
            attn_tiles = weight_tiles(nc, attn_weights, "attn", PROJECT_SHAPES)
            with ExitStack() as bit_weights:
                bit_tiles = weight_tiles(nc, bit_weights, "bit", ffn_shapes(4 * DM))
                with ExitStack() as tail_weights:
                    tail_tiles = weight_tiles(nc, tail_weights, "tail", ffn_shapes(2 * DM))
                    phase(nc, feed_forward, X, ident, a, "tail", 2 * DM, True, tail_tiles, bit_tiles)
                phase(nc, feed_forward, X, ident, a, "bit", 4 * DM, False, bit_tiles, attn_tiles)
            with nc.sbuf_tensor("V", [P, NT, DM], F32) as V:
                phase(nc, project, X, V, ident, attn_tiles, parts_dram)
                phase(nc, attend, V, ident, a, parts_dram, z_dram)
        phase(nc, attention_out, X, a, z_dram)
        with nc.sbuf_tensor("combine", [P, NT, NX], F32) as combine, nc.sbuf_tensor("Y", [P, NT, DM], F32) as Y:
            with nc.sbuf_tensor("nT_high", [P, KD, T], F32R) as high, nc.sbuf_tensor("nT_low", [P, KD, T], F32R) as low:
                halves = {"high": high, "low": low}
                with nc.sbuf_tensor("nT", [P, KD, T], F32) as nT:
                    phase(nc, normed_transposed, X, nT, halves, ident, "r")
                    phase(nc, route, nT, combine, a)
                phase(nc, experts, halves, Y, combine, a)
            phase(nc, experts_out, X, Y, a)


def kernel(**inputs):
    import concourse.bacc as bacc
    from concourse.bass_utils import run_bass_kernel_spmd

    nc = bacc.Bacc("TRN2", target_bir_lowering=False, num_devices=1)
    arrays = host_arrays({name: np.asarray(value) for name, value in inputs.items()})
    a = {name: nc.dram_tensor(f"in_{name}", v.shape, mybir.dt.from_np(v.dtype), kind="ExternalInput").ap()
         for name, v in arrays.items()}
    a["out"] = nc.dram_tensor("out", (1, T, DM), F32, kind="ExternalOutput").ap()
    program(nc, a)
    ran = run_bass_kernel_spmd(nc, [{f"in_{name}": v for name, v in arrays.items()}], core_ids=[0])
    return ran.results[0]["out"]
```
